# Optimizing a Trainium2 kernel written in Bass

```python
import numpy as np
import jax
import jax.numpy as jnp

def _softmax(x, axis=-1):
    return jax.nn.softmax(x, axis=axis)

def _gelu(x):
    return jax.nn.gelu(x, approximate=True)

def _silu(x):
    return jax.nn.silu(x)

def _sigmoid(x):
    return jax.nn.sigmoid(x)

def _layernorm(x, axis=-1, eps=1e-05):
    m = jnp.mean(x, axis=axis, keepdims=True)
    v = jnp.var(x, axis=axis, keepdims=True)
    return (x - m) / jnp.sqrt(v + eps)

def _scatter_add(tgt, idx, src, axis=0):
    return tgt.at[idx].add(src)

def _segment_sum(src, seg, n):
    return jax.ops.segment_sum(src, seg, n)
kernel_name = 'mk_gnn_resnorm_d4_gnn_r64_84c299'

def setup_inputs(seed: int=0):
    np.random.seed(seed)
    _w = jnp.asarray

    def _rec_inputs():
        import jax
        import jax.numpy as jnp
        _gk = jax.random.key(seed)
        x = -0.0008691 + 1 * jax.random.normal(jax.random.fold_in(_gk, 1), (50000, 128), jnp.float32)
        src = jax.random.randint(jax.random.fold_in(_gk, 2), (25000,), 0, 50000, jnp.int32)
        dst = jax.random.randint(jax.random.fold_in(_gk, 3), (25000,), 0, 50000, jnp.int32)
        _o = jnp.argsort(dst, stable=True)
        src = src[_o]
        dst = dst[_o]
        edge_attr_64 = -0.000128692 + 0.999872 * jax.random.normal(jax.random.fold_in(_gk, 11), (25000, 64), jnp.float32)
        return (x, src, dst, edge_attr_64)
    x, src, dst, edge_attr_64 = _rec_inputs()

    def _L0_gnn_setup():
        import jax, jax.numpy as jnp
        import numpy as np
        N = 10000
        E = 10000
        D = 128
        H = 16
        C = D // H
        EF = 64
        LN_EPS = 1e-05

        def _xavier(key, shape):
            fan_in, fan_out = (shape[0], shape[1])
            lim = np.sqrt(6.0 / (fan_in + fan_out)).astype(np.float32)
            return jax.random.uniform(key, shape, jnp.float32, -lim, lim)
        key = jax.random.key(seed)
        ks = jax.random.split(key, 12)
        x = jax.random.normal(ks[0], (N, D), jnp.float32)
        edge_feat = jax.random.normal(ks[1], (E, EF), jnp.float32)
        edge_index = jax.random.randint(ks[2], (2, E), 0, N, jnp.int64)
        Wq = _xavier(ks[3], (D, H * C))
        Wk = _xavier(ks[4], (D, H * C))
        Wv = _xavier(ks[5], (D, H * C))
        We0 = _xavier(ks[6], (EF, H * C))
        We1 = _xavier(ks[7], (EF, H * C))
        W1 = _xavier(ks[8], (2 * D, D))
        b1 = jnp.zeros((D,), jnp.float32)
        ln_g = jnp.ones((D,), jnp.float32)
        ln_b = jnp.zeros((D,), jnp.float32)
        W2 = _xavier(ks[9], (D, D))
        b2 = jnp.zeros((D,), jnp.float32)
        return {'x': x, 'edge_feat': edge_feat, 'edge_index': edge_index, 'Wq': Wq, 'Wk': Wk, 'Wv': Wv, 'We0': We0, 'We1': We1, 'W1': W1, 'b1': b1, 'ln_g': ln_g, 'ln_b': ln_b, 'W2': W2, 'b2': b2}
    _L0_gnn_all = _L0_gnn_setup()
    _L0_gnn_in = {k: v for k, v in _L0_gnn_all.items() if k in ('Wq', 'Wk', 'Wv', 'We0', 'We1', 'W1', 'b1', 'ln_g', 'ln_b', 'W2', 'b2')}
    del _L0_gnn_all

    def _L1_gnn_setup():
        import jax, jax.numpy as jnp
        import numpy as np
        N_NODES = 50000
        N_EDGES = 12500
        IN_DIM = 128
        OUT_DIM = 128
        HEADS = 4
        HEAD_DIM = OUT_DIM // HEADS
        NEG_SLOPE = 0.2
        LN_EPS = 1e-05
        key = jax.random.key(seed)
        ks = jax.random.split(key, 8)
        x = jax.random.normal(ks[0], (N_NODES, IN_DIM), dtype=jnp.float32)
        edge_index = jax.random.randint(ks[1], (2, N_EDGES), 0, N_NODES, dtype=jnp.int64)
        W = jax.random.normal(ks[2], (IN_DIM, HEADS * HEAD_DIM), dtype=jnp.float32) / np.sqrt(IN_DIM)
        att_src = jax.random.normal(ks[3], (HEADS, HEAD_DIM), dtype=jnp.float32) / np.sqrt(HEAD_DIM)
        att_dst = jax.random.normal(ks[4], (HEADS, HEAD_DIM), dtype=jnp.float32) / np.sqrt(HEAD_DIM)
        bias = jnp.zeros((OUT_DIM,), dtype=jnp.float32)
        gamma = jnp.ones((OUT_DIM,), dtype=jnp.float32)
        beta = jnp.zeros((OUT_DIM,), dtype=jnp.float32)
        return {'x': x, 'edge_index': edge_index, 'W': W, 'att_src': att_src, 'att_dst': att_dst, 'bias': bias, 'gamma': gamma, 'beta': beta}
    _L1_gnn_all = _L1_gnn_setup()
    _L1_gnn_in = {k: v for k, v in _L1_gnn_all.items() if k in ('W', 'att_src', 'att_dst', 'bias', 'gamma', 'beta')}
    del _L1_gnn_all

    def _L2_gnn_setup():
        import jax, jax.numpy as jnp
        import numpy as np
        NEG_SLOPE = 0.2

        def _gatv2_layer(x, src, dst, Wl, bl, Wr, br, att, bias, heads, out_ch, concat):
            N = x.shape[0]
            xl = (x @ Wl + bl).reshape(N, heads, out_ch)
            xr = (x @ Wr + br).reshape(N, heads, out_ch)
            e = jax.nn.leaky_relu(xl[src] + xr[dst], NEG_SLOPE)
            logits = jnp.einsum('ehc,hc->eh', e, att)
            m = jax.ops.segment_max(logits, dst, num_segments=N)
            ex = jnp.exp(logits - m[dst])
            denom = jax.ops.segment_sum(ex, dst, num_segments=N)
            alpha = ex / denom[dst]
            msg = xl[src] * alpha[..., None]
            out = jax.ops.segment_sum(msg, dst, num_segments=N)
            if concat:
                out = out.reshape(N, heads * out_ch)
            else:
                out = out.mean(axis=1)
            return out + bias
        key = jax.random.key(seed)
        ks = jax.random.split(key, 16)
        N, F, E = (50000, 128, 12500)
        H1, C1 = (8, 16)
        C2 = 64
        OUT = 128
        s = lambda f: 1.0 / np.sqrt(f)
        inp = {'x': jax.random.normal(ks[0], (N, F), dtype=jnp.float32), 'edge_index': jax.random.randint(ks[1], (2, E), 0, N, dtype=jnp.int64), 'Wl1': jax.random.normal(ks[2], (F, H1 * C1), dtype=jnp.float32) * s(F), 'bl1': jnp.zeros((H1 * C1,), dtype=jnp.float32), 'Wr1': jax.random.normal(ks[3], (F, H1 * C1), dtype=jnp.float32) * s(F), 'br1': jnp.zeros((H1 * C1,), dtype=jnp.float32), 'att1': jax.random.normal(ks[4], (H1, C1), dtype=jnp.float32) * s(C1), 'bias1': jnp.zeros((H1 * C1,), dtype=jnp.float32), 'Wl2': jax.random.normal(ks[5], (H1 * C1, C2), dtype=jnp.float32) * s(H1 * C1), 'bl2': jnp.zeros((C2,), dtype=jnp.float32), 'Wr2': jax.random.normal(ks[6], (H1 * C1, C2), dtype=jnp.float32) * s(H1 * C1), 'br2': jnp.zeros((C2,), dtype=jnp.float32), 'att2': jax.random.normal(ks[7], (1, C2), dtype=jnp.float32) * s(C2), 'bias2': jnp.zeros((C2,), dtype=jnp.float32), 'Wlin': jax.random.normal(ks[8], (C2, OUT), dtype=jnp.float32) * s(C2), 'blin': jnp.zeros((OUT,), dtype=jnp.float32)}
        return inp
    _L2_gnn_all = _L2_gnn_setup()
    _L2_gnn_in = {k: v for k, v in _L2_gnn_all.items() if k in ('Wl1', 'bl1', 'Wr1', 'br1', 'att1', 'bias1', 'Wl2', 'bl2', 'Wr2', 'br2', 'att2', 'bias2', 'Wlin', 'blin')}
    del _L2_gnn_all

    def _L3_gnn_setup():
        import jax, jax.numpy as jnp
        import numpy as np
        N_NODES, N_EDGES = (50000, 9375)
        NODE_DIM, EDGE_DIM = (128, 64)
        H, HD = (4, 32)
        key = jax.random.key(seed)
        k = jax.random.split(key, 6)
        node_features = jax.random.normal(k[0], (N_NODES, NODE_DIM), jnp.float32)
        edge_indices = jax.random.randint(k[1], (2, N_EDGES), 0, N_NODES, jnp.int32)
        edge_features = jax.random.normal(k[2], (N_EDGES, EDGE_DIM), jnp.float32)
        W_node = jax.random.normal(k[3], (H * HD, NODE_DIM), jnp.float32) / np.sqrt(NODE_DIM).astype(np.float32)
        W_edge = jax.random.normal(k[4], (H * HD, EDGE_DIM), jnp.float32) / np.sqrt(EDGE_DIM).astype(np.float32)
        a = jax.random.normal(k[5], (H, 3 * HD), jnp.float32)
        return {'node_features': node_features, 'edge_indices': edge_indices, 'edge_features': edge_features, 'W_node': W_node, 'W_edge': W_edge, 'a': a}
    _L3_gnn_all = _L3_gnn_setup()
    _L3_gnn_in = {k: v for k, v in _L3_gnn_all.items() if k in ('W_node', 'W_edge', 'a')}
    del _L3_gnn_all
    return {'x': x, 'src': src, 'dst': dst, 'edge_attr_64': edge_attr_64, 'L0_gnn_Wq': _L0_gnn_in['Wq'], 'L0_gnn_Wk': _L0_gnn_in['Wk'], 'L0_gnn_Wv': _L0_gnn_in['Wv'], 'L0_gnn_We0': _L0_gnn_in['We0'], 'L0_gnn_We1': _L0_gnn_in['We1'], 'L0_gnn_W1': _L0_gnn_in['W1'], 'L0_gnn_b1': _L0_gnn_in['b1'], 'L0_gnn_ln_g': _L0_gnn_in['ln_g'], 'L0_gnn_ln_b': _L0_gnn_in['ln_b'], 'L0_gnn_W2': _L0_gnn_in['W2'], 'L0_gnn_b2': _L0_gnn_in['b2'], 'L1_gnn_W': _L1_gnn_in['W'], 'L1_gnn_att_src': _L1_gnn_in['att_src'], 'L1_gnn_att_dst': _L1_gnn_in['att_dst'], 'L1_gnn_bias': _L1_gnn_in['bias'], 'L1_gnn_gamma': _L1_gnn_in['gamma'], 'L1_gnn_beta': _L1_gnn_in['beta'], 'L2_gnn_Wl1': _L2_gnn_in['Wl1'], 'L2_gnn_bl1': _L2_gnn_in['bl1'], 'L2_gnn_Wr1': _L2_gnn_in['Wr1'], 'L2_gnn_br1': _L2_gnn_in['br1'], 'L2_gnn_att1': _L2_gnn_in['att1'], 'L2_gnn_bias1': _L2_gnn_in['bias1'], 'L2_gnn_Wl2': _L2_gnn_in['Wl2'], 'L2_gnn_bl2': _L2_gnn_in['bl2'], 'L2_gnn_Wr2': _L2_gnn_in['Wr2'], 'L2_gnn_br2': _L2_gnn_in['br2'], 'L2_gnn_att2': _L2_gnn_in['att2'], 'L2_gnn_bias2': _L2_gnn_in['bias2'], 'L2_gnn_Wlin': _L2_gnn_in['Wlin'], 'L2_gnn_blin': _L2_gnn_in['blin'], 'L3_gnn_W_node': _L3_gnn_in['W_node'], 'L3_gnn_W_edge': _L3_gnn_in['W_edge'], 'L3_gnn_a': _L3_gnn_in['a']}

def reference(x, src, dst, edge_attr_64, L0_gnn_Wq, L0_gnn_Wk, L0_gnn_Wv, L0_gnn_We0, L0_gnn_We1, L0_gnn_W1, L0_gnn_b1, L0_gnn_ln_g, L0_gnn_ln_b, L0_gnn_W2, L0_gnn_b2, L1_gnn_W, L1_gnn_att_src, L1_gnn_att_dst, L1_gnn_bias, L1_gnn_gamma, L1_gnn_beta, L2_gnn_Wl1, L2_gnn_bl1, L2_gnn_Wr1, L2_gnn_br1, L2_gnn_att1, L2_gnn_bias1, L2_gnn_Wl2, L2_gnn_bl2, L2_gnn_Wr2, L2_gnn_br2, L2_gnn_att2, L2_gnn_bias2, L2_gnn_Wlin, L2_gnn_blin, L3_gnn_W_node, L3_gnn_W_edge, L3_gnn_a):
    import jax
    import jax.numpy as jnp

    def _L0_gnn_ref(x, edge_feat, edge_index, Wq, Wk, Wv, We0, We1, W1, b1, ln_g, ln_b, W2, b2):
        import jax, jax.numpy as jnp
        import numpy as np
        N = 10000
        E = 10000
        D = 128
        H = 16
        C = D // H
        EF = 64
        LN_EPS = 1e-05

        def _xavier(key, shape):
            fan_in, fan_out = (shape[0], shape[1])
            lim = np.sqrt(6.0 / (fan_in + fan_out)).astype(np.float32)
            return jax.random.uniform(key, shape, jnp.float32, -lim, lim)
        n = x.shape[0]
        src, dst = (edge_index[0], edge_index[1])
        q = (x @ Wq).reshape(n, H, C)
        k = (x @ Wk).reshape(n, H, C)
        v = (x @ Wv).reshape(n, H, C)
        e0 = jnp.tanh((edge_feat @ We0).reshape(-1, H, C))
        e1 = jnp.tanh((edge_feat @ We1).reshape(-1, H, C))
        alpha = jnp.sum(q[dst] * k[src] * e0, axis=-1) / np.sqrt(C).astype(np.float32)
        amax = jax.ops.segment_max(alpha, dst, num_segments=n)
        expa = jnp.exp(alpha - amax[dst])
        denom = jax.ops.segment_sum(expa, dst, num_segments=n)
        attn = expa / (denom[dst] + 1e-16)
        msg = v[src] * e1 * attn[:, :, None]
        out = jax.ops.segment_sum(msg, dst, num_segments=n).reshape(n, H * C)
        h = jnp.concatenate([out, x], axis=-1) @ W1 + b1
        mu = jnp.mean(h, axis=-1, keepdims=True)
        var = jnp.mean(jnp.square(h - mu), axis=-1, keepdims=True)
        h = (h - mu) / jnp.sqrt(var + LN_EPS) * ln_g + ln_b
        h = jax.nn.relu(h)
        return h @ W2 + b2

    def _L1_gnn_ref(x, edge_index, W, att_src, att_dst, bias, gamma, beta):
        import jax, jax.numpy as jnp
        import numpy as np
        N_NODES = 50000
        N_EDGES = 12500
        IN_DIM = 128
        OUT_DIM = 128
        HEADS = 4
        HEAD_DIM = OUT_DIM // HEADS
        NEG_SLOPE = 0.2
        LN_EPS = 1e-05
        N = x.shape[0]
        loop = jnp.arange(N, dtype=edge_index.dtype)
        src = jnp.concatenate([edge_index[0], loop])
        dst = jnp.concatenate([edge_index[1], loop])
        h = (x @ W).reshape(N, HEADS, HEAD_DIM)
        a_s = jnp.einsum('nhd,hd->nh', h, att_src)
        a_d = jnp.einsum('nhd,hd->nh', h, att_dst)
        e = jax.nn.leaky_relu(a_s[src] + a_d[dst], NEG_SLOPE)
        e_max = jax.ops.segment_max(e, dst, num_segments=N)
        e_exp = jnp.exp(e - e_max[dst])
        denom = jax.ops.segment_sum(e_exp, dst, num_segments=N)
        alpha = e_exp / (denom[dst] + 1e-16)
        msg = h[src] * alpha[..., None]
        out = jax.ops.segment_sum(msg, dst, num_segments=N)
        out = out.reshape(N, HEADS * HEAD_DIM) + bias
        mu = out.mean(-1, keepdims=True)
        var = ((out - mu) ** 2).mean(-1, keepdims=True)
        out = (out - mu) * jax.lax.rsqrt(var + LN_EPS) * gamma + beta
        return jax.nn.gelu(out, approximate=False)

    def _L2_gnn_ref(x, edge_index, Wl1, bl1, Wr1, br1, att1, bias1, Wl2, bl2, Wr2, br2, att2, bias2, Wlin, blin):
        import jax, jax.numpy as jnp
        import numpy as np
        NEG_SLOPE = 0.2

        def _gatv2_layer(x, src, dst, Wl, bl, Wr, br, att, bias, heads, out_ch, concat):
            N = x.shape[0]
            xl = (x @ Wl + bl).reshape(N, heads, out_ch)
            xr = (x @ Wr + br).reshape(N, heads, out_ch)
            e = jax.nn.leaky_relu(xl[src] + xr[dst], NEG_SLOPE)
            logits = jnp.einsum('ehc,hc->eh', e, att)
            m = jax.ops.segment_max(logits, dst, num_segments=N)
            ex = jnp.exp(logits - m[dst])
            denom = jax.ops.segment_sum(ex, dst, num_segments=N)
            alpha = ex / denom[dst]
            msg = xl[src] * alpha[..., None]
            out = jax.ops.segment_sum(msg, dst, num_segments=N)
            if concat:
                out = out.reshape(N, heads * out_ch)
            else:
                out = out.mean(axis=1)
            return out + bias
        N = x.shape[0]
        loops = jnp.arange(N, dtype=edge_index.dtype)
        src = jnp.concatenate([edge_index[0], loops])
        dst = jnp.concatenate([edge_index[1], loops])
        h = _gatv2_layer(x, src, dst, Wl1, bl1, Wr1, br1, att1, bias1, heads=8, out_ch=16, concat=True)
        h = jax.nn.elu(h)
        h = _gatv2_layer(h, src, dst, Wl2, bl2, Wr2, br2, att2, bias2, heads=1, out_ch=64, concat=False)
        h = jax.nn.elu(h)
        h = jax.nn.elu(h @ Wlin + blin)
        return h

    def _L3_gnn_ref(node_features, edge_indices, edge_features, W_node, W_edge, a):
        import jax, jax.numpy as jnp
        import numpy as np
        N_NODES, N_EDGES = (50000, 9375)
        NODE_DIM, EDGE_DIM = (128, 64)
        H, HD = (4, 32)
        num_nodes = node_features.shape[0]
        num_edges = edge_indices.shape[1]
        h = (node_features @ W_node.T).reshape(num_nodes, H, HD)
        e = (edge_features @ W_edge.T).reshape(num_edges, H, HD)
        src, tgt = (edge_indices[0], edge_indices[1])
        h_src = h[src]
        h_tgt = h[tgt]
        att_in = jnp.concatenate([h_src, h_tgt, e], axis=-1)
        att = jnp.sum(att_in * a, axis=-1)
        att = jnp.where(att > 0, att, 0.2 * att)
        m = jnp.maximum(jax.ops.segment_max(att, tgt, num_segments=num_nodes), 0.0)
        ex = jnp.exp(att - m[tgt])
        ones = jnp.ones((num_edges,), node_features.dtype)
        deg = jax.ops.segment_sum(ones, tgt, num_segments=num_nodes)
        denom = jax.ops.segment_sum(ex, tgt, num_segments=num_nodes) + (num_edges - deg)[:, None] * jnp.exp(-m)
        w = ex / denom[tgt]
        h_prime = jax.ops.segment_sum(w[:, :, None] * h_src, tgt, num_segments=num_nodes)
        return h_prime.reshape(num_nodes, H * HD)
    edge_index = jnp.stack([src, dst])
    x = _layernorm(x + _L0_gnn_ref(x, edge_attr_64, edge_index, L0_gnn_Wq, L0_gnn_Wk, L0_gnn_Wv, L0_gnn_We0, L0_gnn_We1, L0_gnn_W1, L0_gnn_b1, L0_gnn_ln_g, L0_gnn_ln_b, L0_gnn_W2, L0_gnn_b2), axis=-1)
    x = _layernorm(x + _L1_gnn_ref(x, edge_index, L1_gnn_W, L1_gnn_att_src, L1_gnn_att_dst, L1_gnn_bias, L1_gnn_gamma, L1_gnn_beta), axis=-1)
    x = _layernorm(x + _L2_gnn_ref(x, edge_index, L2_gnn_Wl1, L2_gnn_bl1, L2_gnn_Wr1, L2_gnn_br1, L2_gnn_att1, L2_gnn_bias1, L2_gnn_Wl2, L2_gnn_bl2, L2_gnn_Wr2, L2_gnn_br2, L2_gnn_att2, L2_gnn_bias2, L2_gnn_Wlin, L2_gnn_blin), axis=-1)
    x = _layernorm(x + _L3_gnn_ref(x, edge_index, edge_attr_64, L3_gnn_W_node, L3_gnn_W_edge, L3_gnn_a), axis=-1)
    return x

_drawn_inputs = setup_inputs


def setup_inputs(seed=0):
    import zlib

    import numpy as np

    out = dict(_drawn_inputs(seed))
    spreads = {'L0_gnn_b1': (0.0, 0.1),
     'L0_gnn_ln_g': (1.0, 0.2),
     'L0_gnn_ln_b': (0.0, 0.1),
     'L0_gnn_b2': (0.0, 0.1),
     'L1_gnn_bias': (0.0, 0.1),
     'L1_gnn_gamma': (1.0, 0.2),
     'L1_gnn_beta': (0.0, 0.1),
     'L2_gnn_bl1': (0.0, 0.1),
     'L2_gnn_br1': (0.0, 0.8),
     'L2_gnn_bias1': (0.0, 0.1),
     'L2_gnn_bl2': (0.0, 0.1),
     'L2_gnn_br2': (0.0, 0.8),
     'L2_gnn_bias2': (0.0, 0.1),
     'L2_gnn_blin': (0.0, 0.1)}
    factors = {'L0_gnn_Wq': 2.702,
     'L0_gnn_Wk': 2.684,
     'L0_gnn_We0': 2.691,
     'L2_gnn_Wr1': 3.119,
     'L2_gnn_Wr2': 5.814}
    for name, (base, spread) in spreads.items():
        noise = np.random.default_rng([zlib.crc32(name.encode()), seed]).standard_normal(out[name].shape)
        drawn = base * np.exp(spread * noise) if base else spread * noise
        out[name] = jnp.asarray(drawn.astype(out[name].dtype))
    for name, factor in factors.items():
        out[name] = (out[name] * factor).astype(out[name].dtype)
    return out
```

```python
from contextlib import ExitStack

import numpy as np

import concourse.bass as bass
from concourse import mybir


class Named:

    def __init__(self, c=None, slots=False, last_flags=None):
        self.c, self.slots, self.last_flags = c, slots, last_flags
        self.PE, self.ACT, self.DVE, self.POOL = [], [], [], []


P = 128
CHUNK = 512
TILES = CHUNK // P
D = 128
EF = 64
N = 50000
E = 25000
BIG = 1.0e30
OUT_OF_RANGE = 1 << 22
LN_EPS = 1e-5
SOFTMAX_EPS = 1e-16
SLOPE = 0.2

NODE_STREAMS = 4
SLOT_STREAMS = 2
ITERS = 25
NODES_PER_ITER = NODE_STREAMS * CHUNK
SLOTS_PER_ITER = SLOT_STREAMS * CHUNK
N_PAD = ITERS * NODES_PER_ITER
E_PAD = ITERS * SLOTS_PER_ITER
SLOT_CHUNKS = E_PAD // CHUNK
SLOT_TILES = E_PAD // P
ROWS = N_PAD + E_PAD
C2 = 64

F32 = mybir.dt.float32
I32 = mybir.dt.int32
ALU = mybir.AluOpType
ACT = mybir.ActivationFunctionType
at_index = bass.IndirectOffsetOnAxis
ds = bass.ds


def upto(steps, i, name):
    return i * len(steps) + steps.index(name) + 1


def norm_steps(tag):
    return [tag + "_stats", tag + "_aggr", tag + "_var", tag + "_norm"]


def tiles_of(t):
    return t.rearrange("p (t n) -> p t n", t=TILES)



def dve_norm(v, g, i, tag, source, ready, out, out_free=None):
    for u in g.streams:
        v.wait_ge(*ready(u))
        for t in range(TILES):
            ins = v.bn_stats(g.stats[u][:, t, :], source(u)[:, t, :])
        ins.then_inc(g.dve_out[u], 1)
    for u in g.streams:
        v.wait_ge(g.dve_out[u], upto(g.DVE, i, tag + "_stats"))
        v.memset(g.raw[u][:, 0:1], 0.0)
        for t in range(TILES):
            ins = v.bn_aggr(g.mv[u][:, t, :], g.stats[u][:, t, :])
        ins.then_inc(g.dve_out[u], 1)
    for u in g.streams:
        v.wait_ge(g.dve_out[u], upto(g.DVE, i, tag + "_aggr"))
        v.tensor_scalar(g.var[u][:, :], g.mv[u][:, :, 1], LN_EPS, None, ALU.add).then_inc(g.dve_out[u], 1)
    for u in g.streams:
        v.wait_ge(g.pool_out[u], upto(g.POOL, i, tag + "_rstd"))
        if out_free is not None:
            v.wait_ge(*out_free(u))
        for t in range(TILES):
            ins = v.tensor_scalar(out(u)[:, t, :], source(u)[:, t, :], g.mv[u][:, t, 0:1], g.rstd[u][:, t:t + 1],
                                  ALU.subtract, ALU.mult)
        ins.then_inc(g.dve_out[u], 1)


def pool_rstd(pool, g, i, tag, u):
    pool.wait_ge(g.dve_out[u], upto(g.DVE, i, tag + "_var"))
    pool.tensor_tensor(g.rstd[u][:, :], g.var[u][:, :], g.c.minus_half[:, :], ALU.pow).then_inc(g.pool_out[u], 1)


def pool_rstd_last(pool, g, i, tag, u):
    pool.wait_ge(g.dve_out[u], upto(g.DVE, i, tag + "_var"))
    pool.tensor_tensor(g.raw[u][:, :], g.var[u][:, :], g.c.minus_half[:, :], ALU.pow).then_inc(g.pool_out[u], 1)
    pool.wait_ge(g.pool_out[u], upto(g.POOL, i, tag + "_pow"))
    flags = g.last_flags[:, ds((i * SLOT_STREAMS + u) * TILES, TILES)]
    pool.tensor_tensor(g.rstd[u][:, :], g.raw[u][:, :], flags, ALU.mult).then_inc(g.pool_out[u], 1)


def pe_rows_to_T(pe, g, i, rows, ready, bank):
    for u in g.streams:
        pe.wait_ge(*ready(u))
        for t in range(TILES):
            ins = pe.transpose(bank(u)[:, t * P:(t + 1) * P], rows(u)[:, t, :], g.c.ident[:, :])
        ins.then_inc(g.pe_out[u], 1)


def pe_T_to_rows(pe, g, i, source, ready, bank):
    for u in g.streams:
        pe.wait_ge(*ready(u))
        for t in range(TILES):
            ins = pe.transpose(bank(u)[:, t * P:(t + 1) * P], source(u)[:, t * P:(t + 1) * P], g.c.ident[:, :])
        ins.then_inc(g.pe_out[u], 1)


def pe_product(pe, g, weights, source, ready, bank, m=P):
    for u in g.streams:
        pe.wait_ge(*ready(u))
        pe.matmul(bank(u)[0:m, :], weights, source(u), start=True, stop=True).then_inc(g.pe_out[u], 1)


def act_copy(act, g, out, source, ready, func=ACT.Copy, bias=0.0, scale=1.0):
    for u in g.streams:
        act.wait_ge(*ready(u))
        act.activation(out(u), source(u), func, bias=bias, scale=scale).then_inc(g.act_out[u], 1)


def dve_elu(v, g, i, tag, source, bias, ready, m=P):
    for u in g.streams:
        v.wait_ge(*ready(u))
        v.tensor_scalar(g.expz[u][0:m, :], g.expz[u][0:m, :], 1.0, -1.0, ALU.min, ALU.add).then_inc(g.dve_out[u], 1)
    for u in g.streams:
        v.wait_ge(g.dve_out[u], upto(g.DVE, i, tag + "_em1"))
        v.scalar_tensor_tensor(out=g.act_T[u][0:m, :], in0=source(u), scalar=bias, in1=g.expz[u][0:m, :],
                               op0=ALU.add, op1=ALU.max).then_inc(g.dve_out[u], 1)


def end_phase(nc, sems):
    nc.clear_and_free_semaphores(sems)
    nc.all_engine_barrier()


def phase_tiles(ctx, nc, g, streams, prefix):
    g.streams = range(streams)
    sb = lambda name, shape, dt=F32: ctx.enter_context(nc.sbuf_tensor(f"{prefix}_{name}", shape, dt))
    g.sb = sb
    g.many = lambda name, shape, dt=F32: [sb(f"{name}{u}", shape, dt) for u in g.streams]
    g.stats = g.many("stats", [P, TILES, 6])
    g.mv = g.many("mv", [P, TILES, 2])
    g.var = g.many("var", [P, TILES])
    g.raw = g.many("raw", [P, TILES])
    g.rstd = g.many("rstd", [P, TILES])
    g.all_sems = []

    def sem(name):
        g.all_sems.append(nc.alloc_semaphore(f"{prefix}_{name}"))
        return g.all_sems[-1]

    g.sem = sem
    g.sems = lambda name: [sem(f"{name}{u}") for u in g.streams]
    g.pe_out = g.sems("pe_out")
    g.act_out = g.sems("act_out")
    g.dve_out = g.sems("dve_out")
    g.pool_out = g.sems("pool_out")



def prepare(nc, a, c, dram, ctx):
    def sb(name, shape, dt=F32):
        return ctx.enter_context(nc.sbuf_tensor(name, shape, dt))

    loads = []

    def load(name, shape, src, dt=F32):
        t = sb(name, shape, dt)
        loads.append((t[:], src))
        return t

    def column(name, src, m=P):
        return load(name, [m, 1], src.rearrange("(p o) -> p o", o=1))

    def row(name, src, m=P):
        return load(name, [P, m], src.partition_broadcast(P))

    c.W1a = load("W1a", [P, D], a["L0_gnn_W1"][0:D, :])
    c.W1b = load("W1b", [P, D], a["L0_gnn_W1"][D:2 * D, :])
    c.W2 = load("W2", [P, D], a["L0_gnn_W2"])
    c.Wq = load("Wq", [P, D], a["L0_gnn_Wq"])
    c.Wk = load("Wk", [P, D], a["L0_gnn_Wk"])
    c.Wv = load("Wv", [P, D], a["L0_gnn_Wv"])
    c.We0 = load("We0", [EF, D], a["L0_gnn_We0"])
    c.We1 = load("We1", [EF, D], a["L0_gnn_We1"])
    c.W = load("W", [P, D], a["L1_gnn_W"])
    c.Wl1 = load("Wl1", [P, D], a["L2_gnn_Wl1"])
    c.Wr1 = load("Wr1", [P, D], a["L2_gnn_Wr1"])
    c.Wl2 = load("Wl2", [P, C2], a["L2_gnn_Wl2"])
    c.Wr2 = load("Wr2", [P, C2], a["L2_gnn_Wr2"])
    att2_column = load("att2_column", [C2, 1], a["L2_gnn_att2"].rearrange("o c -> c o"))
    c.Wlin = load("Wlin", [C2, D], a["L2_gnn_Wlin"])
    c.att2 = sb("att2", [C2, P])
    c.WnT = load("WnT", [P, D], a["W_node_T"])
    c.Wn = load("Wn", [P, D], a["L3_gnn_W_node"])
    c.Wedge = load("Wedge", [P, EF], a["L3_gnn_W_edge"])
    c.b2 = column("b2", a["L0_gnn_b2"])
    c.ln_g = column("ln_g", a["L0_gnn_ln_g"])
    c.ln_b = column("ln_b", a["L0_gnn_ln_b"])
    c.gamma = column("gamma", a["L1_gnn_gamma"])
    c.beta = column("beta", a["L1_gnn_beta"])
    c.bl1 = column("bl1", a["L2_gnn_bl1"])
    c.br1 = column("br1", a["L2_gnn_br1"])
    c.bias1 = column("bias1", a["L2_gnn_bias1"])
    c.bl2 = column("bl2", a["L2_gnn_bl2"], C2)
    c.br2 = column("br2", a["L2_gnn_br2"], C2)
    c.bias2 = column("bias2", a["L2_gnn_bias2"], C2)
    c.blin = column("blin", a["L2_gnn_blin"])
    c.b1_row = row("b1_row", a["L0_gnn_b1"])
    c.bias_row = row("bias_row", a["L1_gnn_bias"])
    c.bl2_row = row("bl2_row", a["L2_gnn_bl2"], C2)

    c.src_cols = load("src_cols", [P, SLOT_TILES], a["src_cols"], I32)
    c.dst_gather_cols = load("dst_gather_cols", [P, SLOT_TILES], a["dst_gather_cols"], I32)
    here = [load(f"here{o}", [P, SLOT_TILES], a["dst_cols"][o], I32) for o in range(2)]
    after = [load(f"after{o}", [P, SLOT_TILES], a["dst_next_cols"][o], I32) for o in range(2)]
    before = load("before", [P, SLOT_TILES], a["dst_prev_cols"], I32)
    row_here = [load(f"row_here{o}", [SLOT_CHUNKS, CHUNK], a["dst_rows"][o], I32) for o in range(2)]
    row_prev = [load(f"row_prev{o}", [SLOT_CHUNKS, CHUNK], a["dst_prev_rows"][o], I32) for o in range(2)]

    blocks = []

    def block_columns(name, heads, width, pieces):
        t = sb(name, [P, heads])
        blocks.append(t)
        for h in range(heads):
            loads_late.append((t[h * width:(h + 1) * width, h:h + 1], pieces(h)))
        return t

    loads_late = []
    c.att_s = block_columns("att_s", 4, 32, lambda h: a["L1_gnn_att_src"][h:h + 1, :].rearrange("o c -> c o"))
    c.att_d = block_columns("att_d", 4, 32, lambda h: a["L1_gnn_att_dst"][h:h + 1, :].rearrange("o c -> c o"))
    c.att1 = block_columns("att1", 8, 16, lambda h: a["L2_gnn_att1"][h:h + 1, :].rearrange("o c -> c o"))
    c.a_src = block_columns("a_src", 4, 32, lambda h: a["L3_gnn_a"][h:h + 1, 0:32].rearrange("o c -> c o"))
    a_tgt = block_columns("a_tgt", 4, 32, lambda h: a["L3_gnn_a"][h:h + 1, 32:64].rearrange("o c -> c o"))
    a_edge = block_columns("a_edge", 4, 32, lambda h: a["L3_gnn_a"][h:h + 1, 64:96].rearrange("o c -> c o"))

    c.ident = sb("ident", [P, P])
    anti = c.anti = sb("anti", [P, P])
    c.spread = {h: sb(f"spread{h}", [h, P]) for h in (4, 8, 16)}
    c.spread[1] = sb("spread1", [1, C2])
    c.collect16 = sb("collect16", [P, 16])
    c.minus_half = sb("minus_half", [P, TILES])
    c.minus_one = sb("minus_one", [4, CHUNK])
    c.att_sd = sb("att_sd", [P, 4])
    c.node_bias1 = sb("node_bias1", [P, 1])
    c.node_bias2 = sb("node_bias2", [C2, 1])
    c.W_tgt = sb("W_tgt", [P, 4])
    c.W_edge = sb("W_edge", [EF, 4])
    c.last = [sb(f"last{o}", [P, SLOT_TILES]) for o in range(2)]
    c.map_index = [sb(f"map_index{o}", [P, SLOT_TILES], I32) for o in range(2)]
    c.out_index = sb("out_index", [P, SLOT_TILES], I32)
    c.payload = [sb(f"payload{o}", [P, SLOT_TILES], I32) for o in range(2)]
    first = sb("first", [P, SLOT_TILES])
    skip = [sb(f"skip{o}", [P, SLOT_TILES]) for o in range(2)]
    keep = [sb(f"keep_r{o}", [SLOT_CHUNKS, CHUNK]) for o in range(2)]
    neg = [sb(f"neg_r{o}", [SLOT_CHUNKS, CHUNK]) for o in range(2)]
    map_rows = 125
    own_row = sb("own_row", [map_rows, N // map_rows, 2], I32)
    psum = c.psum

    with ExitStack() as own:
        sem = lambda name: own.enter_context(nc.semaphore(name))
        loaded, cleared, blocks_loaded = sem("loaded"), sem("cleared"), sem("blocks_loaded")
        made, masks, stored, fused, sums = sem("made"), sem("masks"), sem("prep_stored"), sem("fused"), sem("sums")
        map_started = sem("map_started")
        block = own.enter_context(nc.Block())

        @block.sync
        def _(sp):
            for dst, src in loads:
                sp.dma_start(dst, src).then_inc(loaded, 16)
            sp.wait_ge(masks, 4)
            for o in range(2):
                sp.dma_start(dram.keep[o], keep[o][:, :]).then_inc(stored, 16)
                sp.dma_start(dram.neg[o], neg[o][:, :]).then_inc(stored, 16)
            sp.wait_ge(stored, 64)

        @block.scalar
        def _(act):
            act.wait_ge(cleared, len(blocks))
            with nc.allow_non_contiguous_dma("a few attention vectors"):
                for dst, src in loads_late:
                    act.dma_start(dst, src).then_inc(blocks_loaded, 16)
            act.wait_ge(blocks_loaded, 16 * len(loads_late))

        @block.gpsimd
        def _(pool):
            pool.iota(own_row[:, :, :], pattern=[[1, N // map_rows], [0, 2]], base=0,
                      channel_multiplier=N // map_rows).then_inc(made, 1)
            pool.iota(c.payload[0][:, :], pattern=[[P, SLOT_TILES]], base=N_PAD, channel_multiplier=1).then_inc(made, 1)
            pool.iota(c.payload[1][:, :], pattern=[[-P, SLOT_TILES]], base=N_PAD + E_PAD - 1,
                      channel_multiplier=-1).then_inc(made, 1)
            pool.wait_ge(made, 1)
            pool.dma_start(dram.slot_map.rearrange("(p n) o -> p (n o)", p=map_rows),
                           own_row[:, :, :].rearrange("p n o -> p (n o)")).then_inc(map_started, 16)
            pool.memset(c.ident[:, :], 0.0).then_inc(made, 1)
            pool.memset(anti[:, :], 0.0).then_inc(made, 1)
            for h in (4, 8, 16):
                pool.memset(c.spread[h][:, :], 1.0).then_inc(made, 1)
            pool.memset(c.collect16[:, :], 1.0).then_inc(made, 1)
            pool.memset(c.spread[1][:, :], 1.0).then_inc(made, 1)
            pool.memset(c.minus_half[:, :], -0.5).then_inc(made, 1)
            pool.memset(c.minus_one[:, :], -1.0).then_inc(made, 1)
            pool.wait_ge(made, 12)
            pool.affine_select(out=c.ident[:, :], in_=c.ident[:, :], compare_op=ALU.not_equal, fill=1.0, base=0,
                               pattern=[[-1, P]], channel_multiplier=1).then_inc(made, 1)
            pool.affine_select(out=anti[:, :], in_=anti[:, :], compare_op=ALU.not_equal, fill=1.0, base=-(P - 1),
                               pattern=[[1, P]], channel_multiplier=1).then_inc(made, 1)
            for h in (4, 8, 16):
                pool.affine_select(out=c.spread[h][:, :], in_=c.spread[h][:, :], compare_op=ALU.is_ge, fill=0.0,
                                   base=0, pattern=[[1, P]], channel_multiplier=-(P // h)).then_inc(made, 1)
            pool.affine_select(out=c.collect16[:, :], in_=c.collect16[:, :], compare_op=ALU.is_ge, fill=0.0,
                               base=0, pattern=[[-8, 16]], channel_multiplier=1).then_inc(made, 1)
            pool.wait_ge(made, 18)
            for h in (4, 8, 16):
                pool.affine_select(out=c.spread[h][:, :], in_=c.spread[h][:, :], compare_op=ALU.is_ge, fill=0.0,
                                   base=P // h - 1, pattern=[[-1, P]], channel_multiplier=P // h).then_inc(made, 1)
            pool.affine_select(out=c.collect16[:, :], in_=c.collect16[:, :], compare_op=ALU.is_ge, fill=0.0,
                               base=7, pattern=[[8, 16]], channel_multiplier=-1).then_inc(made, 1)
            pool.wait_ge(made, 22)
            pool.wait_ge(map_started, 16)

        @block.vector
        def _(v):
            for t in blocks:
                v.memset(t[:, :], 0.0).then_inc(cleared, 1)
            v.wait_ge(loaded, 16 * len(loads))
            for o in range(2):
                v.tensor_tensor(keep[o][:, :], row_here[o][:, :], row_prev[o][:, :], ALU.is_equal).then_inc(masks, 1)
            for o in range(2):
                v.wait_ge(masks, o + 1)
                v.tensor_scalar(neg[o][:, :], keep[o][:, :], -1.0, BIG, ALU.add, ALU.mult).then_inc(masks, 1)
            for o in range(2):
                v.tensor_tensor(c.last[o][:, :], here[o][:, :], after[o][:, :], ALU.not_equal).then_inc(sums, 1)
            v.tensor_tensor(first[:, :], here[0][:, :], before[:, :], ALU.not_equal).then_inc(sums, 1)
            v.tensor_tensor(c.node_bias1[:, :], c.bl1[:, :], c.bias1[:, :], ALU.add).then_inc(sums, 1)
            v.tensor_tensor(c.node_bias2[:, :], c.bl2[:, :], c.bias2[:, :], ALU.add).then_inc(sums, 1)
            v.wait_ge(sums, 3)
            v.tensor_scalar(skip[0][:, :], c.last[0][:, :], -1.0 * OUT_OF_RANGE, 1.0 * OUT_OF_RANGE, ALU.mult,
                            ALU.add).then_inc(sums, 1)
            v.tensor_scalar(skip[1][:, :], first[:, :], -1.0 * OUT_OF_RANGE, 1.0 * OUT_OF_RANGE + 1.0, ALU.mult,
                            ALU.add).then_inc(sums, 1)
            v.wait_ge(sums, 7)
            for o in range(2):
                v.scalar_tensor_tensor(out=c.map_index[o][:, :], in0=here[0][:, :], scalar=2.0, in1=skip[o][:, :],
                                       op0=ALU.mult, op1=ALU.add).then_inc(sums, 1)
            v.tensor_tensor(c.out_index[:, :], here[0][:, :], skip[0][:, :], ALU.add).then_inc(sums, 1)
            v.wait_ge(blocks_loaded, 16 * len(loads_late))
            v.tensor_tensor(c.att_sd[:, :], c.att_s[:, :], c.att_d[:, :], ALU.add).then_inc(sums, 1)
            v.wait_ge(fused, 1)
            v.tensor_copy(c.W_tgt[:, :], psum[:, 0, 0:4]).then_inc(sums, 1)
            v.tensor_copy(c.W_edge[:, :], psum[0:EF, 1, 0:4]).then_inc(sums, 1)
            v.tensor_copy(c.att2[:, :], att2_column[:, 0:1].broadcast_to([C2, P])).then_inc(sums, 1)
            v.wait_ge(sums, 14)

        @block.tensor
        def _(pe):
            pe.wait_ge(loaded, 16 * len(loads))
            pe.wait_ge(blocks_loaded, 16 * len(loads_late))
            pe.matmul(psum[:, 0, 0:4], c.Wn[:, :], a_tgt[:, :], start=True, stop=True)
            pe.matmul(psum[0:EF, 1, 0:4], c.Wedge[:, :], a_edge[:, :], start=True, stop=True).then_inc(fused, 1)



def update0(g, tail_T):
    g.PE += ["h0", "z0", "y0", "y0r"] + (["x1T"] if tail_T else [])
    g.ACT += ["relu0"] + (["x1T"] if tail_T else [])
    g.DVE += ["h0b"] + norm_steps("n0") + ["y0T"] + norm_steps("n1")
    g.POOL += ["n0_rstd", "n1_pow", "n1_rstd"] if g.slots else ["n0_rstd", "n1_rstd"]


def pe_update0(pe, g, i, tail_T):
    for u in g.streams:
        pe.wait_ge(*g.xT_ready(u, i))
        pe.wait_ge(g.dve_out[u], g.bank_free(u, i))
        for t in range(TILES):
            cols = slice(t * P, (t + 1) * P)
            ins = pe.matmul(g.bank(u)[:, cols], g.xT[u][:, cols], g.c.W1b[:, :], start=True, stop=not g.slots)
            if g.slots:
                ins = pe.matmul(g.bank(u)[:, cols], g.agg[u][:, cols], g.c.W1a[:, :], start=False, stop=True)
        ins.then_inc(g.pe_out[u], 1)
    pe_rows_to_T(pe, g, i, lambda u: g.z[u], lambda u: (g.dve_out[u], upto(g.DVE, i, "n0_norm")), g.bank)
    pe_product(pe, g, g.c.W2[:, :], lambda u: g.act_T[u][:, :],
               lambda u: (g.act_out[u], upto(g.ACT, i, "relu0")), g.bank)
    pe_T_to_rows(pe, g, i, lambda u: g.yT[u], lambda u: (g.dve_out[u], upto(g.DVE, i, "y0T")), g.bank)
    if tail_T:
        pe_rows_to_T(pe, g, i, lambda u: g.x1[u], lambda u: (g.dve_out[u], upto(g.DVE, i, "n1_norm")), g.bank)


def act_update0(act, g, i, tail_T):
    act_copy(act, g, lambda u: g.act_T[u][:, :], lambda u: g.bank(u),
             lambda u: (g.pe_out[u], upto(g.PE, i, "z0")), ACT.Relu, g.c.ln_b[:, 0:1], g.c.ln_g[:, 0:1])
    if tail_T:
        act_copy(act, g, lambda u: g.xT1[u][:, :], lambda u: g.bank(u), lambda u: (g.pe_out[u], upto(g.PE, i, "x1T")))


def dve_update0(v, g, i):
    for u in g.streams:
        v.wait_ge(g.pe_out[u], upto(g.PE, i, "h0"))
        v.tensor_tensor(g.rows[u][:, :, :], tiles_of(g.bank(u)),
                        g.c.b1_row[:, :].unsqueeze(1).broadcast_to([P, TILES, D]), ALU.add).then_inc(g.dve_out[u], 1)
    dve_norm(v, g, i, "n0", lambda u: g.rows[u], lambda u: (g.dve_out[u], upto(g.DVE, i, "h0b")), lambda u: g.z[u])
    for u in g.streams:
        v.wait_ge(g.pe_out[u], upto(g.PE, i, "y0"))
        v.scalar_tensor_tensor(out=g.yT[u][:, :], in0=g.bank(u), scalar=g.c.b2[:, 0:1], in1=g.xT[u][:, :],
                               op0=ALU.add, op1=ALU.add).then_inc(g.dve_out[u], 1)
    dve_norm(v, g, i, "n1", lambda u: tiles_of(g.bank(u)), lambda u: (g.pe_out[u], upto(g.PE, i, "y0r")),
             lambda u: g.x1[u], lambda u: (g.x1_stored[u], i * 16))


def update1(g, tail_T):
    g.PE += ["h1", "z1", "y1r"] + (["x2T"] if tail_T else [])
    g.ACT += ["gelu1"] + (["x2T"] if tail_T else [])
    g.DVE += ["h1b"] + norm_steps("n2") + ["y1T"] + norm_steps("n3")
    g.POOL += ["n2_rstd", "n3_pow", "n3_rstd"] if g.slots else ["n2_rstd", "n3_rstd"]


def pe_update1(pe, g, i, tail_T):
    for u in g.streams:
        if g.slots:
            pe.wait_ge(g.dve_out[u], upto(g.DVE, i, "agg"))
        else:
            pe.wait_ge(g.act_out[u], upto(g.ACT, i, "x1T"))
        for t in range(TILES):
            cols = slice(t * P, (t + 1) * P)
            if g.slots:
                ins = pe.transpose(g.bank(u)[:, cols], g.agg[u][:, cols], g.c.ident[:, :])
            else:
                ins = pe.matmul(g.bank(u)[:, cols], g.xT1[u][:, cols], g.c.W[:, :], start=True, stop=True)
        ins.then_inc(g.pe_out[u], 1)
    pe_rows_to_T(pe, g, i, lambda u: g.z[u], lambda u: (g.dve_out[u], upto(g.DVE, i, "n2_norm")), g.bank)
    pe_T_to_rows(pe, g, i, lambda u: g.yT[u], lambda u: (g.dve_out[u], upto(g.DVE, i, "y1T")), g.bank)
    if tail_T:
        pe_rows_to_T(pe, g, i, lambda u: g.x2[u], lambda u: (g.dve_out[u], upto(g.DVE, i, "n3_norm")), g.bank)


def act_update1(act, g, i, tail_T):
    act_copy(act, g, lambda u: g.act_T[u][:, :], lambda u: g.bank(u),
             lambda u: (g.pe_out[u], upto(g.PE, i, "z1")), ACT.Gelu, g.c.beta[:, 0:1], g.c.gamma[:, 0:1])
    if tail_T:
        act_copy(act, g, lambda u: g.xT2[u][:, :], lambda u: g.bank(u), lambda u: (g.pe_out[u], upto(g.PE, i, "x2T")))


def dve_update1(v, g, i):
    for u in g.streams:
        v.wait_ge(g.pe_out[u], upto(g.PE, i, "h1"))
        v.tensor_tensor(g.rows[u][:, :, :], tiles_of(g.bank(u)),
                        g.c.bias_row[:, :].unsqueeze(1).broadcast_to([P, TILES, D]), ALU.add).then_inc(g.dve_out[u], 1)
    dve_norm(v, g, i, "n2", lambda u: g.rows[u], lambda u: (g.dve_out[u], upto(g.DVE, i, "h1b")), lambda u: g.z[u])
    for u in g.streams:
        v.wait_ge(g.act_out[u], upto(g.ACT, i, "gelu1"))
        v.tensor_tensor(g.yT[u][:, :], g.act_T[u][:, :], g.xT1[u][:, :], ALU.add).then_inc(g.dve_out[u], 1)
    dve_norm(v, g, i, "n3", lambda u: tiles_of(g.bank(u)), lambda u: (g.pe_out[u], upto(g.PE, i, "y1r")),
             lambda u: g.x2[u], lambda u: (g.x2_stored[u], i * 16))


def update2a(g):
    g.PE += ([] if g.slots else ["z2"]) + ["xl"]
    g.ACT += ["exp2"]
    g.DVE += ["h2_em1", "h2", "xl"]


def pe_update2a(pe, g, i):
    if not g.slots:
        pe_product(pe, g, g.c.Wl1[:, :], lambda u: g.xT2[u][:, :], lambda u: (g.act_out[u], upto(g.ACT, i, "x2T")), g.bank)
    for u in g.streams:
        pe.wait_ge(g.dve_out[u], upto(g.DVE, i, "h2"))
        for t in range(TILES):
            ins = pe.matmul(g.bank(u)[:, t * C2:(t + 1) * C2], g.act_T[u][:, t * P:(t + 1) * P], g.c.Wl2[:, :],
                            start=True, stop=True)
        ins.then_inc(g.pe_out[u], 1)


def act_update2a(act, g, i):
    if g.slots:
        act_copy(act, g, lambda u: g.expz[u][:, :], lambda u: g.agg[u][:, :],
                 lambda u: (g.dve_out[u], upto(g.DVE, i, "agg")), ACT.Exp, g.c.bias1[:, 0:1])
    else:
        act_copy(act, g, lambda u: g.expz[u][:, :], lambda u: g.bank(u),
                 lambda u: (g.pe_out[u], upto(g.PE, i, "z2")), ACT.Exp, g.c.node_bias1[:, 0:1])


def dve_update2a(v, g, i):
    bias = g.c.bias1 if g.slots else g.c.node_bias1
    dve_elu(v, g, i, "h2", (lambda u: g.agg[u][:, :]) if g.slots else (lambda u: g.bank(u)), bias[:, 0:1],
            lambda u: (g.act_out[u], upto(g.ACT, i, "exp2")))
    for u in g.streams:
        v.wait_ge(g.pe_out[u], upto(g.PE, i, "xl"))
        v.wait_ge(g.xl_stored[u], i * 16)
        v.tensor_tensor(g.xl[u][:, :, :], g.bank(u)[:, 0:TILES * C2].rearrange("p (t n) -> p t n", t=TILES),
                        g.c.bl2_row[:, :].unsqueeze(1).broadcast_to([P, TILES, C2]), ALU.add).then_inc(g.dve_out[u], 1)


def update2b(g):
    g.PE += ([] if g.slots else ["z3"]) + ["z4", "y2r"]
    g.ACT += ["exp3", "exp4"]
    g.DVE += ["h3_em1", "h3", "h4_em1", "h4", "y2T"] + norm_steps("n4")
    g.POOL += ["n4_pow", "n4_rstd"] if g.slots else ["n4_rstd"]


def pe_update2b(pe, g, i):
    if not g.slots:
        pe_product(pe, g, g.c.Wl2[:, :], lambda u: g.act_T[u][:, :], lambda u: (g.dve_out[u], upto(g.DVE, i, "xl")),
                   g.bank, C2)
    pe_product(pe, g, g.c.Wlin[:, :], lambda u: g.act_T[u][0:C2, :], lambda u: (g.dve_out[u], upto(g.DVE, i, "h3")), g.bank)
    pe_T_to_rows(pe, g, i, lambda u: g.yT[u], lambda u: (g.dve_out[u], upto(g.DVE, i, "y2T")), g.bank)


def act_update2b(act, g, i):
    if g.slots:
        act_copy(act, g, lambda u: g.expz[u][0:C2, :], lambda u: g.agg[u][0:C2, :],
                 lambda u: (g.dve_out[u], upto(g.DVE, i, "agg")), ACT.Exp, g.c.bias2[:, 0:1])
    else:
        act_copy(act, g, lambda u: g.expz[u][0:C2, :], lambda u: g.bank(u)[0:C2, :],
                 lambda u: (g.pe_out[u], upto(g.PE, i, "z3")), ACT.Exp, g.c.node_bias2[:, 0:1])
    act_copy(act, g, lambda u: g.expz[u][:, :], lambda u: g.bank(u), lambda u: (g.pe_out[u], upto(g.PE, i, "z4")),
             ACT.Exp, g.c.blin[:, 0:1])


def dve_update2b(v, g, i):
    bias = g.c.bias2 if g.slots else g.c.node_bias2
    dve_elu(v, g, i, "h3", (lambda u: g.agg[u][0:C2, :]) if g.slots else (lambda u: g.bank(u)[0:C2, :]),
            bias[:, 0:1], lambda u: (g.act_out[u], upto(g.ACT, i, "exp3")), C2)
    dve_elu(v, g, i, "h4", lambda u: g.bank(u), g.c.blin[:, 0:1], lambda u: (g.act_out[u], upto(g.ACT, i, "exp4")))
    for u in g.streams:
        v.wait_ge(g.dve_out[u], upto(g.DVE, i, "h4"))
        if g.slots:
            v.wait_ge(g.res_ready[u], (i + 1) * 16)
        v.tensor_tensor(g.yT[u][:, :], g.act_T[u][:, :], g.res2(u), ALU.add).then_inc(g.dve_out[u], 1)
    dve_norm(v, g, i, "n4", lambda u: tiles_of(g.bank(u)), lambda u: (g.pe_out[u], upto(g.PE, i, "y2r")),
             lambda u: g.x3[u], lambda u: (g.x3_stored[u], i * 16))



def node_pass(nc, a, c, dram):
    with ExitStack() as ctx:
        g = Named(c)
        phase_tiles(ctx, nc, g, NODE_STREAMS, "node")
        update0(g, True)
        update1(g, True)
        update2a(g)
        update2b(g)
        g.DVE += norm_steps("n5")
        g.POOL += ["n5_rstd"]
        g.xT = g.many("xT", [P, CHUNK])
        g.rows = g.many("rows", [P, TILES, D])
        g.z = g.many("z", [P, TILES, D])
        g.act_T = g.many("act_T", [P, CHUNK])
        g.yT = g.many("yT", [P, CHUNK])
        g.expz = g.many("expz", [P, CHUNK])
        g.x1 = g.many("x1", [P, TILES, D])
        g.x2 = g.many("x2", [P, TILES, D])
        g.x3 = g.many("x3", [P, TILES, D])
        g.x4 = g.many("x4", [P, TILES, D])
        g.xl = g.many("xl", [P, TILES, C2])
        g.xT1 = g.many("xT1", [P, CHUNK])
        g.xT2 = g.many("xT2", [P, CHUNK])
        g.res2 = lambda u: g.xT2[u][:, :]
        g.bank = lambda u: c.psum[:, u, :]
        x_loaded = g.sems("x_loaded")
        g.x1_stored, g.x2_stored, g.x3_stored = g.sems("x1_stored"), g.sems("x2_stored"), g.sems("x3_stored")
        g.xl_stored, x4_stored = g.sems("xl_stored"), g.sems("x4_stored")
        g.xT_ready = lambda u, i: (x_loaded[u], i * 16 + 16)
        g.bank_free = lambda u, i: i * len(g.DVE)

        per_iter = SLOTS_PER_ITER // P
        gathered = [g.sb(f"gathered{k}", [P, per_iter, D]) for k in range(2)]
        index = [g.sb(f"index{k}", [P, per_iter], I32) for k in range(4)]
        value = [g.sb(f"value{k}", [P, per_iter], I32) for k in range(2)]
        gathers_done = [g.sem(f"gathers_done{k}") for k in range(2)]
        staged = [g.sem(f"staged{k}") for k in range(2)]
        scattered = [g.sem(f"scattered{k}") for k in range(2)]
        index_ready = g.sem("index_ready")
        side = [(k, t) for t in range(per_iter) for k in range(4)]
        turns = len(g.POOL) * NODE_STREAMS
        share = [len(side) * n // turns for n in range(turns + 1)]
        ctx.callback(end_phase, nc, g.all_sems)
        block = ctx.enter_context(nc.Block())

        @block.sync
        def _(sp):
            with sp.Fori(0, ITERS) as i:
                for u in g.streams:
                    sp.wait_ge(g.dve_out[u], i * len(g.DVE))
                    sp.dma_start(g.xT[u][:, :], a["x_T"][:, ds(i * NODES_PER_ITER + u * CHUNK, CHUNK)]).then_inc(x_loaded[u], 16)
                for k in range(2):
                    sp.wait_ge(gathers_done[k], (i + 1) * 16 * per_iter)
                    sp.dma_start(dram.staged[k][ds(i * SLOTS_PER_ITER, SLOTS_PER_ITER), :].rearrange("(t p) f -> p t f", p=P),
                                 gathered[k][:, :, :]).then_inc(staged[k], 16)
            for k in range(2):
                sp.wait_ge(staged[k], 16 * ITERS)

        @block.scalar
        def _(act):
            def store(i, u, table, tile, step, stored):
                act.wait_ge(g.dve_out[u], upto(g.DVE, i, step))
                act.dma_start(table[ds(i * NODES_PER_ITER + u * CHUNK, CHUNK), :].rearrange("(t p) f -> p t f", p=P),
                              tile[u][:, :, :]).then_inc(stored[u], 16)

            with act.Fori(0, ITERS) as i:
                act_update0(act, g, i, True)
                for u in g.streams:
                    store(i, u, dram.x1, g.x1, "n1_norm", g.x1_stored)
                act_update1(act, g, i, True)
                for u in g.streams:
                    store(i, u, dram.x2, g.x2, "n3_norm", g.x2_stored)
                act_update2a(act, g, i)
                for u in g.streams:
                    store(i, u, dram.xl2, g.xl, "xl", g.xl_stored)
                act_update2b(act, g, i)
                for u in g.streams:
                    store(i, u, dram.x3, g.x3, "n4_norm", g.x3_stored)
                for u in g.streams:
                    store(i, u, a["out"], g.x4, "n5_norm", x4_stored)
            for stored in (g.x1_stored, g.x2_stored, g.xl_stored, g.x3_stored, x4_stored):
                for u in g.streams:
                    act.wait_ge(stored[u], 16 * ITERS)

        @block.tensor
        def _(pe):
            with pe.Fori(0, ITERS) as i:
                pe_update0(pe, g, i, True)
                pe_update1(pe, g, i, True)
                pe_update2a(pe, g, i)
                pe_update2b(pe, g, i)

        @block.vector
        def _(v):
            with v.Fori(0, ITERS) as i:
                dve_update0(v, g, i)
                dve_update1(v, g, i)
                dve_update2a(v, g, i)
                dve_update2b(v, g, i)
                dve_norm(v, g, i, "n5", lambda u: g.x3[u], lambda u: (g.dve_out[u], upto(g.DVE, i, "n4_norm")),
                         lambda u: g.x4[u], lambda u: (x4_stored[u], i * 16))

        @block.gpsimd
        def _(pool):
            lists = (c.src_cols, c.dst_gather_cols, c.map_index[0], c.map_index[1])
            copies = len(lists) + len(value)
            with pool.Fori(0, ITERS) as i:
                for k in range(2):
                    pool.wait_ge(staged[k], i * 16)
                    pool.tensor_copy(index[k][:, :], lists[k][:, ds(i * per_iter, per_iter)]).then_inc(index_ready, 1)
                for k in range(2):
                    pool.wait_ge(scattered[k], i * 16 * per_iter)
                    pool.tensor_copy(index[2 + k][:, :], lists[2 + k][:, ds(i * per_iter, per_iter)]).then_inc(index_ready, 1)
                    pool.tensor_copy(value[k][:, :], c.payload[k][:, ds(i * per_iter, per_iter)]).then_inc(index_ready, 1)
                pool.wait_ge(index_ready, copies)
                turn = 0
                for tag in ("n0", "n1", "n2", "n3", "n4", "n5"):
                    for u in g.streams:
                        pool_rstd(pool, g, i, tag, u)
                        for k, t in side[share[turn]:share[turn + 1]]:
                            if k < 2:
                                pool.indirect_dma_start(gathered[k][:, t, :], None, a["x"],
                                                        at_index(index[k][:, t:t + 1], 0)).then_inc(gathers_done[k], 16)
                            else:
                                pool.indirect_dma_start(dram.slot_map_flat, at_index(index[k][:, t:t + 1], 0),
                                                        value[k - 2][:, t:t + 1], None, bounds_check=2 * N - 1,
                                                        oob_is_err=False).then_inc(scattered[k - 2], 16)
                        turn += 1
                pool.sem_clear(index_ready)
            for k in range(2):
                pool.wait_ge(scattered[k], 16 * per_iter * ITERS)



HEADS = {"0": 16, "1": 4, "2a": 8, "2b": 1, "3": 4}
ORDER = {"0": 0, "1": 1, "2a": 0, "2b": 1, "3": 0}


def slot_pass(nc, a, c, dram, layer):
    H = HEADS[layer]
    order = ORDER[layer]
    M = C2 if layer == "2b" else P
    own = layer in ("1", "2a", "2b")
    terms = 2 if layer == "0" else 3
    last_iter = ITERS - 1
    with ExitStack() as ctx:
        g = Named(c, True, c.last[order])
        phase_tiles(ctx, nc, g, SLOT_STREAMS, f"slot{layer}")

        def bank(k):
            return lambda u: c.psum[:, 4 * u + k, :]

        g.bank = bank(0)

        g.PE += ["srcT"] + ([] if layer == "2b" else ["dstT"])
        g.PE += {"0": ["k", "q", "e0", "v", "e1", "l"], "1": ["hs", "hd", "l", "ls"],
                 "2a": ["xs", "xd", "xr", "l", "ls"], "2b": ["xd", "xr", "l", "ls"], "3": ["hs", "l"]}[layer]
        g.ACT += ["srcT"] + (["dstT"] if layer == "0" else [])
        g.ACT += {"0": ["k", "e0", "e1", "l"], "1": ["hs", "hd", "l", "ls"], "2a": ["xs", "xd", "l", "ls"],
                  "2b": ["xd", "l", "ls"], "3": ["hs", "l"]}[layer]
        g.DVE += {"0": [], "2b": ["mask", "dst"]}.get(layer, ["dst"])
        g.DVE += {"0": ["qk", "qke", "v"], "1": ["l", "ls"], "2a": ["zs", "zd", "es", "ed"],
                  "2b": ["zs", "zd", "es", "ed"], "3": ["l", "deg"]}[layer]
        g.DVE += ([] if layer == "0" else ["lm"]) + ["fc", "f", "shift", "e_p", "e_c"] + ([] if layer == "0" else ["e_s"])
        g.ACT += ["exp"]
        g.DVE += ["den"] + (["zt"] if layer == "3" else []) + ["dq", "pv", "rec", "num"] + (["sv", "ns"] if own else [])
        g.DVE += ["agg"]
        g.PE += ["pB", "cB"] + (["sB"] if own else []) + ["dqT", "rT", "rB"]
        g.ACT += ["rT"]
        if layer == "0":
            update0(g, False)
        if layer == "1":
            update1(g, False)
        if layer == "2a":
            update2a(g)
        if layer == "2b":
            update2b(g)
        if layer == "3":
            g.PE += ["y3r"]
            g.DVE += ["y3T"] + norm_steps("n5")
            g.POOL += ["n5_rstd"]

        src_width = C2 if layer == "2b" else D
        src_rows = g.many("src_rows", [P, TILES, D])
        dst_rows = g.many("dst_rows", [P, TILES, D])
        keep = g.many("keep", [P, CHUNK])
        neg = g.many("neg", [H, CHUNK])
        edge = g.many("edge", [EF, CHUNK])
        xs = g.many("xs", [P, CHUNK])
        xd = g.many("xd", [P, CHUNK])
        val = xs if layer == "2b" else g.many("val", [P, CHUNK])
        val_own = g.many("val_own", [P, CHUNK])
        t1 = g.many("t1", [P, CHUNK])
        t2 = g.many("t2", [P, CHUNK])
        h2_before = g.many("h2_before", [P, CHUNK])
        logit = g.many("logit", [H, CHUNK])
        logit_own = g.many("logit_own", [H, CHUNK])
        logit_max = g.many("logit_max", [H, CHUNK])
        fmax = g.many("fmax", [H, CHUNK + 1])
        expo = g.many("expo", [H, terms, CHUNK])
        den = g.many("den", [H, CHUNK])
        rest = g.many("rest", [H, CHUNK])
        total = g.many("total", [H, CHUNK])
        recip = g.many("recip", [P, TILES, H])
        recip_T = g.many("recip_T", [H, CHUNK])
        num = g.many("num", [P, CHUNK])
        deg = g.many("deg", [H, CHUNK])
        g.agg = g.many("agg", [P, CHUNK])
        g.rows = g.many("rows", [P, TILES, D])
        g.z = g.many("z", [P, TILES, D])
        g.act_T = g.many("act_T", [P, CHUNK])
        g.yT = g.many("yT", [P, CHUNK])
        g.expz = g.many("expz", [P, CHUNK])
        g.xl = g.many("xl", [P, TILES, C2])
        new = g.many("new", [P, TILES, D])
        g.x1 = g.x2 = g.x3 = new
        g.xT = g.xT1 = xd
        carry_max, carry_den, carry_deg = (g.sb(n, [H, 1]) for n in ("carry_max", "carry_den", "carry_deg"))
        carry_num, carry_x = g.sb("carry_num", [P, 1]), g.sb("carry_x", [P, 1])
        index, out_index = g.many("index", [P, TILES], I32), g.many("out_index", [P, TILES], I32)
        map_index = g.sb("map_index", [P, SLOTS_PER_ITER // P], I32)
        map_rows = g.sb("map_rows", [P, SLOTS_PER_ITER // P, 2], I32)

        src_ready, dst_ready = g.sems("src_ready"), g.sems("dst_ready")
        keep_ready, neg_ready = g.sems("keep_ready"), g.sems("neg_ready")
        edge_ready, g.res_ready = g.sems("edge_ready"), g.sems("res_ready")
        stored, stored_T = g.sems("stored"), g.sems("stored_T")
        per_chunk = 16 * TILES if layer == "3" else 16
        g.x1_stored = g.x2_stored = g.x3_stored = g.xl_stored = stored
        max_carried, den_carried, num_carried = g.sem("max_carried"), g.sem("den_carried"), g.sem("num_carried")
        x_carried, deg_carried = g.sem("x_carried"), g.sem("deg_carried")
        cleared = g.sem("cleared")
        index_ready, map_ready, map_kept = g.sem("index_ready"), g.sem("map_ready"), g.sem("map_kept")

        g.xT_ready = lambda u, i: (g.dve_out[u], upto(g.DVE, i, "agg"))
        g.bank_free = lambda u, i: upto(g.DVE, i, "agg")
        g.res2 = lambda u: dst_rows[u][:, :, :].rearrange("p t n -> p (t n)")[:, ::-1]
        chunk = lambda i, u: i * SLOT_STREAMS + u
        start = lambda i, u: i * SLOTS_PER_ITER + u * CHUNK
        mirrored = lambda i, u: i * -SLOTS_PER_ITER + (E_PAD - (u + 1) * CHUNK)
        table = {"1": dram.x1, "2a": dram.x2, "2b": dram.xl2, "3": dram.x3}.get(layer)

        def rows_of(array, first):
            return array[ds(first, CHUNK), :].rearrange("(t p) f -> p t f", p=P)

        ctx.callback(end_phase, nc, g.all_sems)
        block = ctx.enter_context(nc.Block())

        @block.sync
        def _(sp):
            def load(i, first):
                for u in g.streams:
                    if not first:
                        sp.wait_ge(g.dve_out[u], upto(g.DVE, i - 1, "shift"))
                    sp.dma_start(neg[u][:, :], dram.neg_flat[order][ds(start(i, u), CHUNK)].partition_broadcast(H))\
                      .then_inc(neg_ready[u], 16)
                    if layer != "0":
                        sp.dma_start(keep[u][:, :], dram.keep_flat[order][ds(start(i, u), CHUNK)].partition_broadcast(P))\
                          .then_inc(keep_ready[u], 16)
                    if layer == "0":
                        sp.dma_start(src_rows[u][:, :, :], rows_of(dram.staged[0], start(i, u))).then_inc(src_ready[u], 16)
                        sp.dma_start(dst_rows[u][:, :, :], rows_of(dram.staged[1], start(i, u))).then_inc(dst_ready[u], 16)
                    elif layer == "2b":
                        sp.dma_start(h2_before[u][:, :], dram.h2_T[:, ds(mirrored(i, u), CHUNK)]).then_inc(dst_ready[u], 16)
                    else:
                        sp.dma_start(dst_rows[u][:, :, :], rows_of(table, mirrored(i, u) + N_PAD)).then_inc(dst_ready[u], 16)
                    if layer in ("0", "3"):
                        sp.dma_start(edge[u][:, :], a["edge_T"][:, ds(start(i, u), CHUNK)]).then_inc(edge_ready[u], 16)
                    if layer == "2b":
                        if not first:
                            sp.wait_ge(g.dve_out[u], upto(g.DVE, i - 1, "y2T"))
                        sp.dma_start(dst_rows[u][:, :, :].rearrange("p t n -> p (t n)"),
                                     dram.x2_T[:, ds(mirrored(i, u), CHUNK)]).then_inc(g.res_ready[u], 16)

            load(0, True)
            with sp.Fori(1, ITERS) as i:
                load(i, False)

        @block.gpsimd
        def _(pool):
            def gather_sources(i):
                for u in g.streams:
                    pool.tensor_copy(index[u][:, :], c.src_table_cols[order][:, ds(chunk(i, u) * TILES, TILES)])\
                        .then_inc(index_ready, 1)
                pool.wait_ge(index_ready, SLOT_STREAMS)
                for u in g.streams:
                    for t in range(TILES):
                        pool.indirect_dma_start(src_rows[u][:, t, 0:src_width], None, table, at_index(index[u][:, t:t + 1], 0))\
                            .then_inc(src_ready[u], 16)
                pool.sem_clear(index_ready)

            def gather_map(i):
                n = SLOTS_PER_ITER // P
                pool.tensor_copy(map_index[:, :], c.src_cols[:, ds(i * n, n)]).then_inc(index_ready, 1)
                pool.wait_ge(index_ready, 1)
                for t in range(n):
                    pool.indirect_dma_start(map_rows[:, t, :], None, dram.slot_map, at_index(map_index[:, t:t + 1], 0))\
                        .then_inc(map_ready, 16)
                pool.sem_clear(index_ready)
                pool.wait_ge(map_ready, (i + 1) * 16 * n)
                pool.tensor_copy(c.map_cols[:, ds(i * n, n), :], map_rows[:, :, :]).then_inc(map_kept, 1)
                pool.wait_ge(map_kept, i + 1)

            def rstds(i):
                for tag in {"0": ["n0", "n1"], "1": ["n2", "n3"], "2a": [], "2b": ["n4"], "3": ["n5"]}[layer]:
                    for u in g.streams:
                        if tag in ("n1", "n3", "n4"):
                            pool_rstd_last(pool, g, i, tag, u)
                        else:
                            pool_rstd(pool, g, i, tag, u)

            def scatter_output(i):
                for u in g.streams:
                    pool.wait_ge(g.dve_out[u], upto(g.DVE, i, "n5_norm"))
                    pool.tensor_copy(out_index[u][:, :], c.out_index[:, ds(chunk(i, u) * TILES, TILES)])\
                        .then_inc(index_ready, 1)
                pool.wait_ge(index_ready, SLOT_STREAMS)
                for u in g.streams:
                    for t in range(TILES):
                        pool.indirect_dma_start(a["out"], at_index(out_index[u][:, t:t + 1], 0), new[u][:, t, :], None,
                                                bounds_check=N - 1, oob_is_err=False).then_inc(stored[u], 16)
                pool.sem_clear(index_ready)

            if layer == "0":
                with pool.Fori(0, ITERS) as i:
                    gather_map(i)
                    rstds(i)
            else:
                if layer == "2b":
                    for u in g.streams:
                        pool.memset(src_rows[u][:, :, src_width:], 0.0).then_inc(cleared, 1)
                    pool.wait_ge(cleared, SLOT_STREAMS)
                gather_sources(0)
                with pool.Fori(0, last_iter) as i:
                    for u in g.streams:
                        pool.wait_ge(g.pe_out[u], upto(g.PE, i, "srcT"))
                    gather_sources(i + 1)
                    rstds(i)
                    if layer == "3":
                        scatter_output(i)
                rstds(last_iter)
                if layer == "3":
                    scatter_output(last_iter)
                    for u in g.streams:
                        pool.wait_ge(stored[u], per_chunk * ITERS)

        @block.scalar
        def _(act):
            def store(i, u, array, tile, step, stored):
                act.wait_ge(g.dve_out[u], upto(g.DVE, i, step))
                act.dma_start(rows_of(array, start(i, u) + N_PAD), tile[u][:, :, :]).then_inc(stored[u], 16)

            def store_T(i, u, array, tile, step):
                act.wait_ge(g.dve_out[u], upto(g.DVE, i, step))
                act.dma_start(array[:, ds(start(i, u), CHUNK)], tile[u][:, :]).then_inc(stored_T[u], 16)

            with act.Fori(0, ITERS) as i:
                from_pe = lambda step: (lambda u: (g.pe_out[u], upto(g.PE, i, step)))
                act_copy(act, g, lambda u: xs[u][0:src_width, :], lambda u: bank(0)(u)[0:src_width, :], from_pe("srcT"))
                if layer == "0":
                    act_copy(act, g, lambda u: xd[u][:, :], bank(1), from_pe("dstT"))
                    act_copy(act, g, lambda u: t1[u][:, :], bank(2), from_pe("k"))
                    act_copy(act, g, lambda u: t2[u][:, :], bank(0), from_pe("e0"), ACT.Tanh)
                    act_copy(act, g, lambda u: val_own[u][:, :], bank(2), from_pe("e1"), ACT.Tanh)
                    act_copy(act, g, lambda u: logit[u][:, :], lambda u: bank(3)(u)[0:H, :], from_pe("l"),
                             scale=float((D // H) ** -0.5))
                if layer == "1":
                    act_copy(act, g, lambda u: val[u][:, :], bank(2), from_pe("hs"))
                    act_copy(act, g, lambda u: val_own[u][:, :], bank(3), from_pe("hd"))
                    act_copy(act, g, lambda u: t1[u][0:H, :], lambda u: bank(0)(u)[0:H, :], from_pe("l"), scale=SLOPE)
                    act_copy(act, g, lambda u: t2[u][0:H, :], lambda u: bank(1)(u)[0:H, :], from_pe("ls"), scale=SLOPE)
                if layer == "2a":
                    act_copy(act, g, lambda u: val[u][:, :], bank(2), from_pe("xs"), ACT.Identity, c.bl1[:, 0:1])
                    act_copy(act, g, lambda u: val_own[u][:, :], bank(3), from_pe("xd"), ACT.Identity, c.bl1[:, 0:1])
                    act_copy(act, g, lambda u: logit[u][:, :], lambda u: bank(1)(u)[0:H, :], from_pe("l"))
                    act_copy(act, g, lambda u: logit_own[u][:, :], lambda u: bank(2)(u)[0:H, :], from_pe("ls"))
                if layer == "2b":
                    act_copy(act, g, lambda u: val_own[u][0:M, :], lambda u: bank(3)(u)[0:M, :], from_pe("xd"),
                             ACT.Identity, c.bl2[:, 0:1])
                    act_copy(act, g, lambda u: logit[u][:, :], lambda u: bank(2)(u)[0:H, :], from_pe("l"))
                    act_copy(act, g, lambda u: logit_own[u][:, :], lambda u: bank(0)(u)[0:H, :], from_pe("ls"))
                if layer == "3":
                    act_copy(act, g, lambda u: val[u][:, :], bank(2), from_pe("hs"))
                    act_copy(act, g, lambda u: t1[u][0:H, :], lambda u: bank(3)(u)[0:H, :], from_pe("l"), scale=SLOPE)
                act_copy(act, g, lambda u: expo[u][:, :, :], lambda u: expo[u][:, :, :],
                         lambda u: (g.dve_out[u], upto(g.DVE, i, "e_c" if layer == "0" else "e_s")), ACT.Exp)
                act_copy(act, g, lambda u: recip_T[u][:, :], lambda u: bank(3)(u)[0:H, :], from_pe("rT"))
                if layer == "0":
                    act_update0(act, g, i, False)
                    for u in g.streams:
                        store(i, u, dram.x1, new, "n1_norm", stored)
                if layer == "1":
                    act_update1(act, g, i, False)
                    for u in g.streams:
                        store(i, u, dram.x2, new, "n3_norm", stored)
                if layer == "2a":
                    act_update2a(act, g, i)
                    for u in g.streams:
                        store_T(i, u, dram.x2_T, xd, "dst")
                        store_T(i, u, dram.h2_T, g.act_T, "h2")
                        store(i, u, dram.xl2, g.xl, "xl", stored)
                if layer == "2b":
                    act_update2b(act, g, i)
                    for u in g.streams:
                        store(i, u, dram.x3, new, "n4_norm", stored)
            if layer != "3":
                for u in g.streams:
                    act.wait_ge(stored[u], 16 * ITERS)
            if layer == "2a":
                for u in g.streams:
                    act.wait_ge(stored_T[u], 32 * ITERS)

        @block.tensor
        def _(pe):
            with pe.Fori(0, ITERS) as i:
                from_act = lambda step: (lambda u: (g.act_out[u], upto(g.ACT, i, step)))
                from_dve = lambda step: (lambda u: (g.dve_out[u], upto(g.DVE, i, step)))
                for u in g.streams:
                    pe.wait_ge(src_ready[u], (i + 1) * (16 if layer == "0" else 16 * TILES))
                    pe.wait_ge(g.dve_out[u], i * len(g.DVE))
                    for t in range(TILES):
                        ins = pe.transpose(bank(0)(u)[:, t * P:(t + 1) * P], src_rows[u][:, t, :], c.ident[:, :])
                    ins.then_inc(g.pe_out[u], 1)
                if layer != "2b":
                    pe_rows_to_T(pe, g, i, lambda u: dst_rows[u], lambda u: (dst_ready[u], (i + 1) * 16), bank(1))
                if layer == "0":
                    pe_product(pe, g, c.Wk[:, :], lambda u: xs[u][:, :], from_act("srcT"), bank(2))
                    pe_product(pe, g, c.Wq[:, :], lambda u: xd[u][:, :], from_act("dstT"), bank(3))
                    pe_product(pe, g, c.We0[:, :], lambda u: edge[u][:, :], lambda u: (edge_ready[u], (i + 1) * 16), bank(0))
                    pe_product(pe, g, c.Wv[:, :], lambda u: xs[u][:, :], from_act("dstT"), bank(1))
                    pe_product(pe, g, c.We1[:, :], lambda u: edge[u][:, :], from_act("k"), bank(2))
                    pe_product(pe, g, c.collect16[:, :], lambda u: t1[u][:, :], from_dve("qke"), bank(3), H)
                if layer == "1":
                    pe_product(pe, g, c.W[:, :], lambda u: xs[u][:, :], from_act("srcT"), bank(2))
                    pe_product(pe, g, c.W[:, :], lambda u: xd[u][:, :], from_dve("dst"), bank(3))
                    for u in g.streams:
                        pe.wait_ge(g.act_out[u], upto(g.ACT, i, "hd"))
                        pe.matmul(bank(0)(u)[0:H, :], c.att_s[:, :], val[u][:, :], start=True, stop=False)
                        pe.matmul(bank(0)(u)[0:H, :], c.att_d[:, :], val_own[u][:, :], start=False, stop=True)\
                          .then_inc(g.pe_out[u], 1)
                    pe_product(pe, g, c.att_sd[:, :], lambda u: val_own[u][:, :], from_dve("dst"), bank(1), H)
                if layer == "2a":
                    pe_product(pe, g, c.Wl1[:, :], lambda u: xs[u][:, :], from_act("srcT"), bank(2))
                    pe_product(pe, g, c.Wl1[:, :], lambda u: xd[u][:, :], from_dve("dst"), bank(3))
                    pe_product(pe, g, c.Wr1[:, :], lambda u: xd[u][:, :], from_dve("dst"), bank(0))
                    pe_product(pe, g, c.att1[:, :], lambda u: t1[u][:, :], from_dve("es"), bank(1), H)
                    pe_product(pe, g, c.att1[:, :], lambda u: t2[u][:, :], from_dve("ed"), bank(2), H)
                if layer == "2b":
                    pe_product(pe, g, c.Wl2[:, :], lambda u: xd[u][:, :], from_dve("dst"), bank(3), M)
                    pe_product(pe, g, c.Wr2[:, :], lambda u: xd[u][:, :], from_dve("dst"), bank(1), M)
                    pe_product(pe, g, c.att2[:, :], lambda u: t1[u][0:M, :], from_dve("es"), bank(2))
                    pe_product(pe, g, c.att2[:, :], lambda u: t2[u][0:M, :], from_dve("ed"), bank(0))
                if layer == "3":
                    pe_product(pe, g, c.WnT[:, :], lambda u: xs[u][:, :], from_act("srcT"), bank(2))
                    for u in g.streams:
                        pe.wait_ge(g.act_out[u], upto(g.ACT, i, "hs"))
                        pe.wait_ge(g.dve_out[u], upto(g.DVE, i, "dst"))
                        pe.wait_ge(edge_ready[u], (i + 1) * 16)
                        pe.matmul(bank(3)(u)[0:H, :], c.a_src[:, :], val[u][:, :], start=True, stop=False)
                        pe.matmul(bank(3)(u)[0:H, :], c.W_tgt[:, :], xd[u][:, :], start=False, stop=False)
                        pe.matmul(bank(3)(u)[0:H, :], c.W_edge[:, :], edge[u][:, :], start=False, stop=True)\
                          .then_inc(g.pe_out[u], 1)
                pe_product(pe, g, c.spread[H][:, :], lambda u: expo[u][:, 0, :], from_act("exp"), bank(0), M)
                pe_product(pe, g, c.spread[H][:, :], lambda u: expo[u][:, 1, :], from_act("exp"), bank(1), M)
                if own:
                    pe_product(pe, g, c.spread[H][:, :], lambda u: expo[u][:, 2, :], from_act("exp"), bank(2), M)
                for u in g.streams:
                    pe.wait_ge(g.dve_out[u], upto(g.DVE, i, "dq"))
                    for t in range(TILES):
                        ins = pe.matmul(bank(3)(u)[:, t * H:(t + 1) * H], total[u][:, t * P:(t + 1) * P], c.ident[0:H, 0:H],
                                        start=True, stop=True)
                    ins.then_inc(g.pe_out[u], 1)
                for u in g.streams:
                    pe.wait_ge(g.dve_out[u], upto(g.DVE, i, "rec"))
                    for t in range(TILES):
                        ins = pe.transpose(bank(3)(u)[0:H, t * P:(t + 1) * P], recip[u][:, t, :], c.ident[:, :])
                    ins.then_inc(g.pe_out[u], 1)
                pe_product(pe, g, c.spread[H][:, :], lambda u: recip_T[u][:, :], from_act("rT"), bank(3), M)
                if layer == "0":
                    pe_update0(pe, g, i, False)
                if layer == "1":
                    pe_update1(pe, g, i, False)
                if layer == "2a":
                    pe_update2a(pe, g, i)
                if layer == "2b":
                    pe_update2b(pe, g, i)
                if layer == "3":
                    pe_T_to_rows(pe, g, i, lambda u: g.yT[u], from_dve("y3T"), g.bank)

        @block.vector
        def _(v):
            for t, carried in ((carry_max, max_carried), (carry_den, den_carried), (carry_num, num_carried),
                               (carry_x, x_carried), (carry_deg, deg_carried)):
                v.memset(t[:, :], 0.0).then_inc(carried, 1)

            with v.Fori(0, ITERS) as i:
                def after(u, step):
                    v.wait_ge(g.dve_out[u], upto(g.DVE, i, step))

                if layer == "2b":
                    for u in g.streams:
                        v.wait_ge(dst_ready[u], (i + 1) * 16)
                        v.wait_ge(keep_ready[u], (i + 1) * 16)
                        v.scalar_tensor_tensor(out=t1[u][:, :], in0=keep[u][:, :], scalar=-1.0, in1=h2_before[u][:, ::-1],
                                               op0=ALU.add, op1=ALU.mult).then_inc(g.dve_out[u], 1)
                if layer != "0":
                    for u in g.streams:
                        v.wait_ge(x_carried, chunk(i, u) + 1)
                        if layer == "2b":
                            after(u, "mask")
                            v.tensor_tensor_scan(xd[u][:, :], keep[u][:, :], t1[u][:, :], carry_x[:, 0:1],
                                                 ALU.mult, ALU.subtract).then_inc(g.dve_out[u], 1)
                        else:
                            if layer == "2a":
                                v.wait_ge(stored_T[u], i * 32)
                            v.wait_ge(keep_ready[u], (i + 1) * 16)
                            v.wait_ge(g.pe_out[u], upto(g.PE, i, "dstT"))
                            v.tensor_tensor_scan(xd[u][:, :], keep[u][:, :], bank(1)(u)[:, ::-1], carry_x[:, 0:1],
                                                 ALU.mult, ALU.add).then_inc(g.dve_out[u], 1)
                        after(u, "dst")
                        v.tensor_copy(carry_x[:, :], xd[u][:, CHUNK - 1:CHUNK]).then_inc(x_carried, 1)
                if layer == "0":
                    for u in g.streams:
                        v.wait_ge(g.pe_out[u], upto(g.PE, i, "q"))
                        v.wait_ge(g.act_out[u], upto(g.ACT, i, "k"))
                        v.tensor_tensor(t1[u][:, :], bank(3)(u), t1[u][:, :], ALU.mult).then_inc(g.dve_out[u], 1)
                    for u in g.streams:
                        after(u, "qk")
                        v.wait_ge(g.act_out[u], upto(g.ACT, i, "e0"))
                        v.tensor_tensor(t1[u][:, :], t1[u][:, :], t2[u][:, :], ALU.mult).then_inc(g.dve_out[u], 1)
                    for u in g.streams:
                        v.wait_ge(g.pe_out[u], upto(g.PE, i, "v"))
                        v.wait_ge(g.act_out[u], upto(g.ACT, i, "e1"))
                        v.tensor_tensor(val[u][:, :], bank(1)(u), val_own[u][:, :], ALU.mult).then_inc(g.dve_out[u], 1)
                if layer == "1":
                    for u in g.streams:
                        v.wait_ge(g.act_out[u], upto(g.ACT, i, "l"))
                        v.tensor_tensor(logit[u][:, :], bank(0)(u)[0:H, :], t1[u][0:H, :], ALU.max).then_inc(g.dve_out[u], 1)
                    for u in g.streams:
                        v.wait_ge(g.act_out[u], upto(g.ACT, i, "ls"))
                        v.tensor_tensor(logit_own[u][:, :], bank(1)(u)[0:H, :], t2[u][0:H, :], ALU.max).then_inc(g.dve_out[u], 1)
                if layer in ("2a", "2b"):
                    br = c.br1 if layer == "2a" else c.br2
                    xr = bank(0 if layer == "2a" else 1)
                    for u in g.streams:
                        v.wait_ge(g.pe_out[u], upto(g.PE, i, "xr"))
                        v.wait_ge(g.act_out[u], upto(g.ACT, i, "srcT" if layer == "2b" else "xs"))
                        v.scalar_tensor_tensor(out=t1[u][0:M, :], in0=xr(u)[0:M, :], scalar=br[:, 0:1], in1=val[u][0:M, :],
                                               op0=ALU.add, op1=ALU.add).then_inc(g.dve_out[u], 1)
                    for u in g.streams:
                        v.wait_ge(g.act_out[u], upto(g.ACT, i, "xd"))
                        v.scalar_tensor_tensor(out=t2[u][0:M, :], in0=xr(u)[0:M, :], scalar=br[:, 0:1],
                                               in1=val_own[u][0:M, :], op0=ALU.add, op1=ALU.add).then_inc(g.dve_out[u], 1)
                    for z, step in ((t1, "zs"), (t2, "zd")):
                        for u in g.streams:
                            after(u, step)
                            v.scalar_tensor_tensor(out=z[u][0:M, :], in0=z[u][0:M, :], scalar=SLOPE, in1=z[u][0:M, :],
                                                   op0=ALU.mult, op1=ALU.max).then_inc(g.dve_out[u], 1)
                if layer == "3":
                    for u in g.streams:
                        v.wait_ge(g.act_out[u], upto(g.ACT, i, "l"))
                        v.tensor_tensor(logit[u][:, :], bank(3)(u)[0:H, :], t1[u][0:H, :], ALU.max).then_inc(g.dve_out[u], 1)
                    for u in g.streams:
                        v.wait_ge(deg_carried, chunk(i, u) + 1)
                        v.tensor_tensor_scan(deg[u][:, :], keep[u][0:H, :], c.minus_one[:, :], carry_deg[:, 0:1],
                                             ALU.mult, ALU.add).then_inc(g.dve_out[u], 1)
                        after(u, "deg")
                        v.tensor_copy(carry_deg[:, :], deg[u][:, CHUNK - 1:CHUNK]).then_inc(deg_carried, 1)
                for u in g.streams:
                    if own:
                        v.wait_ge(g.act_out[u], upto(g.ACT, i, "ls"))
                        if layer == "1":
                            after(u, "ls")
                        v.tensor_tensor(logit_max[u][:, :], logit[u][:, :], logit_own[u][:, :], ALU.max)\
                         .then_inc(g.dve_out[u], 1)
                    elif layer == "3":
                        after(u, "l")
                        v.tensor_scalar(logit_max[u][:, :], logit[u][:, :], 0.0, None, ALU.max).then_inc(g.dve_out[u], 1)
                highest = logit if layer == "0" else logit_max
                for u in g.streams:
                    v.wait_ge(max_carried, chunk(i, u) + 1)
                    v.tensor_copy(fmax[u][:, 0:1], carry_max[:, :]).then_inc(g.dve_out[u], 1)
                    after(u, "fc")
                    v.wait_ge(neg_ready[u], (i + 1) * 16)
                    if layer == "0":
                        v.wait_ge(g.act_out[u], upto(g.ACT, i, "l"))
                    v.tensor_tensor_scan(fmax[u][:, 1:CHUNK + 1], neg[u][:, :], highest[u][:, :], fmax[u][:, 0:1],
                                         ALU.add, ALU.max).then_inc(g.dve_out[u], 1)
                    after(u, "f")
                    v.tensor_copy(carry_max[:, :], fmax[u][:, CHUNK:CHUNK + 1]).then_inc(max_carried, 1)
                for u in g.streams:
                    v.tensor_tensor(expo[u][:, 1, :], fmax[u][:, 0:CHUNK], neg[u][:, :], ALU.add).then_inc(g.dve_out[u], 1)
                for u in g.streams:
                    v.tensor_tensor(expo[u][:, 0, :], logit[u][:, :], fmax[u][:, 1:CHUNK + 1], ALU.subtract)\
                     .then_inc(g.dve_out[u], 1)
                for u in g.streams:
                    after(u, "shift")
                    v.tensor_tensor(expo[u][:, 1, :], expo[u][:, 1, :], fmax[u][:, 1:CHUNK + 1], ALU.subtract)\
                     .then_inc(g.dve_out[u], 1)
                if layer != "0":
                    for u in g.streams:
                        if own:
                            v.tensor_tensor(expo[u][:, 2, :], logit_own[u][:, :], fmax[u][:, 1:CHUNK + 1], ALU.subtract)\
                             .then_inc(g.dve_out[u], 1)
                        else:
                            v.tensor_scalar(expo[u][:, 2, :], fmax[u][:, 1:CHUNK + 1], -1.0, None, ALU.mult)\
                             .then_inc(g.dve_out[u], 1)
                for u in g.streams:
                    v.wait_ge(g.act_out[u], upto(g.ACT, i, "exp"))
                    v.wait_ge(den_carried, chunk(i, u) + 1)
                    v.tensor_tensor_scan(den[u][:, :], expo[u][:, 1, :], expo[u][:, 0, :], carry_den[:, 0:1],
                                         ALU.mult, ALU.add).then_inc(g.dve_out[u], 1)
                    after(u, "den")
                    v.tensor_copy(carry_den[:, :], den[u][:, CHUNK - 1:CHUNK]).then_inc(den_carried, 1)
                if layer == "3":
                    for u in g.streams:
                        v.scalar_tensor_tensor(out=rest[u][:, :], in0=deg[u][:, :], scalar=float(E), in1=expo[u][:, 2, :],
                                               op0=ALU.add, op1=ALU.mult).then_inc(g.dve_out[u], 1)
                for u in g.streams:
                    if layer == "0":
                        v.tensor_scalar(total[u][:, :], den[u][:, :], SOFTMAX_EPS, None, ALU.add).then_inc(g.dve_out[u], 1)
                    elif layer == "1":
                        v.scalar_tensor_tensor(out=total[u][:, :], in0=den[u][:, :], scalar=SOFTMAX_EPS,
                                               in1=expo[u][:, 2, :], op0=ALU.add, op1=ALU.add).then_inc(g.dve_out[u], 1)
                    elif own:
                        v.tensor_tensor(total[u][:, :], den[u][:, :], expo[u][:, 2, :], ALU.add).then_inc(g.dve_out[u], 1)
                    else:
                        after(u, "zt")
                        v.tensor_tensor(total[u][:, :], den[u][:, :], rest[u][:, :], ALU.add).then_inc(g.dve_out[u], 1)
                for u in g.streams:
                    v.wait_ge(g.pe_out[u], upto(g.PE, i, "pB"))
                    if layer == "0":
                        after(u, "v")
                    v.tensor_tensor(t1[u][0:M, :], bank(0)(u)[0:M, :], val[u][0:M, :], ALU.mult).then_inc(g.dve_out[u], 1)
                for u in g.streams:
                    v.wait_ge(g.pe_out[u], upto(g.PE, i, "dqT"))
                    v.reciprocal(recip[u][:, :, :], bank(3)(u)[:, 0:TILES * H].rearrange("p (t h) -> p t h", t=TILES))\
                     .then_inc(g.dve_out[u], 1)
                for u in g.streams:
                    v.wait_ge(g.pe_out[u], upto(g.PE, i, "cB"))
                    v.wait_ge(num_carried, chunk(i, u) + 1)
                    after(u, "pv")
                    v.tensor_tensor_scan(num[u][0:M, :], bank(1)(u)[0:M, :], t1[u][0:M, :], carry_num[0:M, 0:1],
                                         ALU.mult, ALU.add).then_inc(g.dve_out[u], 1)
                    after(u, "num")
                    v.tensor_copy(carry_num[0:M, :], num[u][0:M, CHUNK - 1:CHUNK]).then_inc(num_carried, 1)
                if own:
                    for u in g.streams:
                        v.wait_ge(g.pe_out[u], upto(g.PE, i, "sB"))
                        v.tensor_tensor(t2[u][0:M, :], bank(2)(u)[0:M, :], val_own[u][0:M, :], ALU.mult)\
                         .then_inc(g.dve_out[u], 1)
                    for u in g.streams:
                        after(u, "sv")
                        v.tensor_tensor(t2[u][0:M, :], t2[u][0:M, :], num[u][0:M, :], ALU.add).then_inc(g.dve_out[u], 1)
                weighted = t2 if own else num
                for u in g.streams:
                    v.wait_ge(g.pe_out[u], upto(g.PE, i, "rB"))
                    if own:
                        after(u, "ns")
                    v.tensor_tensor(g.agg[u][0:M, :], weighted[u][0:M, :], bank(3)(u)[0:M, :], ALU.mult)\
                     .then_inc(g.dve_out[u], 1)
                if layer == "0":
                    dve_update0(v, g, i)
                if layer == "1":
                    dve_update1(v, g, i)
                if layer == "2a":
                    dve_update2a(v, g, i)
                if layer == "2b":
                    dve_update2b(v, g, i)
                if layer == "3":
                    for u in g.streams:
                        after(u, "agg")
                        v.tensor_tensor(g.yT[u][:, :], g.agg[u][:, :], xd[u][:, :], ALU.add).then_inc(g.dve_out[u], 1)
                    dve_norm(v, g, i, "n5", lambda u: tiles_of(g.bank(u)), lambda u: (g.pe_out[u], upto(g.PE, i, "y3r")),
                             lambda u: new[u], lambda u: (stored[u], i * per_chunk))


def source_columns(nc, c):
    with ExitStack() as own:
        as_float = own.enter_context(nc.sbuf_tensor("map_as_float", [P, SLOT_TILES], F32))
        sem = lambda name: own.enter_context(nc.semaphore(name))
        copied, flipped = sem("map_copied"), sem("map_flipped")
        block = own.enter_context(nc.Block())

        @block.vector
        def _(v):
            v.tensor_copy(as_float[:, :], c.map_cols[:, :, 0]).then_inc(copied, 1)
            v.tensor_copy(c.src_table_cols[0][:, :], c.map_cols[:, :, 1]).then_inc(copied, 1)
            v.wait_ge(flipped, 1)
            v.tensor_copy(c.src_table_cols[1][:, :], c.psum[:, 0, SLOT_TILES - 1::-1]).then_inc(copied, 1)
            v.wait_ge(copied, 3)

        @block.tensor
        def _(pe):
            pe.wait_ge(copied, 1)
            pe.matmul(c.psum[:, 0, 0:SLOT_TILES], c.anti[:, :], as_float[:, :], start=True, stop=True).then_inc(flipped, 1)


def build(nc, a):
    c, dram = Named(), Named()

    def scratch(name, shape, dt=F32):
        return nc.dram_tensor(name, shape, dt, kind="Internal").ap()

    dram.x1, dram.x2, dram.x3 = (scratch(n, [ROWS, D]) for n in ("x1", "x2", "x3"))
    dram.xl2 = scratch("xl2", [ROWS, C2])
    dram.x2_T, dram.h2_T = scratch("x2_T", [D, E_PAD]), scratch("h2_T", [D, E_PAD])
    dram.staged = [scratch(f"staged{k}", [E_PAD, D]) for k in range(2)]
    dram.slot_map = scratch("slot_map", [N, 2], I32)
    dram.slot_map_flat = dram.slot_map.rearrange("n (o k) -> (n o) k", k=1)
    dram.keep = [scratch(f"keep{o}", [SLOT_CHUNKS, CHUNK]) for o in range(2)]
    dram.neg = [scratch(f"neg{o}", [SLOT_CHUNKS, CHUNK]) for o in range(2)]
    dram.keep_flat = [t.rearrange("a b -> (a b)") for t in dram.keep]
    dram.neg_flat = [t.rearrange("a b -> (a b)") for t in dram.neg]

    with ExitStack() as ctx:
        c.psum = ctx.enter_context(nc.psum_tensor("psum", [P, 8, CHUNK], F32))
        c.map_cols = ctx.enter_context(nc.sbuf_tensor("map_cols", [P, SLOT_TILES, 2], I32))
        c.src_table_cols = [ctx.enter_context(nc.sbuf_tensor(f"src_table_cols{o}", [P, SLOT_TILES], I32)) for o in range(2)]
        prepare(nc, a, c, dram, ctx)
        node_pass(nc, a, c, dram)
        slot_pass(nc, a, c, dram, "0")
        source_columns(nc, c)
        for layer in ("1", "2a", "2b", "3"):
            slot_pass(nc, a, c, dram, layer)



def lay_out(inputs):
    out = {k: np.ascontiguousarray(v) for k, v in inputs.items() if k not in ("src", "dst", "edge_attr_64", "L3_gnn_W_node")}
    out["L3_gnn_W_node"] = np.ascontiguousarray(inputs["L3_gnn_W_node"])
    out["W_node_T"] = np.ascontiguousarray(np.asarray(inputs["L3_gnn_W_node"]).T)
    x_T = np.zeros((D, N_PAD), np.float32)
    x_T[:, :N] = np.asarray(inputs["x"]).T
    out["x_T"] = x_T
    edge_T = np.zeros((EF, E_PAD), np.float32)
    edge_T[:, :E] = np.asarray(inputs["edge_attr_64"]).T
    out["edge_T"] = edge_T
    src, dst = np.asarray(inputs["src"]), np.asarray(inputs["dst"])
    more = E_PAD - E

    def columns(t):
        return np.ascontiguousarray(t.reshape(SLOT_TILES, P).T)

    def chunks(t):
        return np.ascontiguousarray(t.reshape(SLOT_CHUNKS, CHUNK))

    out["src_cols"] = columns(np.concatenate([src, np.zeros(more, src.dtype)]))
    out["dst_gather_cols"] = columns(np.concatenate([dst, np.zeros(more, dst.dtype)]))
    ended = np.concatenate([np.full(1, -1, dst.dtype), dst, np.full(more, N, dst.dtype), np.full(1, -1, dst.dtype)])
    both = [ended, ended[::-1]]
    out["dst_cols"] = np.stack([columns(t[1:-1]) for t in both])
    out["dst_next_cols"] = np.stack([columns(t[2:]) for t in both])
    out["dst_prev_cols"] = columns(ended[:-2])
    out["dst_rows"] = np.stack([chunks(t[1:-1]) for t in both])
    out["dst_prev_rows"] = np.stack([chunks(t[:-2]) for t in both])
    return out


def kernel(**inputs):
    import concourse.bacc as bacc
    from concourse.bass_utils import run_bass_kernel_spmd

    nc = bacc.Bacc("TRN2", target_bir_lowering=False, num_devices=1)
    a = {}
    arrays = {}
    for name, array in lay_out(inputs).items():
        arrays[f"in_{name}"] = array
        a[name] = nc.dram_tensor(f"in_{name}", array.shape, mybir.dt.from_np(array.dtype),
                                          kind="ExternalInput").ap()
    a["out"] = nc.dram_tensor("out_nodes", [N_PAD, D], F32, kind="ExternalOutput").ap()
    build(nc, a)
    r = run_bass_kernel_spmd(nc, [arrays], core_ids=[0])
    return r.results[0]["out_nodes"][:N]
```

```python
from contextlib import ExitStack

import numpy as np

import concourse.bass as bass
from concourse import mybir


class Named:

    def __init__(self, c=None, slots=False, last_flags=None):
        self.c, self.slots, self.last_flags = c, slots, last_flags


P = 128
CHUNK = 512
TILES = CHUNK // P
D = 128
EF = 64
N = 50000
E = 25000
BIG = 1.0e30
OUT_OF_RANGE = 1 << 22
LN_EPS = 1e-5
SOFTMAX_EPS = 1e-16
SLOPE = 0.2

NODE_STREAMS = 7
STREAMS = 4
NODE_ITERS = -(-N // (NODE_STREAMS * CHUNK))
SLOT_ITERS = -(-E // (STREAMS * CHUNK))
PER_ITER = STREAMS * CHUNK
NODES_PER_ITER = NODE_STREAMS * CHUNK
N_PAD = NODE_ITERS * NODES_PER_ITER
E_PAD = SLOT_ITERS * PER_ITER
SIDE_TILES = -(-E // (P * NODE_ITERS))
E_STAGED = NODE_ITERS * SIDE_TILES * P
SLOT_CHUNKS = E_PAD // CHUNK
SLOT_TILES = E_PAD // P
ROWS = N_PAD + E_PAD
C2 = 64

F32 = mybir.dt.float32
BF16 = mybir.dt.bfloat16
I32 = mybir.dt.int32
ALU = mybir.AluOpType
ACT = mybir.ActivationFunctionType
at_index = bass.IndirectOffsetOnAxis
ds = bass.ds


class Steps:

    def __init__(self, sems, primed=0):
        self.sems, self.primed, self.names = sems, primed, []

    def done(self, u, i, name):
        return self.sems[u], i * len(self.names) + self.names.index(name) + 1 + self.primed

    def before(self, u, i):
        return self.sems[u], i * len(self.names) + self.primed


def order_of_work(chain, streams, others=()):
    total = sum(time for _, _, time in chain)
    placed = []
    for u in range(streams):
        now = u * total / streams
        for n, (engine, step, time) in enumerate(chain):
            placed.append((now % total, u, int(now // total), engine, step))
            now += time
    for n, (engine, step) in enumerate(others):
        placed.append(((n + 0.5) * total / len(others), -1, 0, engine, step))
    placed.sort(key=lambda item: item[0])
    return [item[1:] for item in placed]


def turns(g, engine, i, part):
    for u, late, of, step in g.order:
        if of == engine and (part == "all" or late == (part == "out")):
            yield u, (i - 1 if late else i), step


def plan(g, chain, others=()):
    g.order = order_of_work(chain, len(g.streams), others)
    for steps, engine in ((g.PE, "PE"), (g.ACT, "ACT"), (g.DVE, "DVE"), (g.POOL, "POOL")):
        steps.names = [step for of, step, _ in chain if of == engine and not step.startswith(UNCOUNTED)]


UNCOUNTED = ("store", "index", "gather", "keep_map", "scatter")


def tiles_of(t):
    return t.rearrange("p (t n) -> p t n", t=TILES)


def tile_cols(t, width=P):
    return slice(t * width, (t + 1) * width)



def pe_rows(pe, g, u, bank, parts, bias=None, width=P):
    if bias is not None:
        pe.matmul(bank(u)[:, 0:TILES * width], g.c.ones[:, :], bias[:, 0:TILES * width], start=True, stop=False)
    for t in range(TILES):
        for k, (tile, weights) in enumerate(parts):
            ins = pe.matmul(bank(u)[:, tile_cols(t, width)], tile[:, tile_cols(t)], weights,
                            start=bias is None and k == 0,
                            stop=k == len(parts) - 1 and (bias is None or t == TILES - 1))
    ins.then_inc(g.pe_out[u], 1)


def pe_transposes(pe, g, u, bank, rows):
    for t in range(TILES):
        ins = pe.transpose(bank(u)[:, tile_cols(t)], rows[:, t, :], g.c.ident[:, :])
    ins.then_inc(g.pe_out[u], 1)


def act_copy(act, g, u, out, source, func=ACT.Copy, bias=0.0, scale=1.0):
    act.activation(out, source, func, bias=bias, scale=scale).then_inc(g.act_out[u], 1)


def act_squares(act, g, u, rows):
    for t in range(TILES):
        ins = act.activation(g.z[u][:, t, :], rows[:, t, :], ACT.Square, scale=float(D ** -0.5),
                             accum_out=g.mean_square[u][:, t:t + 1])
    ins.then_inc(g.act_out[u], 1)


def dve_scale_rows(v, g, u, source, out):
    v.tensor_tensor(out[:, :, :], source, g.rstd[u][:, :].unsqueeze(2).broadcast_to([P, TILES, D]), ALU.mult)\
     .then_inc(g.dve_out[u], 1)


def norm_chain(tag, out, last=False):
    return [("ACT", tag, 1.2), ("POOL", tag + "_eps", 0.3), ("POOL", tag + ("_pow" if last else "_rstd"), 1.2)] + \
        ([("POOL", tag + "_rstd", 0.3)] if last else []) + [("DVE", out, 0.8)]


def end_phase(nc, sems):
    nc.clear_and_free_semaphores(sems)
    nc.all_engine_barrier()


def phase_tiles(ctx, nc, g, prefix, streams, primed):
    g.streams = range(streams)

    def sb(name, shape, dt=F32):
        return ctx.enter_context(nc.sbuf_tensor(f"{prefix}_{name}", shape, dt))

    g.sb = sb
    g.many = lambda name, shape, dt=F32: [sb(f"{name}{u}", shape, dt) for u in g.streams]
    g.mean_square = g.many("mean_square", [P, TILES])
    g.variance = g.many("variance", [P, TILES])
    g.raw = g.many("raw", [P, TILES])
    g.rstd = g.many("rstd", [P, TILES])
    g.all_sems = []

    def sem(name):
        g.all_sems.append(nc.alloc_semaphore(f"{prefix}_{name}"))
        return g.all_sems[-1]

    g.sem = sem
    g.sems = lambda name: [sem(f"{name}{u}") for u in g.streams]
    g.pe_out, g.act_out, g.dve_out, g.pool_out = (g.sems(n) for n in ("pe_out", "act_out", "dve_out", "pool_out"))
    g.PE, g.ACT, g.POOL = Steps(g.pe_out), Steps(g.act_out), Steps(g.pool_out)
    g.DVE = Steps(g.dve_out, primed)
    g.A = lambda u: g.c.psum[:, 2 * u, :]
    g.B = lambda u: g.c.psum[:, 2 * u + 1, :]



def prepare(nc, a, c, dram, ctx):
    def sb(name, shape, dt=F32):
        return ctx.enter_context(nc.sbuf_tensor(name, shape, dt))

    loads = []

    def load(name, shape, src, dt=F32, room=None):
        t = (room or sb)(name, shape, dt)
        loads.append((t[:], src))
        return t

    def column(name, src, m=P):
        return load(name, [m, 1], src.rearrange("(p o) -> p o", o=1))

    def row(name, src, m=P):
        return load(name, [P, m], src.partition_broadcast(P))

    own = ExitStack()

    def temp(name, shape, dt=F32):
        return own.enter_context(nc.sbuf_tensor(name, shape, dt))

    c.Wq = load("Wq", [P, D], a["L0_gnn_Wq"])
    c.Wk = load("Wk", [P, D], a["L0_gnn_Wk"])
    c.Wv = load("Wv", [P, D], a["L0_gnn_Wv"])
    c.We0 = load("We0", [EF, D], a["L0_gnn_We0"])
    c.We1 = load("We1", [EF, D], a["L0_gnn_We1"])
    c.W = load("W", [P, D], a["L1_gnn_W"])
    c.Wl1 = load("Wl1", [P, D], a["L2_gnn_Wl1"])
    c.Wr1 = load("Wr1", [P, D], a["L2_gnn_Wr1"])
    c.Wl2 = load("Wl2", [P, C2], a["L2_gnn_Wl2"])
    c.Wr2 = load("Wr2", [P, C2], a["L2_gnn_Wr2"])
    c.Wlin = load("Wlin", [C2, D], a["L2_gnn_Wlin"])
    c.WnT = load("WnT", [P, D], a["W_node_T"])
    c.ln_g = column("ln_g", a["L0_gnn_ln_g"])
    c.ln_b = column("ln_b", a["L0_gnn_ln_b"])
    c.gamma = column("gamma", a["L1_gnn_gamma"])
    c.beta = column("beta", a["L1_gnn_beta"])
    c.bl1 = column("bl1", a["L2_gnn_bl1"])
    br1 = column("br1", a["L2_gnn_br1"])
    c.bias1 = column("bias1", a["L2_gnn_bias1"])
    c.bl2 = column("bl2", a["L2_gnn_bl2"], C2)
    c.br2 = column("br2", a["L2_gnn_br2"], C2)
    c.bias2 = column("bias2", a["L2_gnn_bias2"], C2)
    c.blin = column("blin", a["L2_gnn_blin"])

    c.ident = sb("ident", [P, P])
    c.anti = sb("anti", [P, P])
    c.center = sb("center", [P, P])
    c.ones = sb("ones", [P, P], BF16)
    c.minus_half = sb("minus_half", [P, TILES])
    c.eps = sb("eps", [P, TILES])
    c.minus_one = sb("minus_one", [P, CHUNK])
    c.W1a, c.W1b, c.W2, c.Wc = (sb(n, [P, D]) for n in ("W1a", "W1b", "W2", "Wc"))
    c.Wsa, c.Wda, c.Wsd = (sb(n, [P, D]) for n in ("Wsa", "Wda", "Wsd"))
    c.Wlr1, c.Wlr2 = sb("Wlr1", [P, D]), sb("Wlr2", [P, C2])
    c.Wsrc, c.Wtgt, c.Wedge = sb("Wsrc", [P, D]), sb("Wtgt", [P, D]), sb("Wedge", [EF, D])
    c.S16, c.S1, c.S2 = sb("S16", [P, D]), sb("S1", [P, D]), sb("S2", [C2, D])
    c.blr1, c.blr2, c.node_bias2 = sb("blr1", [P, 1]), sb("blr2", [C2, 1]), sb("node_bias2", [C2, 1])
    c.node_bias1 = sb("node_bias1", [P, 1])
    c.b1_rows, c.b2_rows, c.bias_rows = (sb(n, [P, CHUNK], BF16) for n in ("b1_rows", "b2_rows", "bias_rows"))
    c.bl2_rows = sb("bl2_rows", [P, TILES * C2], BF16)
    c.src_cols = load("src_cols", [P, SLOT_TILES], a["src_cols"], I32)
    c.dst_gather_cols = load("dst_gather_cols", [P, SLOT_TILES], a["dst_gather_cols"], I32)
    c.last = [sb(f"last{o}", [P, SLOT_TILES]) for o in range(2)]
    c.map_index = [sb(f"map_index{o}", [P, SLOT_TILES], I32) for o in range(2)]
    c.out_index = sb("out_index", [P, SLOT_TILES], I32)
    c.payload = [sb(f"payload{o}", [P, SLOT_TILES], I32) for o in range(2)]

    raw = {n: load("raw_" + n, [P, D], src, room=temp) for n, src in (
        ("W1a", a["L0_gnn_W1"][0:D, :]), ("W1b", a["L0_gnn_W1"][D:2 * D, :]), ("W2", a["L0_gnn_W2"]), ("Wn", a["L3_gnn_W_node"]))}
    raw_edge = load("raw_edge", [P, EF], a["L3_gnn_W_edge"], room=temp)
    raw_b1 = load("raw_b1", [P, D], a["L0_gnn_b1"].partition_broadcast(P), room=temp)
    raw_b2 = load("raw_b2", [P, D], a["L0_gnn_b2"].partition_broadcast(P), room=temp)
    raw_bias = load("raw_bias", [P, D], a["L1_gnn_bias"].partition_broadcast(P), room=temp)
    raw_bl2 = load("raw_bl2", [P, C2], a["L2_gnn_bl2"].partition_broadcast(P), room=temp)
    vectors = {}
    for n, src, m in (("att_src", a["L1_gnn_att_src"], P), ("att_dst", a["L1_gnn_att_dst"], P),
                      ("att1", a["L2_gnn_att1"], P), ("att2", a["L2_gnn_att2"], C2)):
        vectors[n] = load("col_" + n, [m, 1], src.rearrange("h (c o) -> (h c) o", o=1), room=temp)
    for k, n in enumerate(("a_src", "a_tgt", "a_edge")):
        vectors[n] = temp("col_" + n, [P, 1])
        for h in range(4):
            loads.append((vectors[n][32 * h:32 * h + 32, :],
                          a["L3_gnn_a"][h:h + 1, 32 * k:32 * k + 32].rearrange("o c -> c o")))
    here = [load(f"here{o}", [P, SLOT_TILES], a["dst_cols"][o], I32, temp) for o in range(2)]
    after = [load(f"after{o}", [P, SLOT_TILES], a["dst_next_cols"][o], I32, temp) for o in range(2)]
    before = load("before", [P, SLOT_TILES], a["dst_prev_cols"], I32, temp)
    row_here = [load(f"row_here{o}", [SLOT_CHUNKS, CHUNK], a["dst_rows"][o], I32, temp) for o in range(2)]
    row_prev = [load(f"row_prev{o}", [SLOT_CHUNKS, CHUNK], a["dst_prev_rows"][o], I32, temp) for o in range(2)]
    first = temp("first", [P, SLOT_TILES])
    skip = [temp(f"skip{o}", [P, SLOT_TILES]) for o in range(2)]
    keep = [temp(f"keep_r{o}", [SLOT_CHUNKS, CHUNK]) for o in range(2)]
    S = {n: temp("S_" + n, [P, D]) for n in ("att_src", "att_dst", "a_src", "a_tgt", "a_edge")}
    same_head = {4: temp("same_head4", [P, D]), 8: temp("same_head8", [P, D]), 16: c.S16}
    stats, mean = temp("stats", [P, 7, 6]), temp("mean", [P, 7, 2])
    row_f = [temp(f"row_f{k}", [P, D]) for k in range(4)]
    row_rest = [temp(f"row_rest{k}", [P, D]) for k in range(4)]
    part = [temp(f"part{k}", [P, D], BF16) for k in range(4)]
    WT = temp("W_transposed", [P, D])
    map_rows = 125
    own_row = temp("own_row", [map_rows, N // map_rows, 2], I32)
    psum = c.psum

    with own:
        sem = lambda name: own.enter_context(nc.semaphore(name))
        loaded, made, masks, stored = sem("loaded"), sem("made"), sem("masks"), sem("prep_stored")
        worked, products, map_started = sem("worked"), sem("products"), sem("map_started")
        block = own.enter_context(nc.Block())

        @block.sync
        def _(sp):
            with nc.allow_non_contiguous_dma("a few vectors"):
                for dst, src in loads:
                    sp.dma_start(dst, src).then_inc(loaded, 16)
            for k in range(2):
                sp.dma_start(dram.staged[k][E_STAGED:E_PAD, :], a["x"][0:E_PAD - E_STAGED, :]).then_inc(stored, 16)
            sp.wait_ge(masks, 2)
            for o in range(2):
                sp.dma_start(dram.keep[o], keep[o][:, :]).then_inc(stored, 16)
            sp.wait_ge(stored, 64)

        @block.gpsimd
        def _(pool):
            pool.iota(own_row[:, :, :], pattern=[[1, N // map_rows], [0, 2]], base=0,
                      channel_multiplier=N // map_rows).then_inc(made, 1)
            pool.iota(c.payload[0][:, :], pattern=[[P, SLOT_TILES]], base=N_PAD, channel_multiplier=1).then_inc(made, 1)
            pool.iota(c.payload[1][:, :], pattern=[[-P, SLOT_TILES]], base=N_PAD + E_PAD - 1,
                      channel_multiplier=-1).then_inc(made, 1)
            pool.wait_ge(made, 1)
            pool.dma_start(dram.slot_map.rearrange("(p n) o -> p (n o)", p=map_rows),
                           own_row[:, :, :].rearrange("p n o -> p (n o)")).then_inc(map_started, 16)
            for t, value in ((c.ident, 0.0), (c.anti, 0.0), (same_head[4], 1.0), (same_head[8], 1.0),
                             (same_head[16], 1.0), (c.minus_half, -0.5), (c.eps, LN_EPS), (c.minus_one, -1.0), (c.ones, 1.0),
                             (c.b1_rows, 0.0), (c.b2_rows, 0.0), (c.bias_rows, 0.0), (c.bl2_rows, 0.0)):
                pool.memset(t[:, :], value).then_inc(made, 1)
            pool.wait_ge(made, 16)
            pool.affine_select(out=c.ident[:, :], in_=c.ident[:, :], compare_op=ALU.not_equal, fill=1.0, base=0,
                               pattern=[[-1, P]], channel_multiplier=1).then_inc(made, 1)
            pool.affine_select(out=c.anti[:, :], in_=c.anti[:, :], compare_op=ALU.not_equal, fill=1.0, base=-(P - 1),
                               pattern=[[1, P]], channel_multiplier=1).then_inc(made, 1)
            for h, t in same_head.items():
                pool.affine_select(out=t[:, :], in_=t[:, :], compare_op=ALU.is_ge, fill=0.0, base=0,
                                   pattern=[[-(D // h), h], [0, D // h]], channel_multiplier=1).then_inc(made, 1)
            pool.wait_ge(made, 21)
            for h, t in same_head.items():
                pool.affine_select(out=t[:, :], in_=t[:, :], compare_op=ALU.is_ge, fill=0.0, base=D // h - 1,
                                   pattern=[[D // h, h], [0, D // h]], channel_multiplier=-1).then_inc(made, 1)
            pool.wait_ge(made, 24)
            pool.wait_ge(map_started, 16)

        @block.vector
        def _(v):
            v.wait_ge(loaded, 16 * len(loads))
            for o in range(2):
                v.tensor_tensor(keep[o][:, :], row_here[o][:, :], row_prev[o][:, :], ALU.is_equal).then_inc(masks, 1)
            v.wait_ge(made, 24)
            v.tensor_scalar(c.center[:, :], c.ident[:, :], -1.0 / D, None, ALU.add).then_inc(worked, 1)
            for n in S:
                v.tensor_scalar(S[n][:, :], same_head[4][:, :], vectors[n][:, 0:1], None, ALU.mult).then_inc(worked, 1)
            v.tensor_scalar(c.S1[:, :], same_head[8][:, :], vectors["att1"][:, 0:1], None, ALU.mult).then_inc(worked, 1)
            v.tensor_copy(c.S2[:, :], vectors["att2"][:, 0:1].broadcast_to([C2, D])).then_inc(worked, 1)
            v.tensor_tensor(c.Wlr1[:, :], c.Wl1[:, :], c.Wr1[:, :], ALU.add).then_inc(worked, 1)
            v.tensor_tensor(c.Wlr2[:, :], c.Wl2[:, :], c.Wr2[:, :], ALU.add).then_inc(worked, 1)
            v.tensor_tensor(c.blr1[:, :], c.bl1[:, :], br1[:, :], ALU.add).then_inc(worked, 1)
            v.tensor_tensor(c.blr2[:, :], c.bl2[:, :], c.br2[:, :], ALU.add).then_inc(worked, 1)
            v.tensor_tensor(c.node_bias1[:, :], c.bl1[:, :], c.bias1[:, :], ALU.add).then_inc(worked, 1)
            v.tensor_tensor(c.node_bias2[:, :], c.bl2[:, :], c.bias2[:, :], ALU.add).then_inc(worked, 1)
            for o in range(2):
                v.tensor_tensor(c.last[o][:, :], here[o][:, :], after[o][:, :], ALU.not_equal).then_inc(worked, 1)
            v.tensor_tensor(first[:, :], here[0][:, :], before[:, :], ALU.not_equal).then_inc(worked, 1)
            v.tensor_copy(row_f[3][:, 0:C2], raw_bl2[:, :]).then_inc(worked, 1)
            to_center = ((raw["W1a"], c.W1a), (raw["W1b"], c.W1b), (raw["W2"], c.W2), (c.W, c.Wc),
                         (raw_b1, row_f[0]), (raw_b2, row_f[1]), (raw_bias, row_f[2]))
            for k, (source, _) in enumerate(to_center):
                v.bn_stats(stats[:, k, :], source[:, :]).then_inc(worked, 1)
            n = 18 + len(to_center)
            v.wait_ge(worked, n)
            v.tensor_scalar(skip[0][:, :], c.last[0][:, :], -1.0 * OUT_OF_RANGE, 1.0 * OUT_OF_RANGE, ALU.mult,
                            ALU.add).then_inc(worked, 1)
            v.tensor_scalar(skip[1][:, :], first[:, :], -1.0 * OUT_OF_RANGE, 1.0 * OUT_OF_RANGE + 1.0, ALU.mult,
                            ALU.add).then_inc(worked, 1)
            for k in range(len(to_center)):
                v.bn_aggr(mean[:, k, :], stats[:, k, :]).then_inc(worked, 1)
            n += 9
            v.wait_ge(worked, n)
            for o in range(2):
                v.scalar_tensor_tensor(out=c.map_index[o][:, :], in0=here[0][:, :], scalar=2.0, in1=skip[o][:, :],
                                       op0=ALU.mult, op1=ALU.add).then_inc(worked, 1)
            v.tensor_tensor(c.out_index[:, :], here[0][:, :], skip[0][:, :], ALU.add).then_inc(worked, 1)
            for k, (source, out) in enumerate(to_center):
                v.tensor_scalar(out[:, :], source[:, :], mean[:, k, 0:1], None, ALU.subtract).then_inc(worked, 1)
            n += 10
            targets = ((c.b1_rows, D), (c.b2_rows, D), (c.bias_rows, D), (c.bl2_rows, C2))
            rest = row_f
            for level in range(3):
                v.wait_ge(worked, n)
                for k, (_, m) in enumerate(targets):
                    v.tensor_copy(part[k][:, 0:m], rest[k][:, 0:m]).then_inc(worked, 1)
                n += len(targets)
                v.wait_ge(worked, n)
                p = 32 * level
                for k, (out, m) in enumerate(targets):
                    v.tensor_copy(tiles_of(out[p:p + 1, :]), part[k][p:p + 1, 0:m].unsqueeze(1).broadcast_to([1, TILES, m]))\
                     .then_inc(worked, 1)
                n += len(targets)
                if level < 2:
                    following = row_rest if level == 0 else row_f
                    for k, (_, m) in enumerate(targets):
                        v.tensor_tensor(following[k][:, 0:m], rest[k][:, 0:m], part[k][:, 0:m], ALU.subtract)\
                         .then_inc(worked, 1)
                    n += len(targets)
                    rest = following
            v.wait_ge(products, 1)
            v.tensor_copy(WT[:, :], psum[:, 0, 0:D]).then_inc(worked, 1)
            n += 1
            v.wait_ge(products, 2)
            for b, out in ((1, c.Wsa), (2, c.Wda), (3, c.Wsrc), (4, c.Wtgt)):
                v.tensor_copy(out[:, :], psum[:, b, 0:D]).then_inc(worked, 1)
            v.tensor_copy(c.Wedge[:, :], psum[0:EF, 5, 0:D]).then_inc(worked, 1)
            n += 5
            v.wait_ge(worked, n)
            v.tensor_tensor(c.Wsd[:, :], c.Wsa[:, :], c.Wda[:, :], ALU.add).then_inc(worked, 1)
            v.wait_ge(worked, n + 1)

        @block.tensor
        def _(pe):
            pe.wait_ge(loaded, 16 * len(loads))
            pe.wait_ge(made, 24)
            pe.transpose(psum[:, 0, 0:D], c.W[:, :], c.ident[:, :]).then_inc(products, 1)
            pe.wait_ge(worked, 25 + 9 + 10 + 4 * 8 + 1)
            for b, lhs, rhs, m in ((1, WT, S["att_src"], D), (2, WT, S["att_dst"], D), (3, raw["Wn"], S["a_src"], D),
                                   (4, raw["Wn"], S["a_tgt"], D), (5, raw_edge, S["a_edge"], EF)):
                ins = pe.matmul(psum[0:m, b, 0:D], lhs[:, :], rhs[:, :], start=True, stop=True)
            ins.then_inc(products, 1)



def chain0(slots, tail_T):
    return [("PE", "h0", 2.0 if slots else 1.3)] + norm_chain("sq0", "z0") + \
        [("PE", "z0T", 0.7), ("ACT", "relu0", 0.6), ("PE", "y0", 2.1)] + norm_chain("sq1", "x1", slots) + \
        ([("PE", "x1T", 0.7), ("ACT", "x1T", 0.6)] if tail_T else []) + [("ACT", "store_x1", 0.0)]


def chain1(slots, tail_T):
    return [("PE", "h1", 1.3)] + norm_chain("sq2", "z1") + \
        [("PE", "z1T", 0.7), ("ACT", "gelu1", 1.0)] + ([] if slots else [("DVE", "y1T", 0.7)]) + \
        [("PE", "y1", 2.0 if slots else 1.1)] + norm_chain("sq3", "x2", slots) + \
        ([("PE", "x2T", 0.7), ("ACT", "x2T", 0.6)] if tail_T else []) + [("ACT", "store_x2", 0.0)]


def chain2a(slots):
    return ([] if slots else [("PE", "z2", 1.1)]) + \
        [("ACT", "exp2", 0.7), ("DVE", "h2_em1", 0.5), ("DVE", "h2", 0.7), ("PE", "xl", 0.7), ("ACT", "xl", 0.5),
         ("ACT", "store_xl", 0.0)]


def chain2b(slots):
    return ([] if slots else [("PE", "z3", 1.1)]) + \
        [("ACT", "exp3", 0.7), ("DVE", "h3_em1", 0.5), ("DVE", "h3", 0.7), ("PE", "z4", 1.1), ("ACT", "exp4", 0.7),
         ("DVE", "h4_em1", 0.5), ("DVE", "h4", 0.7), ("DVE", "y2T", 0.7), ("PE", "y2", 1.1)] + \
        norm_chain("sq4", "x3", slots) + [("ACT", "store_x3", 0.0)]


def pe_update(pe, g, u, i, step):
    c = g.c
    if step == "h0":
        if g.slots:
            pe.wait_ge(*g.DVE.done(u, i, "agg"))
            pe_rows(pe, g, u, g.A, [(g.xT[u], c.W1b[:, :]), (g.agg[u], c.W1a[:, :])], c.b1_rows)
        else:
            pe.wait_ge(*g.DVE.before(u, i))
            pe.wait_ge(g.x_loaded[u], i * 16 + 16)
            pe_rows(pe, g, u, g.A, [(g.xT[u], c.W1b[:, :])], c.b1_rows)
    if step == "z0T":
        pe.wait_ge(*g.DVE.done(u, i, "z0"))
        pe_transposes(pe, g, u, g.B, g.z[u])
    if step == "y0":
        pe.wait_ge(*g.ACT.done(u, i, "relu0"))
        pe_rows(pe, g, u, g.A, [(g.act_T[u], c.W2[:, :]), (g.xT[u], c.center[:, :])], c.b2_rows)
    if step == "x1T":
        pe.wait_ge(*g.DVE.done(u, i, "x1"))
        pe_transposes(pe, g, u, g.B, g.x1[u])
    if step == "h1":
        if g.slots:
            pe.wait_ge(*g.DVE.done(u, i, "agg"))
            pe_rows(pe, g, u, g.A, [(g.agg[u], c.center[:, :])], c.bias_rows)
        else:
            pe.wait_ge(*g.DVE.done(u, i, "x1"))
            pe.wait_ge(*g.ACT.done(u, i, "x1T"))
            pe_rows(pe, g, u, g.A, [(g.xT1[u], c.Wc[:, :])], c.bias_rows)
    if step == "z1T":
        pe.wait_ge(*g.DVE.done(u, i, "z1"))
        pe_transposes(pe, g, u, g.B, g.z[u])
    if step == "y1":
        if g.slots:
            pe.wait_ge(*g.ACT.done(u, i, "gelu1"))
            pe_rows(pe, g, u, g.A, [(g.act_T[u], c.center[:, :]), (g.xT1[u], c.center[:, :])])
        else:
            pe.wait_ge(*g.DVE.done(u, i, "y1T"))
            pe_rows(pe, g, u, g.A, [(g.yT[u], c.center[:, :])])
    if step == "x2T":
        pe.wait_ge(*g.DVE.done(u, i, "x2"))
        pe_transposes(pe, g, u, g.B, g.x2[u])
    if step == "z2":
        pe.wait_ge(*g.DVE.done(u, i, "x2"))
        pe.wait_ge(*g.ACT.done(u, i, "x2T"))
        pe.matmul(g.A(u), c.Wl1[:, :], g.xT2[u][:, :], start=True, stop=True).then_inc(g.pe_out[u], 1)
    if step == "xl":
        pe.wait_ge(*g.DVE.done(u, i, "h2"))
        pe_rows(pe, g, u, g.B, [(g.act_T[u], c.Wl2[:, :])], c.bl2_rows, C2)
    if step == "z3":
        pe.wait_ge(*g.ACT.done(u, i, "xl"))
        pe.matmul(g.A(u)[0:C2, :], c.Wl2[:, :], g.act_T[u][:, :], start=True, stop=True).then_inc(g.pe_out[u], 1)
    if step == "z4":
        pe.wait_ge(*(g.DVE.done(u, i, "agg") if g.slots else g.ACT.done(u, i, "xl")))
        pe.wait_ge(*g.DVE.done(u, i, "h3"))
        pe.matmul(g.B(u), c.Wlin[:, :], g.act_T[u][0:C2, :], start=True, stop=True).then_inc(g.pe_out[u], 1)
    if step == "y2":
        pe.wait_ge(*g.DVE.done(u, i, "y2T"))
        pe_rows(pe, g, u, g.A, [(g.yT[u], c.center[:, :])])


def act_update(act, g, u, i, step):
    c = g.c
    rows = {"sq0": "h0", "sq1": "y0", "sq2": "h1", "sq3": "y1", "sq4": "y2"}
    if step in rows:
        act.wait_ge(*g.PE.done(u, i, rows[step]))
        act_squares(act, g, u, tiles_of(g.A(u)))
    if step == "relu0":
        act.wait_ge(*g.PE.done(u, i, "z0T"))
        act_copy(act, g, u, g.act_T[u][:, :], g.B(u), ACT.Relu, c.ln_b[:, 0:1], c.ln_g[:, 0:1])
    if step == "x1T":
        act.wait_ge(*g.PE.done(u, i, "x1T"))
        act_copy(act, g, u, g.xT1[u][:, :], g.B(u))
    if step == "gelu1":
        act.wait_ge(*g.PE.done(u, i, "z1T"))
        act_copy(act, g, u, g.act_T[u][:, :], g.B(u), ACT.Gelu, c.beta[:, 0:1], c.gamma[:, 0:1])
    if step == "x2T":
        act.wait_ge(*g.PE.done(u, i, "x2T"))
        act_copy(act, g, u, g.xT2[u][:, :], g.B(u))
    if step == "exp2":
        if g.slots:
            act.wait_ge(*g.DVE.done(u, i, "agg"))
            act_copy(act, g, u, g.expz[u][:, :], g.agg[u][:, :], ACT.Exp, c.bias1[:, 0:1])
        else:
            act.wait_ge(*g.PE.done(u, i, "z2"))
            act_copy(act, g, u, g.expz[u][:, :], g.A(u), ACT.Exp, c.node_bias1[:, 0:1])
    if step == "xl":
        act.wait_ge(g.xl_stored[u], i * 16 + 16)
        act.wait_ge(*g.PE.done(u, i, "xl"))
        act_copy(act, g, u, g.xl[u][:, :, :], tiles_of(g.B(u)[:, 0:TILES * C2]))
    if step == "exp3":
        if g.slots:
            act.wait_ge(*g.DVE.done(u, i, "agg"))
            act_copy(act, g, u, g.expz[u][0:C2, :], g.agg[u][0:C2, :], ACT.Exp, c.bias2[:, 0:1])
        else:
            act.wait_ge(*g.PE.done(u, i, "z3"))
            act_copy(act, g, u, g.expz[u][0:C2, :], g.A(u)[0:C2, :], ACT.Exp, c.node_bias2[:, 0:1])
    if step == "exp4":
        act.wait_ge(*g.PE.done(u, i, "z4"))
        act_copy(act, g, u, g.expz[u][:, :], g.B(u), ACT.Exp, c.blin[:, 0:1])
    if step == "store_x1":
        act.wait_ge(*g.DVE.done(u, i, "x1"))
        act.dma_start(g.rows_in_table(c.dram.x1, i, u), g.x1[u][:, :, :]).then_inc(g.x1_stored[u], 16)
    if step == "store_x2":
        act.wait_ge(*g.DVE.done(u, i, "x2"))
        act.dma_start(g.rows_in_table(c.dram.x2, i, u), g.x2[u][:, :, :]).then_inc(g.x2_stored[u], 16)
    if step == "store_xl":
        act.wait_ge(*g.ACT.done(u, i, "xl"))
        act.dma_start(g.rows_in_table(c.dram.xl2, i, u), g.xl[u][:, :, :]).then_inc(g.xl_stored[u], 16)
    if step == "store_x3":
        act.wait_ge(*g.DVE.done(u, i, "x3"))
        act.dma_start(g.rows_in_table(c.dram.x3, i, u), g.x3[u][:, :, :]).then_inc(g.x3_stored[u], 16)


def dve_update(v, g, u, i, step):
    c = g.c
    if step == "z0":
        v.wait_ge(*g.POOL.done(u, i, "sq0_rstd"))
        dve_scale_rows(v, g, u, tiles_of(g.A(u)), g.z[u])
    if step == "z1":
        v.wait_ge(*g.POOL.done(u, i, "sq2_rstd"))
        dve_scale_rows(v, g, u, tiles_of(g.A(u)), g.z[u])
    if step == "x1":
        v.wait_ge((g.x1_stored if g.slots else g.x4_stored)[u], i * 16 + 16)
        v.wait_ge(*g.POOL.done(u, i, "sq1_rstd"))
        dve_scale_rows(v, g, u, tiles_of(g.A(u)), g.x1[u])
    if step == "x2":
        v.wait_ge(g.x2_stored[u], i * 16 + 16)
        v.wait_ge(*g.POOL.done(u, i, "sq3_rstd"))
        dve_scale_rows(v, g, u, tiles_of(g.A(u)), g.x2[u])
    if step == "x3":
        v.wait_ge(g.x3_stored[u], i * 16 + 16)
        v.wait_ge(*g.POOL.done(u, i, "sq4_rstd"))
        dve_scale_rows(v, g, u, tiles_of(g.A(u)), g.x3[u])
    if step == "y1T":
        v.wait_ge(*g.ACT.done(u, i, "gelu1"))
        v.tensor_tensor(g.yT[u][:, :], g.act_T[u][:, :], g.xT1[u][:, :], ALU.add).then_inc(g.dve_out[u], 1)
    m = C2 if step.startswith("h3") else P
    exp_step = {"h2_em1": "exp2", "h3_em1": "exp3", "h4_em1": "exp4"}
    if step in exp_step:
        v.wait_ge(*g.ACT.done(u, i, exp_step[step]))
        v.tensor_scalar(g.expz[u][0:m, :], g.expz[u][0:m, :], 1.0, -1.0, ALU.min, ALU.add).then_inc(g.dve_out[u], 1)
    if step in ("h2", "h3", "h4"):
        if step == "h4":
            source, bias = g.B(u), c.blin
        elif g.slots:
            source, bias = g.agg[u][0:m, :], {"h2": c.bias1, "h3": c.bias2}[step]
        else:
            source, bias = g.A(u)[0:m, :], {"h2": c.node_bias1, "h3": c.node_bias2}[step]
        v.wait_ge(*g.DVE.done(u, i, step + "_em1"))
        v.scalar_tensor_tensor(out=g.act_T[u][0:m, :], in0=source, scalar=bias[:, 0:1], in1=g.expz[u][0:m, :],
                               op0=ALU.add, op1=ALU.max).then_inc(g.dve_out[u], 1)
    if step == "y2T":
        if g.slots:
            v.wait_ge(g.res_ready[u], (i + 1) * 16)
        v.wait_ge(*g.DVE.done(u, i, "h4"))
        v.tensor_tensor(g.yT[u][:, :], g.act_T[u][:, :], g.res2(u), ALU.add).then_inc(g.dve_out[u], 1)


def pool_update(pool, g, u, i, step):
    squares, _, what = step.partition("_")
    if what == "eps":
        pool.wait_ge(*g.ACT.done(u, i, squares))
        pool.tensor_tensor(g.variance[u][:, :], g.mean_square[u][:, :], g.c.eps[:, :], ALU.add).then_inc(g.pool_out[u], 1)
    flagged = squares + "_pow" in g.POOL.names
    if what == "pow" or (what == "rstd" and not flagged):
        pool.wait_ge(*g.POOL.done(u, i, squares + "_eps"))
        out = g.raw[u] if flagged else g.rstd[u]
        pool.tensor_tensor(out[:, :], g.variance[u][:, :], g.c.minus_half[:, :], ALU.pow).then_inc(g.pool_out[u], 1)
    if what == "rstd" and flagged:
        pool.wait_ge(*g.POOL.done(u, i, squares + "_pow"))
        flags = g.last_flags[:, ds((i * STREAMS + u) * TILES, TILES)]
        pool.tensor_tensor(g.rstd[u][:, :], g.raw[u][:, :], flags, ALU.mult).then_inc(g.pool_out[u], 1)



def node_pass(nc, a, c, dram):
    with ExitStack() as ctx:
        g = Named(c)
        phase_tiles(ctx, nc, g, "node", NODE_STREAMS, primed=1)
        g.A = g.B = lambda u: c.psum[:, u, :]
        gathers = [("POOL", (k, t)) for t in range(SIDE_TILES) for k in (0, 1)]
        scatters = [("POOL", (k, t)) for t in range(SIDE_TILES) for k in (2, 3)]
        others = [("POOL", "side_index")] + gathers + scatters[:4] + [("ACT", "stage")] + scatters[4:] + [("POOL", "side_end")]
        plan(g, chain0(False, True) + chain1(False, True) + chain2a(False) + chain2b(False) + norm_chain("sq5", "x4") +
             [("ACT", "store_x4", 0.0)], others)
        g.xT = g.many("xT", [P, CHUNK])
        g.z = g.many("z", [P, TILES, D])
        g.act_T = g.many("act_T", [P, CHUNK])
        g.yT = g.act_T
        g.expz = [t[:, :, :].rearrange("p t n -> p (t n)") for t in g.z]
        g.x1 = g.many("x1", [P, TILES, D])
        g.x2 = g.many("x2", [P, TILES, D])
        g.x3 = g.many("x3", [P, TILES, D])
        x4 = g.x1
        g.xl = g.many("xl", [P, TILES, C2])
        g.xT1 = g.many("xT1", [P, CHUNK])
        g.xT2 = g.xT1
        g.res2 = lambda u: g.xT2[u][:, :]
        g.x_loaded = g.sems("x_loaded")
        g.x1_stored, g.x2_stored, g.x3_stored = g.sems("x1_stored"), g.sems("x2_stored"), g.sems("x3_stored")
        g.xl_stored, g.x4_stored = g.sems("xl_stored"), g.sems("x4_stored")
        g.rows_in_table = lambda table, i, u: table[ds(i * NODES_PER_ITER + u * CHUNK, CHUNK), :]\
            .rearrange("(t p) f -> p t f", p=P)

        gathered = [g.sb(f"gathered{k}", [P, SIDE_TILES, D]) for k in range(2)]
        index = [g.sb(f"index{k}", [P, SIDE_TILES], I32) for k in range(4)]
        value = [g.sb(f"value{k}", [P, SIDE_TILES], I32) for k in range(2)]
        gathers_done = [g.sem(f"gathers_done{k}") for k in range(2)]
        staged = [g.sem(f"staged{k}") for k in range(2)]
        scattered = [g.sem(f"scattered{k}") for k in range(2)]
        index_ready = g.sem("index_ready")
        ctx.callback(end_phase, nc, g.all_sems)
        block = ctx.enter_context(nc.Block())

        @block.sync
        def _(sp):
            def load(i):
                for u in g.streams:
                    if not isinstance(i, int):
                        sp.wait_ge(*g.PE.done(u, i - 1, "y0"))
                    sp.dma_start(g.xT[u][:, :], a["x_T"][:, ds(i * NODES_PER_ITER + u * CHUNK, CHUNK)]).then_inc(g.x_loaded[u], 16)

            load(0)
            with sp.Fori(1, NODE_ITERS) as i:
                load(i)

        @block.scalar
        def _(act):
            def stage(i):
                for k in range(2):
                    act.wait_ge(gathers_done[k], (i + 1) * 16 * SIDE_TILES)
                    act.dma_start(dram.staged[k][ds(i * (SIDE_TILES * P), SIDE_TILES * P), :].rearrange("(t p) f -> p t f", p=P),
                                  gathered[k][:, :, :]).then_inc(staged[k], 16)

            def run(i, part):
                for u, i, step in turns(g, "ACT", i, part):
                    if step == "stage":
                        stage(i)
                    else:
                        act_update(act, g, u, i, step)
                    if step == "sq5":
                        act.wait_ge(*g.DVE.done(u, i, "x3"))
                        act_squares(act, g, u, g.x3[u])
                    if step == "store_x4":
                        act.wait_ge(*g.DVE.done(u, i, "x4"))
                        act.dma_start(g.rows_in_table(a["out"], i, u), x4[u][:, :, :]).then_inc(g.x4_stored[u], 16)

            run(0, "in")
            with act.Fori(1, NODE_ITERS) as i:
                run(i, "all")
            run(NODE_ITERS, "out")
            for stored in (g.x1_stored, g.x2_stored, g.xl_stored, g.x3_stored, g.x4_stored):
                for u in g.streams:
                    act.wait_ge(stored[u], 16 * NODE_ITERS + 16)
            for k in range(2):
                act.wait_ge(staged[k], 16 * NODE_ITERS + 16)

        @block.tensor
        def _(pe):
            def run(i, part):
                for u, i, step in turns(g, "PE", i, part):
                    pe_update(pe, g, u, i, step)

            run(0, "in")
            with pe.Fori(1, NODE_ITERS) as i:
                run(i, "all")
            run(NODE_ITERS, "out")

        @block.vector
        def _(v):
            for u in g.streams:
                for k, stored in enumerate((g.x1_stored, g.x2_stored, g.x3_stored, g.x4_stored)):
                    v.memset(g.raw[u][:, k:k + 1], 0.0).then_inc(stored[u], 16)
                v.memset(g.variance[u][:, 0:1], 0.0).then_inc(g.xl_stored[u], 16)
                v.memset(g.variance[u][:, 1:], 0.0).then_inc(g.dve_out[u], 1)

            def run(i, part):
                for u, i, step in turns(g, "DVE", i, part):
                    dve_update(v, g, u, i, step)
                    if step == "x4":
                        v.wait_ge(g.x1_stored[u], i * 16 + 32)
                        v.wait_ge(*g.POOL.done(u, i, "sq5_rstd"))
                        dve_scale_rows(v, g, u, g.x3[u][:, :, :], x4[u])

            run(0, "in")
            with v.Fori(1, NODE_ITERS) as i:
                run(i, "all")
            run(NODE_ITERS, "out")

        @block.gpsimd
        def _(pool):
            lists = (c.src_cols, c.dst_gather_cols, c.map_index[0], c.map_index[1])
            for k in range(2):
                pool.memset(index[k][:, :], 0).then_inc(staged[k], 16)

            def side_work(i, step):
                if step == "side_index":
                    cols = ds(i * SIDE_TILES, SIDE_TILES)
                    for k in range(2):
                        pool.wait_ge(staged[k], i * 16 + 16)
                        pool.tensor_copy(index[k][:, :], lists[k][:, cols]).then_inc(index_ready, 1)
                    for k in range(2):
                        pool.tensor_copy(index[2 + k][:, :], lists[2 + k][:, cols]).then_inc(index_ready, 1)
                        pool.tensor_copy(value[k][:, :], c.payload[k][:, cols]).then_inc(index_ready, 1)
                    pool.wait_ge(index_ready, len(lists) + len(value))
                elif step == "side_end":
                    pool.sem_clear(index_ready)
                    for k in range(2):
                        pool.wait_ge(scattered[k], (i + 1) * 16 * SIDE_TILES)
                elif step[0] < 2:
                    k, t = step
                    pool.indirect_dma_start(gathered[k][:, t, :], None, a["x"],
                                            at_index(index[k][:, t:t + 1], 0)).then_inc(gathers_done[k], 16)
                else:
                    k, t = step
                    pool.indirect_dma_start(dram.slot_map_flat, at_index(index[k][:, t:t + 1], 0),
                                            value[k - 2][:, t:t + 1], None, bounds_check=2 * N - 1,
                                            oob_is_err=False).then_inc(scattered[k - 2], 16)

            def run(i, part):
                for u, i, step in turns(g, "POOL", i, part):
                    if u >= 0:
                        pool_update(pool, g, u, i, step)
                    else:
                        side_work(i, step)

            run(0, "in")
            with pool.Fori(1, NODE_ITERS) as i:
                run(i, "all")
            run(NODE_ITERS, "out")



HEADS = {"0": 16, "1": 4, "2a": 8, "2b": 1, "3": 4}
ORDER = {"0": 0, "1": 1, "2a": 0, "2b": 1, "3": 0}
ITER_TILES = PER_ITER // P


def slot_chain(layer):
    own = layer in ("1", "2a", "2b")
    front = {
        "0": [("ACT", "neg", 0.6), ("PE", "srcT", 0.6), ("PE", "dstT", 0.6), ("ACT", "srcT", 0.6), ("ACT", "dstT", 0.6),
              ("PE", "k", 1.0), ("PE", "q", 1.0), ("ACT", "k", 0.6), ("PE", "e0", 1.0), ("DVE", "qk", 0.7),
              ("ACT", "e0", 0.6), ("PE", "e1", 1.0), ("DVE", "qke", 0.7), ("ACT", "e1", 0.6), ("PE", "l", 1.0),
              ("ACT", "l", 0.6), ("PE", "v", 0.4)],
        "1": [("ACT", "neg", 0.6), ("PE", "srcT", 0.6), ("PE", "dstT", 0.6), ("ACT", "srcT", 0.6), ("DVE", "dst", 0.7),
              ("PE", "l", 1.8), ("PE", "ls", 1.0), ("ACT", "l", 0.6), ("ACT", "ls", 0.6), ("DVE", "l", 0.7),
              ("DVE", "ls", 0.7), ("PE", "v", 0.4), ("PE", "o", 0.4), ("DVE", "lm", 0.7)],
        "2a": [("ACT", "neg", 0.6), ("PE", "srcT", 0.6), ("PE", "dstT", 0.6), ("ACT", "srcT", 0.6), ("DVE", "dst", 0.7),
               ("PE", "z", 1.8), ("PE", "zo", 1.0), ("ACT", "z", 0.6), ("ACT", "zo", 0.6), ("DVE", "z", 0.7),
               ("DVE", "zo", 0.7), ("PE", "l", 1.0), ("PE", "ls", 1.0), ("ACT", "l", 0.6), ("ACT", "ls", 0.6),
               ("PE", "v", 0.4), ("PE", "o", 0.4), ("DVE", "lm", 0.7)],
        "2b": [("ACT", "neg", 0.6), ("DVE", "mask", 0.7), ("DVE", "dst", 0.7), ("PE", "srcT", 0.6), ("ACT", "srcT", 0.6),
               ("PE", "z", 1.8), ("PE", "zo", 1.0), ("ACT", "z", 0.6), ("ACT", "zo", 0.6), ("DVE", "z", 0.7),
               ("DVE", "zo", 0.7), ("PE", "l", 1.0), ("PE", "ls", 1.0), ("ACT", "l", 0.6), ("ACT", "ls", 0.6),
               ("PE", "o", 0.4), ("DVE", "lm", 0.7)],
        "3": [("ACT", "neg", 0.6), ("PE", "srcT", 0.6), ("PE", "dstT", 0.6), ("ACT", "srcT", 0.6), ("DVE", "dst", 0.7),
              ("DVE", "deg", 0.4), ("PE", "l", 2.6), ("ACT", "l", 0.6), ("DVE", "l", 0.7), ("PE", "v", 0.4),
              ("DVE", "lm", 0.5)]}[layer]
    softmax = [("DVE", "fc", 0.2), ("DVE", "f", 0.8), ("POOL", "shift", 0.6), ("DVE", "e_p", 0.6)] + \
        ([("DVE", "e_s", 0.7)] if own else []) + ([("DVE", "v", 0.7)] if layer == "0" else []) + \
        [("DVE", "e_c", 0.8), ("ACT", "exp", 1.5)] + ([("ACT", "exps", 0.5)] if layer == "3" else []) + \
        [("DVE", "den", 0.7), ("DVE", "pv", 0.7), ("PE", "tot", 0.5), ("DVE", "num", 0.7)] + \
        ([("DVE", "sv", 0.7), ("POOL", "ns", 0.7)] if own else []) + \
        {"0": [("DVE", "tot", 0.3)], "1": [("DVE", "tot", 0.3)],
         "3": [("DVE", "degE", 0.2), ("DVE", "rest", 0.2), ("DVE", "tot", 0.2)]}.get(layer, []) + \
        [("DVE", "rec", 0.5), ("ACT", "rs", 0.6), ("PE", "rB", 0.6), ("DVE", "agg", 0.8)]
    back = {"0": chain0(True, False), "1": chain1(True, False), "2a": chain2a(True) + [("ACT", "store_T", 0.0)],
            "2b": chain2b(True), "3": [("PE", "y3", 1.9)] + norm_chain("sq5", "x4")}[layer]
    chain = front + softmax + back
    at = chain.index(("ACT", "srcT", 0.6)) + 1
    chain.insert(at, ("POOL", "index", 0.0))
    room = (len(chain) - at - 2) // TILES
    for t in range(TILES):
        chain.insert(at + 2 + t * (room + 1), ("POOL", f"gather{t}", 0.0))
    return chain + {"0": [("POOL", "keep_map", 0.0)], "3": [("POOL", "scatter", 0.0)]}.get(layer, [])


def slot_pass(nc, a, c, dram, layer):
    H = HEADS[layer]
    order = ORDER[layer]
    M = C2 if layer == "2b" else P
    own = layer in ("1", "2a", "2b")
    gatv2 = layer in ("2a", "2b")
    final = SLOT_ITERS - 1
    with ExitStack() as ctx:
        g = Named(c, True, c.last[order])
        phase_tiles(ctx, nc, g, f"slot{layer}", STREAMS, primed=5)
        A, B = g.A, g.B
        plan(g, slot_chain(layer))

        src_width = C2 if layer == "2b" else D
        src_rows = g.many("src_rows", [P, TILES, D])
        dst_rows = g.many("dst_rows", [P, TILES, D])
        keep, neg = g.many("keep", [P, CHUNK]), g.many("neg", [P, CHUNK])
        xs, xd = g.many("xs", [P, CHUNK]), g.many("xd", [P, CHUNK])
        t1, t2 = g.many("t1", [P, CHUNK]), g.many("t2", [P, CHUNK])
        logit_rows = g.many("logit", [P, TILES, D])
        logit = [t[:, :, :].rearrange("p t n -> p (t n)") for t in logit_rows]
        fmax = g.many("fmax", [P, CHUNK + 1])
        expo = g.many("expo", [P, 3, CHUNK])
        den, num = g.many("den", [P, CHUNK]), g.many("num", [P, CHUNK])
        new = g.many("new", [P, TILES, D])
        extra = g.many("extra", [P, CHUNK])
        edge = g.many("edge", [EF, CHUNK]) if layer in ("0", "3") else None
        h2_before = g.many("h2_before", [P, CHUNK]) if layer == "2b" else None
        g.xl = g.many("xl", [P, TILES, C2]) if layer == "2a" else None
        small, recip = g.many("small", [P, TILES, H]), g.many("recip", [P, TILES, H])
        count = g.many("count", [P, TILES])
        g.agg = g.yT = t1
        g.act_T = t2
        g.z = logit_rows
        g.expz = [t[:, 1, :] for t in expo]
        g.x1 = g.x2 = g.x3 = new
        g.xT = g.xT1 = xd
        index, out_index = g.many("index", [P, TILES], I32), g.many("out_index", [P, TILES], I32)
        map_rows = g.many("map_rows", [P, TILES, 2], I32)

        src_ready, dst_ready, keep_ready = g.sems("src_ready"), g.sems("dst_ready"), g.sems("keep_ready")
        edge_ready, g.res_ready = g.sems("edge_ready"), g.sems("res_ready")
        stored, stored_T = g.sems("stored"), g.sems("stored_T")
        g.x1_stored = g.x2_stored = g.x3_stored = g.xl_stored = stored
        index_ready, out_index_ready = g.sems("index_ready"), g.sems("out_index_ready")
        map_ready, map_kept, cleared = g.sems("map_ready"), g.sems("map_kept"), g.sem("cleared")

        g.res2 = lambda u: dst_rows[u][:, :, :].rearrange("p t n -> p (t n)")[:, ::-1]
        start = lambda i, u: i * PER_ITER + u * CHUNK
        mirrored = lambda i, u: i * -PER_ITER + (E_PAD - (u + 1) * CHUNK)
        table = {"1": dram.x1, "2a": dram.x2, "2b": dram.xl2, "3": dram.x3}.get(layer)

        def rows_of(array, first):
            return array[ds(first, CHUNK), :].rearrange("(t p) f -> p t f", p=P)

        g.rows_in_table = lambda array, i, u: rows_of(array, start(i, u) + N_PAD)
        ctx.callback(end_phase, nc, g.all_sems)
        block = ctx.enter_context(nc.Block())

        @block.sync
        def _(sp):
            def load(i, first):
                for u in g.streams:
                    if not first:
                        sp.wait_ge(*g.DVE.done(u, i - 1, "e_c"))
                    sp.dma_start(keep[u][:, :], dram.keep_flat[order][ds(start(i, u), CHUNK)].partition_broadcast(P))\
                      .then_inc(keep_ready[u], 16)
                    if layer == "0":
                        sp.dma_start(src_rows[u][:, :, :], rows_of(dram.staged[0], start(i, u))).then_inc(src_ready[u], 16)
                        sp.dma_start(dst_rows[u][:, :, :], rows_of(dram.staged[1], start(i, u))).then_inc(dst_ready[u], 16)
                    elif layer == "2b":
                        sp.dma_start(h2_before[u][:, :], dram.h2_T[:, ds(mirrored(i, u), CHUNK)]).then_inc(dst_ready[u], 16)
                    else:
                        sp.dma_start(dst_rows[u][:, :, :], rows_of(table, mirrored(i, u) + N_PAD)).then_inc(dst_ready[u], 16)
                    if layer in ("0", "3"):
                        sp.dma_start(edge[u][:, :], a["edge_T"][:, ds(start(i, u), CHUNK)]).then_inc(edge_ready[u], 16)
                    if layer == "2b":
                        if not first:
                            sp.wait_ge(*g.DVE.done(u, i - 1, "y2T"))
                        sp.dma_start(dst_rows[u][:, :, :].rearrange("p t n -> p (t n)"),
                                     dram.x2_T[:, ds(mirrored(i, u), CHUNK)]).then_inc(g.res_ready[u], 16)

            load(0, True)
            with sp.Fori(1, SLOT_ITERS) as i:
                load(i, False)

        @block.gpsimd
        def _(pool):
            def serve(u, i, step):
                if step == "index" and layer == "0":
                    pool.wait_ge(map_kept[u], i + 1)
                    cols, tile_index = c.src_cols, i * ITER_TILES + u * TILES
                elif step == "index":
                    pool.wait_ge(*g.PE.done(u, i, "srcT"))
                    cols, tile_index = c.src_table_cols[order], i * ITER_TILES + (ITER_TILES + u * TILES)
                if step == "index":
                    pool.tensor_copy(index[u][:, :], cols[:, ds(tile_index, TILES)]).then_inc(index_ready[u], 1)
                    pool.wait_ge(index_ready[u], 1)
                    pool.sem_clear(index_ready[u])
                if step.startswith("gather"):
                    gather(u, int(step[-1]))
                if step == "keep_map":
                    pool.wait_ge(map_ready[u], (i + 1) * 16 * TILES)
                    pool.tensor_copy(c.map_cols[:, ds(i * ITER_TILES + u * TILES, TILES), :], map_rows[u][:, :, :])\
                        .then_inc(map_kept[u], 1)
                if step == "scatter":
                    pool.wait_ge(*g.DVE.done(u, i, "x4"))
                    pool.tensor_copy(out_index[u][:, :], c.out_index[:, ds(i * ITER_TILES + u * TILES, TILES)])\
                        .then_inc(out_index_ready[u], 1)
                    pool.wait_ge(out_index_ready[u], 1)
                    pool.sem_clear(out_index_ready[u])
                    for t in range(TILES):
                        pool.indirect_dma_start(a["out"], at_index(out_index[u][:, t:t + 1], 0), new[u][:, t, :], None,
                                                bounds_check=N - 1, oob_is_err=False).then_inc(stored[u], 16)

            def gather(u, t):
                if layer == "0":
                    pool.indirect_dma_start(map_rows[u][:, t, :], None, dram.slot_map, at_index(index[u][:, t:t + 1], 0))\
                        .then_inc(map_ready[u], 16)
                else:
                    pool.indirect_dma_start(src_rows[u][:, t, 0:src_width], None, table, at_index(index[u][:, t:t + 1], 0))\
                        .then_inc(src_ready[u], 16)

            def run(i, part):
                for u, i, step in turns(g, "POOL", i, part):
                    if step == "index" and layer == "3" and not (isinstance(i, int) and i == 0):
                        pool.wait_ge(stored[u], i * 16 * TILES)
                    if step == "shift":
                        pool.wait_ge(*g.ACT.done(u, i, "neg"))
                        pool.wait_ge(*g.DVE.done(u, i, "f"))
                        pool.tensor_tensor(expo[u][0:M, 1, :], fmax[u][0:M, 0:CHUNK], neg[u][0:M, :], ALU.add)\
                            .then_inc(g.pool_out[u], 1)
                    elif step == "ns":
                        pool.wait_ge(*g.DVE.done(u, i, "sv"))
                        pool.tensor_tensor(t2[u][0:M, :], t2[u][0:M, :], num[u][0:M, :], ALU.add).then_inc(g.pool_out[u], 1)
                    elif step.startswith("sq"):
                        pool_update(pool, g, u, i, step)
                    elif layer in ("0",) or step == "scatter" or not (isinstance(i, int) and i == final):
                        serve(u, i, step)

            if layer == "0":
                for u in g.streams:
                    pool.memset(map_rows[u][:, :, :], 0).then_inc(map_kept[u], 1)
            else:
                if layer == "2b":
                    for u in g.streams:
                        pool.memset(src_rows[u][:, :, src_width:], 0.0).then_inc(cleared, 1)
                    pool.wait_ge(cleared, STREAMS)
                for u in g.streams:
                    pool.tensor_copy(index[u][:, :], c.src_table_cols[order][:, u * TILES:(u + 1) * TILES])\
                        .then_inc(index_ready[u], 1)
                for u in g.streams:
                    pool.wait_ge(index_ready[u], 1)
                    pool.sem_clear(index_ready[u])
                    for t in range(TILES):
                        gather(u, t)
            run(0, "in")
            with pool.Fori(1, final) as i:
                run(i, "all")
            run(final, "all")
            run(SLOT_ITERS, "out")
            if layer == "3":
                for u in g.streams:
                    pool.wait_ge(stored[u], SLOT_ITERS * 16 * TILES)

        @block.scalar
        def _(act):
            exps = 3 if own else 2
            z_bias, own_bias = (c.blr1, c.blr1) if layer == "2a" else (c.br2, c.blr2)

            def run(i, part):
                for u, i, step in turns(g, "ACT", i, part):
                    if step == "neg":
                        act.wait_ge(keep_ready[u], (i + 1) * 16)
                        act_copy(act, g, u, neg[u][:, :], keep[u][:, :], scale=BIG, bias=-BIG)
                    elif step == "srcT":
                        act.wait_ge(*g.PE.done(u, i, "srcT"))
                        act_copy(act, g, u, xs[u][0:src_width, :], A(u)[0:src_width, :])
                    elif step == "dstT":
                        act.wait_ge(*g.PE.done(u, i, "dstT"))
                        act_copy(act, g, u, xd[u][:, :], B(u))
                    elif step == "k":
                        act.wait_ge(*g.PE.done(u, i, "k"))
                        act_copy(act, g, u, t1[u][:, :], A(u))
                    elif step == "e0":
                        act.wait_ge(*g.PE.done(u, i, "e0"))
                        act_copy(act, g, u, t2[u][:, :], A(u), ACT.Tanh)
                    elif step == "e1":
                        act.wait_ge(*g.PE.done(u, i, "e1"))
                        act_copy(act, g, u, extra[u][:, :], B(u), ACT.Tanh)
                    elif step == "z":
                        if layer == "2a":
                            act.wait_ge(stored_T[u], i * 32 + 16)
                        act.wait_ge(*g.PE.done(u, i, "z"))
                        act_copy(act, g, u, t1[u][0:M, :], A(u)[0:M, :], ACT.Identity, z_bias[:, 0:1])
                    elif step == "zo":
                        act.wait_ge(*g.PE.done(u, i, "zo"))
                        act_copy(act, g, u, t2[u][0:M, :], B(u)[0:M, :], ACT.Identity, own_bias[:, 0:1])
                    elif step == "l":
                        act.wait_ge(*g.PE.done(u, i, "l"))
                        if layer == "0":
                            act_copy(act, g, u, logit[u], A(u), scale=float((D // H) ** -0.5))
                        elif gatv2:
                            act_copy(act, g, u, logit[u][0:M, :], A(u)[0:M, :])
                        else:
                            act_copy(act, g, u, t1[u][:, :], A(u), scale=SLOPE)
                    elif step == "ls":
                        act.wait_ge(*g.PE.done(u, i, "ls"))
                        if gatv2:
                            act_copy(act, g, u, extra[u][0:M, :], B(u)[0:M, :])
                        else:
                            act_copy(act, g, u, t2[u][:, :], B(u), scale=SLOPE)
                    elif step == "exp":
                        act.wait_ge(*g.DVE.done(u, i, "e_c"))
                        act_copy(act, g, u, expo[u][0:M, 0:exps, :], expo[u][0:M, 0:exps, :], ACT.Exp)
                    elif step == "exps":
                        act_copy(act, g, u, expo[u][:, 2, :], fmax[u][:, 1:CHUNK + 1], ACT.Exp, scale=-1.0)
                    elif step == "rs":
                        act.wait_ge(*g.DVE.done(u, i, "rec"))
                        act_copy(act, g, u, expo[u][:, 0, :].rearrange("p (t h k) -> p t h k", t=TILES, h=H),
                                 recip[u][:, :, :].unsqueeze(3).broadcast_to([P, TILES, H, D // H]))
                    elif step == "sq5":
                        act.wait_ge(*g.PE.done(u, i, "y3"))
                        act_squares(act, g, u, tiles_of(A(u)))
                    elif step == "store_T":
                        for array, tile, ready in ((dram.x2_T, xd, "dst"), (dram.h2_T, g.act_T, "h2")):
                            act.wait_ge(*g.DVE.done(u, i, ready))
                            act.dma_start(array[:, ds(start(i, u), CHUNK)], tile[u][:, :]).then_inc(stored_T[u], 16)
                    else:
                        act_update(act, g, u, i, step)

            run(0, "in")
            with act.Fori(1, SLOT_ITERS) as i:
                run(i, "all")
            run(SLOT_ITERS, "out")
            if layer != "3":
                for u in g.streams:
                    act.wait_ge(stored[u], 16 * SLOT_ITERS + 16)
            if layer == "2a":
                for u in g.streams:
                    act.wait_ge(stored_T[u], 32 * SLOT_ITERS + 16)

        @block.tensor
        def _(pe):
            heads = c.ident[0:M, 0:M:D // H] if layer != "2b" else c.ident[0:M, 0:1]

            def product(u, bank, pairs, m=P):
                for k, (weights, tile) in enumerate(pairs):
                    ins = pe.matmul(bank(u)[0:m, :], weights, tile, start=k == 0, stop=k == len(pairs) - 1)
                ins.then_inc(g.pe_out[u], 1)

            def run(i, part):
                for u, i, step in turns(g, "PE", i, part):
                    src, dst, first, second = xs[u][:, :], xd[u][:, :], t1[u][0:M, :], t2[u][0:M, :]
                    if step == "srcT":
                        pe.wait_ge(*g.DVE.before(u, i))
                        if layer == "2a":
                            pe.wait_ge(stored[u], i * 16 + 16)
                        pe.wait_ge(src_ready[u], (i + 1) * (16 if layer == "0" else 16 * TILES))
                        pe_transposes(pe, g, u, A, src_rows[u])
                    elif step == "dstT":
                        pe.wait_ge(dst_ready[u], (i + 1) * 16)
                        pe_transposes(pe, g, u, B, dst_rows[u])
                    elif layer == "0" and step == "k":
                        pe.wait_ge(*g.ACT.done(u, i, "srcT"))
                        product(u, A, [(c.Wk[:, :], src)])
                    elif layer == "0" and step == "q":
                        pe.wait_ge(*g.ACT.done(u, i, "dstT"))
                        product(u, B, [(c.Wq[:, :], dst)])
                    elif layer == "0" and step == "e0":
                        pe.wait_ge(edge_ready[u], (i + 1) * 16)
                        pe.wait_ge(*g.ACT.done(u, i, "k"))
                        product(u, A, [(c.We0[:, :], edge[u][:, :])])
                    elif layer == "0" and step == "e1":
                        pe.wait_ge(*g.DVE.done(u, i, "qk"))
                        product(u, B, [(c.We1[:, :], edge[u][:, :])])
                    elif layer == "0" and step == "l":
                        pe.wait_ge(*g.DVE.done(u, i, "qke"))
                        product(u, A, [(c.S16[:, :], first)])
                    elif layer == "0" and step == "v":
                        pe.wait_ge(*g.ACT.done(u, i, "e1"))
                        product(u, B, [(c.Wv[:, :], src)])
                    elif layer == "1" and step == "l":
                        pe.wait_ge(*g.ACT.done(u, i, "srcT"))
                        pe.wait_ge(*g.DVE.done(u, i, "dst"))
                        product(u, A, [(c.Wsa[:, :], src), (c.Wda[:, :], dst)])
                    elif layer == "1" and step == "ls":
                        product(u, B, [(c.Wsd[:, :], dst)])
                    elif layer == "1" and step in ("v", "o"):
                        pe.wait_ge(*g.DVE.done(u, i, "l" if step == "v" else "ls"))
                        product(u, A if step == "v" else B, [(c.W[:, :], src if step == "v" else dst)])
                    elif gatv2 and step == "z":
                        pe.wait_ge(*g.ACT.done(u, i, "srcT"))
                        pe.wait_ge(*g.DVE.done(u, i, "dst"))
                        if layer == "2a":
                            product(u, A, [(c.Wl1[:, :], src), (c.Wr1[:, :], dst)])
                        else:
                            product(u, A, [(c.Wr2[:, :], dst), (c.ident[0:C2, 0:C2], xs[u][0:C2, :])], M)
                    elif gatv2 and step == "zo":
                        pe.wait_ge(*g.DVE.done(u, i, "dst"))
                        product(u, B, [((c.Wlr1 if layer == "2a" else c.Wlr2)[:, :], dst)], M)
                    elif gatv2 and step in ("l", "ls"):
                        pe.wait_ge(*g.DVE.done(u, i, "z" if step == "l" else "zo"))
                        product(u, A if step == "l" else B,
                                [((c.S1 if layer == "2a" else c.S2)[:, :], first if step == "l" else second)])
                    elif gatv2 and step in ("v", "o"):
                        pe.wait_ge(*g.ACT.done(u, i, "l" if step == "v" else "ls"))
                        product(u, A if step == "v" else B,
                                [((c.Wl1 if layer == "2a" else c.Wl2)[:, :], src if step == "v" else dst)], M)
                    elif layer == "3" and step == "l":
                        pe.wait_ge(edge_ready[u], (i + 1) * 16)
                        pe.wait_ge(*g.ACT.done(u, i, "srcT"))
                        pe.wait_ge(*g.DVE.done(u, i, "dst"))
                        product(u, A, [(c.Wsrc[:, :], src), (c.Wtgt[:, :], dst), (c.Wedge[:, :], edge[u][:, :])])
                    elif layer == "3" and step == "v":
                        pe.wait_ge(*g.DVE.done(u, i, "l"))
                        product(u, A, [(c.WnT[:, :], src)])
                    elif step == "tot":
                        pe.wait_ge(*g.DVE.done(u, i, "pv"))
                        for t in range(TILES):
                            cols = slice(t * H, (t + 1) * H)
                            ins = pe.matmul(A(u)[:, cols], den[u][0:M, tile_cols(t)], heads, start=True, stop=not own)
                            if own:
                                ins = pe.matmul(A(u)[:, cols], expo[u][0:M, 2, tile_cols(t)], heads, start=False, stop=True)
                            if layer == "3":
                                pe.matmul(A(u)[:, 16 + t * H:16 + (t + 1) * H], expo[u][:, 2, tile_cols(t)], heads,
                                          start=True, stop=True)
                                ins = pe.matmul(A(u)[:, 32 + t:33 + t], extra[u][:, tile_cols(t)], c.ident[:, 0:1],
                                                start=True, stop=True)
                        ins.then_inc(g.pe_out[u], 1)
                    elif step == "rB":
                        pe.wait_ge(*g.ACT.done(u, i, "rs"))
                        pe_transposes(pe, g, u, B, tiles_of(expo[u][:, 0, :]))
                    elif step == "y3":
                        pe.wait_ge(*g.DVE.done(u, i, "agg"))
                        pe_rows(pe, g, u, A, [(g.agg[u], c.center[:, :]), (xd[u], c.center[:, :])])
                    else:
                        pe_update(pe, g, u, i, step)

            run(0, "in")
            with pe.Fori(1, SLOT_ITERS) as i:
                run(i, "all")
            run(SLOT_ITERS, "out")

        @block.vector
        def _(v):
            for u in g.streams:
                if layer != "3":
                    v.memset(new[u][:, 0, 0:1], 0.0).then_inc(stored[u], 16)
                v.memset(t2[u][:, 0:1], 0.0).then_inc(stored_T[u], 16)
                for t, col in ((xd, CHUNK - 1), (extra, CHUNK - 1), (fmax, CHUNK), (den, CHUNK - 1), (num, CHUNK - 1)):
                    v.memset(t[u][:, col:col + 1], 0.0).then_inc(g.dve_out[u], 1)

            sums = lambda u: A(u)[:, 0:TILES * H].rearrange("p (t h) -> p t h", t=TILES)

            def carry(u, i, tile, step, m=P):
                if u > 0:
                    v.wait_ge(*g.DVE.done(u - 1, i, step))
                elif isinstance(i, int):
                    v.wait_ge(*g.DVE.before(STREAMS - 1, 0))
                else:
                    v.wait_ge(*g.DVE.done(STREAMS - 1, i - 1, step))
                return tile[u - 1][0:m, -1:]

            def run(i, part):
                for u, i, step in turns(g, "DVE", i, part):
                    def after(name):
                        v.wait_ge(*g.DVE.done(u, i, name))

                    ins = None
                    f = fmax[u][0:M, 1:CHUNK + 1]
                    if step == "mask":
                        v.wait_ge(dst_ready[u], (i + 1) * 16)
                        v.wait_ge(keep_ready[u], (i + 1) * 16)
                        ins = v.scalar_tensor_tensor(out=t1[u][:, :], in0=keep[u][:, :], scalar=-1.0,
                                                     in1=h2_before[u][:, ::-1], op0=ALU.add, op1=ALU.mult)
                    elif step == "dst":
                        before = carry(u, i, xd, "dst")
                        if layer == "2b":
                            after("mask")
                            ins = v.tensor_tensor_scan(xd[u][:, :], keep[u][:, :], t1[u][:, :], before, ALU.mult, ALU.subtract)
                        else:
                            if layer == "2a":
                                v.wait_ge(stored_T[u], i * 32 + 16)
                            v.wait_ge(keep_ready[u], (i + 1) * 16)
                            v.wait_ge(*g.PE.done(u, i, "dstT"))
                            ins = v.tensor_tensor_scan(xd[u][:, :], keep[u][:, :], B(u)[:, ::-1], before, ALU.mult, ALU.add)
                    elif step == "deg":
                        before = carry(u, i, extra, "deg")
                        ins = v.tensor_tensor_scan(extra[u][:, :], keep[u][:, :], c.minus_one[:, :], before, ALU.mult, ALU.add)
                    elif step == "qk":
                        v.wait_ge(*g.PE.done(u, i, "q"))
                        v.wait_ge(*g.ACT.done(u, i, "k"))
                        ins = v.tensor_tensor(t1[u][:, :], B(u), t1[u][:, :], ALU.mult)
                    elif step == "qke":
                        after("qk")
                        v.wait_ge(*g.ACT.done(u, i, "e0"))
                        ins = v.tensor_tensor(t1[u][:, :], t1[u][:, :], t2[u][:, :], ALU.mult)
                    elif step == "l":
                        v.wait_ge(*g.ACT.done(u, i, "l"))
                        ins = v.tensor_tensor(logit[u], A(u), t1[u][:, :], ALU.max)
                    elif step == "ls":
                        v.wait_ge(*g.ACT.done(u, i, "ls"))
                        ins = v.tensor_tensor(extra[u][:, :], B(u), t2[u][:, :], ALU.max)
                    elif step in ("z", "zo"):
                        z = (t1 if step == "z" else t2)[u][0:M, :]
                        v.wait_ge(*g.ACT.done(u, i, step))
                        ins = v.scalar_tensor_tensor(out=z, in0=z, scalar=SLOPE, in1=z, op0=ALU.mult, op1=ALU.max)
                    elif step == "lm" and own:
                        if gatv2:
                            v.wait_ge(*g.ACT.done(u, i, "ls"))
                        else:
                            after("ls")
                        ins = v.tensor_tensor(t1[u][0:M, :], logit[u][0:M, :], extra[u][0:M, :], ALU.max)
                    elif step == "lm":
                        after("l")
                        ins = v.tensor_scalar(t1[u][:, :], logit[u], 0.0, None, ALU.max)
                    elif step == "fc":
                        ins = v.tensor_copy(fmax[u][0:M, 0:1], carry(u, i, fmax, "f", M))
                    elif step == "f":
                        highest = logit[u] if layer == "0" else t1[u][:, :]
                        v.wait_ge(*g.ACT.done(u, i, "l" if layer == "0" else "neg"))
                        after("fc")
                        ins = v.tensor_tensor_scan(f, neg[u][0:M, :], highest[0:M, :], fmax[u][0:M, 0:1], ALU.add, ALU.max)
                    elif step == "e_p":
                        after("f")
                        ins = v.tensor_tensor(expo[u][0:M, 0, :], logit[u][0:M, :], f, ALU.subtract)
                    elif step == "e_s":
                        after("f")
                        ins = v.tensor_tensor(expo[u][0:M, 2, :], extra[u][0:M, :], f, ALU.subtract)
                    elif step == "e_c":
                        v.wait_ge(*g.POOL.done(u, i, "shift"))
                        ins = v.tensor_tensor(expo[u][0:M, 1, :], expo[u][0:M, 1, :], f, ALU.subtract)
                    elif step == "v":
                        v.wait_ge(*g.PE.done(u, i, "v"))
                        ins = v.tensor_tensor(extra[u][:, :], B(u), extra[u][:, :], ALU.mult)
                    elif step == "den":
                        before = carry(u, i, den, "den", M)
                        v.wait_ge(*g.ACT.done(u, i, "exps" if layer == "3" else "exp"))
                        ins = v.tensor_tensor_scan(den[u][0:M, :], expo[u][0:M, 1, :], expo[u][0:M, 0, :], before,
                                                   ALU.mult, ALU.add)
                    elif step == "pv" and layer == "0":
                        after("v")
                        ins = v.tensor_tensor(t1[u][:, :], extra[u][:, :], expo[u][:, 0, :], ALU.mult)
                    elif step == "pv" and layer == "2b":
                        ins = v.tensor_tensor(t1[u][0:M, :], xs[u][0:M, :], expo[u][0:M, 0, :], ALU.mult)
                    elif step == "pv":
                        v.wait_ge(*g.PE.done(u, i, "v"))
                        if layer == "2a":
                            ins = v.scalar_tensor_tensor(out=t1[u][:, :], in0=A(u), scalar=c.bl1[:, 0:1],
                                                         in1=expo[u][:, 0, :], op0=ALU.add, op1=ALU.mult)
                        else:
                            ins = v.tensor_tensor(t1[u][:, :], A(u), expo[u][:, 0, :], ALU.mult)
                    elif step == "num":
                        before = carry(u, i, num, "num", M)
                        after("pv")
                        ins = v.tensor_tensor_scan(num[u][0:M, :], expo[u][0:M, 1, :], t1[u][0:M, :], before, ALU.mult, ALU.add)
                    elif step == "sv":
                        v.wait_ge(*g.PE.done(u, i, "o"))
                        if layer == "1":
                            ins = v.tensor_tensor(t2[u][:, :], B(u), expo[u][:, 2, :], ALU.mult)
                        else:
                            bias = c.bl1 if layer == "2a" else c.bl2
                            ins = v.scalar_tensor_tensor(out=t2[u][0:M, :], in0=B(u)[0:M, :], scalar=bias[:, 0:1],
                                                         in1=expo[u][0:M, 2, :], op0=ALU.add, op1=ALU.mult)
                    elif step == "degE":
                        v.wait_ge(*g.PE.done(u, i, "tot"))
                        ins = v.tensor_scalar(count[u][:, :], A(u)[:, 32:32 + TILES], float(E), None, ALU.add)
                    elif step == "rest":
                        after("degE")
                        ins = v.tensor_tensor(small[u][:, :, :], A(u)[:, 16:16 + TILES * H].rearrange("p (t h) -> p t h", t=TILES),
                                              count[u][:, :].unsqueeze(2).broadcast_to([P, TILES, H]), ALU.mult)
                    elif step == "tot" and layer == "3":
                        after("rest")
                        ins = v.tensor_tensor(small[u][:, :, :], sums(u), small[u][:, :, :], ALU.add)
                    elif step == "tot":
                        v.wait_ge(*g.PE.done(u, i, "tot"))
                        ins = v.tensor_scalar(small[u][:, :, :], sums(u), SOFTMAX_EPS, None, ALU.add)
                    elif step == "rec" and gatv2:
                        v.wait_ge(*g.PE.done(u, i, "tot"))
                        ins = v.reciprocal(recip[u][:, :, :], sums(u))
                    elif step == "rec":
                        after("tot")
                        ins = v.reciprocal(recip[u][:, :, :], small[u][:, :, :])
                    elif step == "agg":
                        if own:
                            v.wait_ge(*g.POOL.done(u, i, "ns"))
                        else:
                            after("num")
                        v.wait_ge(*g.PE.done(u, i, "rB"))
                        weighted = (t2 if own else num)[u]
                        ins = v.tensor_tensor(g.agg[u][0:M, :], weighted[0:M, :], B(u)[0:M, :], ALU.mult)
                    elif step == "x4":
                        v.wait_ge(*g.POOL.done(u, i, "sq5_rstd"))
                        dve_scale_rows(v, g, u, tiles_of(A(u)), new[u])
                    else:
                        dve_update(v, g, u, i, step)
                    if ins is not None:
                        ins.then_inc(g.dve_out[u], 1)

            run(0, "in")
            with v.Fori(1, SLOT_ITERS) as i:
                run(i, "all")
            run(SLOT_ITERS, "out")


def source_columns(nc, c):
    with ExitStack() as own:
        as_float = own.enter_context(nc.sbuf_tensor("map_as_float", [P, SLOT_TILES], F32))
        sem = lambda name: own.enter_context(nc.semaphore(name))
        copied, flipped = sem("map_copied"), sem("map_flipped")
        block = own.enter_context(nc.Block())

        @block.vector
        def _(v):
            v.tensor_copy(as_float[:, :], c.map_cols[:, :, 0]).then_inc(copied, 1)
            v.tensor_copy(c.src_table_cols[0][:, :], c.map_cols[:, :, 1]).then_inc(copied, 1)
            v.wait_ge(flipped, 1)
            v.tensor_copy(c.src_table_cols[1][:, :], c.psum[:, 0, SLOT_TILES - 1::-1]).then_inc(copied, 1)
            v.wait_ge(copied, 3)

        @block.tensor
        def _(pe):
            pe.wait_ge(copied, 1)
            pe.matmul(c.psum[:, 0, 0:SLOT_TILES], c.anti[:, :], as_float[:, :], start=True, stop=True).then_inc(flipped, 1)


def build(nc, a):
    c, dram = Named(), Named()
    c.dram = dram

    def scratch(name, shape, dt=F32):
        return nc.dram_tensor(name, shape, dt, kind="Internal").ap()

    dram.x1, dram.x2, dram.x3 = (scratch(n, [ROWS, D]) for n in ("x1", "x2", "x3"))
    dram.xl2 = scratch("xl2", [ROWS, C2])
    dram.x2_T, dram.h2_T = scratch("x2_T", [D, E_PAD]), scratch("h2_T", [D, E_PAD])
    dram.staged = [scratch(f"staged{k}", [E_PAD, D]) for k in range(2)]
    dram.slot_map = scratch("slot_map", [N, 2], I32)
    dram.slot_map_flat = dram.slot_map.rearrange("n (o k) -> (n o) k", k=1)
    dram.keep = [scratch(f"keep{o}", [SLOT_CHUNKS, CHUNK]) for o in range(2)]
    dram.neg = [scratch(f"neg{o}", [SLOT_CHUNKS, CHUNK]) for o in range(2)]
    dram.keep_flat = [t.rearrange("a b -> (a b)") for t in dram.keep]
    dram.neg_flat = [t.rearrange("a b -> (a b)") for t in dram.neg]

    with ExitStack() as ctx:
        c.psum = ctx.enter_context(nc.psum_tensor("psum", [P, 8, CHUNK], F32))
        c.map_cols = ctx.enter_context(nc.sbuf_tensor("map_cols", [P, SLOT_TILES, 2], I32))
        c.src_table_cols = [ctx.enter_context(nc.sbuf_tensor(f"src_table_cols{o}", [P, SLOT_TILES], I32)) for o in range(2)]
        prepare(nc, a, c, dram, ctx)
        node_pass(nc, a, c, dram)
        slot_pass(nc, a, c, dram, "0")
        source_columns(nc, c)
        for layer in ("1", "2a", "2b", "3"):
            slot_pass(nc, a, c, dram, layer)



def lay_out(inputs):
    out = {k: np.ascontiguousarray(v) for k, v in inputs.items() if k not in ("src", "dst", "edge_attr_64", "L3_gnn_W_node")}
    out["L3_gnn_W_node"] = np.ascontiguousarray(inputs["L3_gnn_W_node"])
    out["W_node_T"] = np.ascontiguousarray(np.asarray(inputs["L3_gnn_W_node"]).T)
    x_T = np.zeros((D, N_PAD), np.float32)
    x_T[:, :N] = np.asarray(inputs["x"]).T
    out["x_T"] = x_T
    edge_T = np.zeros((EF, E_PAD), np.float32)
    edge_T[:, :E] = np.asarray(inputs["edge_attr_64"]).T
    out["edge_T"] = edge_T
    src, dst = np.asarray(inputs["src"]), np.asarray(inputs["dst"])
    more = E_PAD - E

    def columns(t):
        return np.ascontiguousarray(t.reshape(SLOT_TILES, P).T)

    def chunks(t):
        return np.ascontiguousarray(t.reshape(SLOT_CHUNKS, CHUNK))

    out["src_cols"] = columns(np.concatenate([src, np.zeros(more, src.dtype)]))
    out["dst_gather_cols"] = columns(np.concatenate([dst, np.zeros(more, dst.dtype)]))
    ended = np.concatenate([np.full(1, -1, dst.dtype), dst, np.full(more, N, dst.dtype), np.full(1, -1, dst.dtype)])
    both = [ended, ended[::-1]]
    out["dst_cols"] = np.stack([columns(t[1:-1]) for t in both])
    out["dst_next_cols"] = np.stack([columns(t[2:]) for t in both])
    out["dst_prev_cols"] = columns(ended[:-2])
    out["dst_rows"] = np.stack([chunks(t[1:-1]) for t in both])
    out["dst_prev_rows"] = np.stack([chunks(t[:-2]) for t in both])
    return out


def kernel(**inputs):
    import concourse.bacc as bacc
    from concourse.bass_utils import run_bass_kernel_spmd

    nc = bacc.Bacc("TRN2", target_bir_lowering=False, num_devices=1)
    a = {}
    arrays = {}
    for name, array in lay_out(inputs).items():
        arrays[f"in_{name}"] = array
        a[name] = nc.dram_tensor(f"in_{name}", array.shape, mybir.dt.from_np(array.dtype),
                                          kind="ExternalInput").ap()
    a["out"] = nc.dram_tensor("out_nodes", [N_PAD, D], F32, kind="ExternalOutput").ap()
    build(nc, a)
    r = run_bass_kernel_spmd(nc, [arrays], core_ids=[0])
    return r.results[0]["out_nodes"][:N]
```

```python
from contextlib import ExitStack

import numpy as np

import concourse.bass as bass
from concourse import mybir


class Named:

    def __init__(self, c=None, slots=False, last_flags=None):
        self.c, self.slots, self.last_flags = c, slots, last_flags


P = 128
CHUNK = 512
TILES = CHUNK // P
D = 128
EF = 64
N = 50000
E = 25000
BIG = 1.0e30
OUT_OF_RANGE = 1 << 22
LN_EPS = 1e-5
SOFTMAX_EPS = 1e-16
SLOPE = 0.2

NODE_STREAMS = 7
STREAMS = 4
NODE_ITERS = -(-N // (NODE_STREAMS * CHUNK))
SLOT_ITERS = -(-E // (STREAMS * CHUNK))
PER_ITER = STREAMS * CHUNK
NODES_PER_ITER = NODE_STREAMS * CHUNK
N_PAD = NODE_ITERS * NODES_PER_ITER
E_PAD = SLOT_ITERS * PER_ITER
SIDE_TILES = -(-E // (P * NODE_ITERS))
E_STAGED = NODE_ITERS * SIDE_TILES * P
SLOT_CHUNKS = E_PAD // CHUNK
SLOT_TILES = E_PAD // P
ROWS = N_PAD + E_PAD
C2 = 64

F32 = mybir.dt.float32
BF16 = mybir.dt.bfloat16
I32 = mybir.dt.int32
ALU = mybir.AluOpType
ACT = mybir.ActivationFunctionType
at_index = bass.IndirectOffsetOnAxis
ds = bass.ds


class Steps:

    def __init__(self, sems, primed=0):
        self.sems, self.primed, self.names = sems, primed, []

    def done(self, u, i, name):
        return self.sems[u], i * len(self.names) + self.names.index(name) + 1 + self.primed

    def before(self, u, i):
        return self.sems[u], i * len(self.names) + self.primed


PLAN = {
        "node": (6.61, (2.400, 2.660, 3.600, 3.610, 4.820, 4.830, 4.840, 6.530, 7.930, 10.210, 10.220, 10.720,
        24.360, 10.730, 12.540, 12.550, 12.560, 14.960, 16.410, 17.230, 17.240, 17.380, 21.100, 23.000, 23.010,
        25.030, 26.700, 27.420, 27.430, 27.430, 27.950, 29.310, 29.320, 30.300, 30.320, 30.330, 30.340, 35.290,
        30.580, 32.640, 35.560, 35.570, 36.900, 36.910, 37.220, 37.230, 38.260, 38.270, 38.650, 41.370, 42.390,
        42.850, 43.830, 43.280, 44.400, 44.410, 45.750, 45.760), (0.01, 0.55, 1.50, 3.45, 3.86, 6.01)),
        "0": (16.18, (0.010, 0.010, 2.540, 2.930, 3.690, 4.420, 6.540, 6.200, 6.660, 8.620, 8.720, 8.630, 8.730,
        15.430, 9.780, 15.440, 15.440, 17.860, 17.870, 18.200, 18.640, 18.650, 19.340, 18.660, 20.250, 20.260,
        22.150, 22.150, 22.550, 23.150, 23.160, 24.570, 27.580, 27.590, 32.520, 35.880, 37.490, 40.090, 42.090,
        48.580, 51.420, 52.330, 55.000, 58.250, 58.510, 62.320, 62.330, 10.460, 18.670, 16.860, 17.600, 13.540,
        24.610, 29.830, 36.210, 36.120, 25.970, 35.260), ()),
        "1": (14.38, (0.010, 0.010, 6.420, 3.920, 6.430, 9.970, 13.380, 10.830, 15.500, 16.950, 17.560, 18.630,
        20.150, 17.570, 17.670, 18.320, 18.330, 19.400, 19.410, 19.420, 21.470, 24.440, 24.450, 26.210, 25.320,
        27.160, 27.700, 30.140, 31.610, 31.620, 31.630, 36.340, 36.350, 38.030, 38.040, 40.860, 45.720, 45.730,
        46.030, 49.800, 51.220, 51.580, 51.590, 51.600, 56.940, 56.950, 7.740, 33.290, 34.320, 34.720, 15.320), ()),
        "2a": (8.79, (0.010, 0.010, 0.050, 1.490, 0.550, 3.010, 3.120, 4.190, 4.320, 4.950, 7.340, 5.970, 7.540,
        7.410, 7.780, 7.560, 9.880, 10.100, 11.580, 14.900, 15.920, 16.820, 17.210, 17.720, 19.160, 19.400, 21.990,
        23.440, 25.770, 25.780, 27.120, 25.890, 27.140, 27.150, 27.600, 29.120, 29.130, 30.380, 31.740, 32.960,
        32.970, 33.570, 13.680, 14.340, 20.400, 28.830, 23.450), ()),
        "2b": (14.94, (0.010, 1.220, 1.990, 3.460, 4.040, 4.860, 4.870, 8.070, 9.100, 8.510, 9.110, 10.040, 10.050,
        12.620, 12.720, 17.450, 15.890, 15.900, 16.030, 16.040, 16.690, 16.050, 18.130, 19.220, 22.220, 22.920,
        29.640, 23.410, 24.800, 27.890, 30.900, 31.900, 31.910, 31.920, 34.130, 34.190, 36.600, 36.710, 41.990,
        42.370, 42.700, 44.700, 49.410, 51.520, 51.750, 55.620, 57.090, 57.370, 58.030, 4.550, 33.600, 24.920,
        42.630, 34.030), ()),
        "3": (6.15, (0.000, 0.602, 1.204, 1.806, 2.410, 3.114, 3.516, 6.118, 6.720, 7.422, 7.824, 8.326, 8.530,
        9.332, 9.934, 10.536, 11.338, 12.840, 13.342, 14.046, 14.748, 15.250, 15.952, 16.154, 16.356, 16.558,
        17.062, 17.664, 18.266, 19.068, 20.970, 22.172, 22.474, 23.676, 24.478, 2.408, 3.112, 8.528, 14.044,
        17.060), ()),
}


def order_of_work(chain, phase, streams, others=()):
    period, starts, between = PLAN[phase]
    placed = []
    for u in range(streams):
        for (engine, step), start in zip(chain, starts, strict=True):
            now = start + u * period
            placed.append((now % (streams * period), u, int(now // (streams * period)), engine, step))
    for n, step in enumerate(others):
        placed.append((n // len(between) * period + between[n % len(between)], -1, 0, "POOL", step))
    placed.sort(key=lambda item: item[0])
    return [item[1:] for item in placed]


def turns(g, engine, i, part):
    for u, late, of, step in g.order:
        if of == engine and (part == "all" or late == (part == "out")):
            yield u, (i - 1 if late else i), step


def plan(g, chain, phase, others=()):
    g.order = order_of_work(chain, phase, len(g.streams), others)
    for steps, engine in ((g.PE, "PE"), (g.ACT, "ACT"), (g.DVE, "DVE"), (g.POOL, "POOL")):
        steps.names = [step for of, step in chain if of == engine and not step.startswith(UNCOUNTED)]


UNCOUNTED = ("store", "index", "gather", "dst_index", "dst_gather", "keep_map", "scatter")


def tiles_of(t):
    return t.rearrange("p (t n) -> p t n", t=TILES)


def tile_cols(t, width=P):
    return slice(t * width, (t + 1) * width)



def pe_rows(pe, g, u, bank, parts, bias=None, width=P):
    if bias is not None:
        pe.matmul(bank(u)[:, 0:TILES * width], g.c.ones[:, :], bias[:, 0:TILES * width], start=True, stop=False)
    for t in range(TILES):
        for k, (tile, weights) in enumerate(parts):
            ins = pe.matmul(bank(u)[:, tile_cols(t, width)], tile[:, tile_cols(t)], weights,
                            start=bias is None and k == 0,
                            stop=k == len(parts) - 1 and (bias is None or t == TILES - 1))
    ins.then_inc(g.pe_out[u], 1)


def pe_transposes(pe, g, u, bank, rows):
    for t in range(TILES):
        ins = pe.transpose(bank(u)[:, tile_cols(t)], rows[:, t, :], g.c.ident[:, :])
    ins.then_inc(g.pe_out[u], 1)


def act_copy(act, g, u, out, source, func=ACT.Copy, bias=0.0, scale=1.0):
    act.activation(out, source, func, bias=bias, scale=scale).then_inc(g.act_out[u], 1)


def act_squares(act, g, u, rows):
    for t in range(TILES):
        ins = act.activation(g.z[u][:, t, :], rows[:, t, :], ACT.Square, scale=float(D ** -0.5),
                             accum_out=g.mean_square[u][:, t:t + 1])
    ins.then_inc(g.act_out[u], 1)


def dve_scale_rows(v, g, u, source, out):
    v.tensor_tensor(out[:, :, :], source, g.rstd[u][:, :].unsqueeze(2).broadcast_to([P, TILES, D]), ALU.mult)\
     .then_inc(g.dve_out[u], 1)


def norm_chain(tag, out, last=False):
    return [("ACT", tag), ("POOL", tag + "_eps"), ("POOL", tag + ("_pow" if last else "_rstd"))] + \
        ([("POOL", tag + "_rstd")] if last else []) + [("DVE", out)]


def end_phase(nc, sems):
    nc.clear_and_free_semaphores(sems)
    nc.all_engine_barrier()


def phase_tiles(ctx, nc, g, prefix, streams, primed):
    g.streams = range(streams)

    def sb(name, shape, dt=F32):
        return ctx.enter_context(nc.sbuf_tensor(f"{prefix}_{name}", shape, dt))

    g.sb = sb
    g.many = lambda name, shape, dt=F32: [sb(f"{name}{u}", shape, dt) for u in g.streams]
    g.mean_square = g.many("mean_square", [P, TILES])
    g.variance = g.many("variance", [P, TILES])
    g.raw = g.many("raw", [P, TILES])
    g.rstd = g.many("rstd", [P, TILES])
    g.all_sems = []

    def sem(name):
        g.all_sems.append(nc.alloc_semaphore(f"{prefix}_{name}"))
        return g.all_sems[-1]

    g.sem = sem
    g.sems = lambda name: [sem(f"{name}{u}") for u in g.streams]
    g.pe_out, g.act_out, g.dve_out, g.pool_out = (g.sems(n) for n in ("pe_out", "act_out", "dve_out", "pool_out"))
    g.PE, g.ACT, g.POOL = Steps(g.pe_out), Steps(g.act_out), Steps(g.pool_out)
    g.DVE = Steps(g.dve_out, primed)
    g.A = lambda u: g.c.psum[:, 2 * u, :]
    g.B = lambda u: g.c.psum[:, 2 * u + 1, :]



def prepare(nc, a, c, dram, ctx):
    def sb(name, shape, dt=F32):
        return ctx.enter_context(nc.sbuf_tensor(name, shape, dt))

    loads = []

    def load(name, shape, src, dt=F32, room=None):
        t = (room or sb)(name, shape, dt)
        loads.append((t[:], src))
        return t

    def column(name, src, m=P):
        return load(name, [m, 1], src.rearrange("(p o) -> p o", o=1))

    def row(name, src, m=P):
        return load(name, [P, m], src.partition_broadcast(P))

    own = ExitStack()

    def temp(name, shape, dt=F32):
        return own.enter_context(nc.sbuf_tensor(name, shape, dt))

    c.Wq = load("Wq", [P, D], a["L0_gnn_Wq"])
    c.Wk = load("Wk", [P, D], a["L0_gnn_Wk"])
    c.Wv = load("Wv", [P, D], a["L0_gnn_Wv"])
    c.We0 = load("We0", [EF, D], a["L0_gnn_We0"])
    c.We1 = load("We1", [EF, D], a["L0_gnn_We1"])
    c.W = load("W", [P, D], a["L1_gnn_W"])
    c.Wl1 = load("Wl1", [P, D], a["L2_gnn_Wl1"])
    c.Wr1 = load("Wr1", [P, D], a["L2_gnn_Wr1"])
    c.Wl2 = load("Wl2", [P, C2], a["L2_gnn_Wl2"])
    c.Wr2 = load("Wr2", [P, C2], a["L2_gnn_Wr2"])
    c.Wlin = load("Wlin", [C2, D], a["L2_gnn_Wlin"])
    c.WnT = load("WnT", [P, D], a["W_node_T"])
    c.ln_g = column("ln_g", a["L0_gnn_ln_g"])
    c.ln_b = column("ln_b", a["L0_gnn_ln_b"])
    c.gamma = column("gamma", a["L1_gnn_gamma"])
    c.beta = column("beta", a["L1_gnn_beta"])
    c.bl1 = column("bl1", a["L2_gnn_bl1"])
    br1 = column("br1", a["L2_gnn_br1"])
    c.bias1 = column("bias1", a["L2_gnn_bias1"])
    c.bl2 = column("bl2", a["L2_gnn_bl2"], C2)
    c.br2 = column("br2", a["L2_gnn_br2"], C2)
    c.bias2 = column("bias2", a["L2_gnn_bias2"], C2)
    c.blin = column("blin", a["L2_gnn_blin"])

    c.ident = sb("ident", [P, P])
    c.anti = sb("anti", [P, P])
    c.center = sb("center", [P, P])
    c.ones = sb("ones", [P, P], BF16)
    c.minus_half = sb("minus_half", [P, TILES])
    c.eps = sb("eps", [P, TILES])
    c.minus_one = sb("minus_one", [P, CHUNK])
    c.W1a, c.W1b, c.W2, c.Wc = (sb(n, [P, D]) for n in ("W1a", "W1b", "W2", "Wc"))
    c.Wsa, c.Wda, c.Wsd = (sb(n, [P, D]) for n in ("Wsa", "Wda", "Wsd"))
    c.Wlr1, c.Wlr2 = sb("Wlr1", [P, D]), sb("Wlr2", [P, C2])
    c.Wsrc, c.Wtgt, c.Wedge = sb("Wsrc", [P, D]), sb("Wtgt", [P, D]), sb("Wedge", [EF, D])
    c.S16, c.S1, c.S2 = sb("S16", [P, D]), sb("S1", [P, D]), sb("S2", [C2, D])
    c.blr1, c.blr2, c.node_bias2 = sb("blr1", [P, 1]), sb("blr2", [C2, 1]), sb("node_bias2", [C2, 1])
    c.node_bias1 = sb("node_bias1", [P, 1])
    c.b1_rows, c.b2_rows, c.bias_rows = (sb(n, [P, CHUNK], BF16) for n in ("b1_rows", "b2_rows", "bias_rows"))
    c.bl2_rows = sb("bl2_rows", [P, TILES * C2], BF16)
    c.src_cols = load("src_cols", [P, SLOT_TILES], a["src_cols"], I32)
    c.dst_gather_cols = load("dst_gather_cols", [P, SLOT_TILES], a["dst_gather_cols"], I32)
    c.last = [sb(f"last{o}", [P, SLOT_TILES]) for o in range(2)]
    c.map_index = [sb(f"map_index{o}", [P, SLOT_TILES], I32) for o in range(2)]
    c.out_index = sb("out_index", [P, SLOT_TILES], I32)
    c.payload = [sb(f"payload{o}", [P, SLOT_TILES], I32) for o in range(2)]

    raw = {n: load("raw_" + n, [P, D], src, room=temp) for n, src in (
        ("W1a", a["L0_gnn_W1"][0:D, :]), ("W1b", a["L0_gnn_W1"][D:2 * D, :]), ("W2", a["L0_gnn_W2"]), ("Wn", a["L3_gnn_W_node"]))}
    raw_edge = load("raw_edge", [P, EF], a["L3_gnn_W_edge"], room=temp)
    raw_b1 = load("raw_b1", [P, D], a["L0_gnn_b1"].partition_broadcast(P), room=temp)
    raw_b2 = load("raw_b2", [P, D], a["L0_gnn_b2"].partition_broadcast(P), room=temp)
    raw_bias = load("raw_bias", [P, D], a["L1_gnn_bias"].partition_broadcast(P), room=temp)
    raw_bl2 = load("raw_bl2", [P, C2], a["L2_gnn_bl2"].partition_broadcast(P), room=temp)
    vectors = {}
    for n, src, m in (("att_src", a["L1_gnn_att_src"], P), ("att_dst", a["L1_gnn_att_dst"], P),
                      ("att1", a["L2_gnn_att1"], P), ("att2", a["L2_gnn_att2"], C2)):
        vectors[n] = load("col_" + n, [m, 1], src.rearrange("h (c o) -> (h c) o", o=1), room=temp)
    for k, n in enumerate(("a_src", "a_tgt", "a_edge")):
        vectors[n] = temp("col_" + n, [P, 1])
        for h in range(4):
            loads.append((vectors[n][32 * h:32 * h + 32, :],
                          a["L3_gnn_a"][h:h + 1, 32 * k:32 * k + 32].rearrange("o c -> c o")))
    here = [load(f"here{o}", [P, SLOT_TILES], a["dst_cols"][o], I32, temp) for o in range(2)]
    after = [load(f"after{o}", [P, SLOT_TILES], a["dst_next_cols"][o], I32, temp) for o in range(2)]
    before = load("before", [P, SLOT_TILES], a["dst_prev_cols"], I32, temp)
    row_here = [load(f"row_here{o}", [SLOT_CHUNKS, CHUNK], a["dst_rows"][o], I32, temp) for o in range(2)]
    row_prev = [load(f"row_prev{o}", [SLOT_CHUNKS, CHUNK], a["dst_prev_rows"][o], I32, temp) for o in range(2)]
    first = temp("first", [P, SLOT_TILES])
    skip = [temp(f"skip{o}", [P, SLOT_TILES]) for o in range(2)]
    keep = [temp(f"keep_r{o}", [SLOT_CHUNKS, CHUNK]) for o in range(2)]
    S = {n: temp("S_" + n, [P, D]) for n in ("att_src", "att_dst", "a_src", "a_tgt", "a_edge")}
    same_head = {4: temp("same_head4", [P, D]), 8: temp("same_head8", [P, D]), 16: c.S16}
    stats, mean = temp("stats", [P, 7, 6]), temp("mean", [P, 7, 2])
    row_f = [temp(f"row_f{k}", [P, D]) for k in range(4)]
    row_rest = [temp(f"row_rest{k}", [P, D]) for k in range(4)]
    part = [temp(f"part{k}", [P, D], BF16) for k in range(4)]
    WT = temp("W_transposed", [P, D])
    map_rows = 125
    own_row = temp("own_row", [map_rows, N // map_rows, 2], I32)
    psum = c.psum

    with own:
        sem = lambda name: own.enter_context(nc.semaphore(name))
        loaded, made, masks, stored = sem("loaded"), sem("made"), sem("masks"), sem("prep_stored")
        worked, products, map_started = sem("worked"), sem("products"), sem("map_started")
        block = own.enter_context(nc.Block())

        @block.sync
        def _(sp):
            with nc.allow_non_contiguous_dma("a few vectors"):
                for dst, src in loads:
                    sp.dma_start(dst, src).then_inc(loaded, 16)
            sp.dma_start(dram.staged[E_STAGED:E_PAD, :], a["x"][0:E_PAD - E_STAGED, :]).then_inc(stored, 16)
            sp.wait_ge(masks, 2)
            for o in range(2):
                sp.dma_start(dram.keep[o], keep[o][:, :]).then_inc(stored, 16)
            sp.wait_ge(stored, 48)

        @block.gpsimd
        def _(pool):
            pool.iota(own_row[:, :, :], pattern=[[1, N // map_rows], [0, 2]], base=0,
                      channel_multiplier=N // map_rows).then_inc(made, 1)
            pool.iota(c.payload[0][:, :], pattern=[[P, SLOT_TILES]], base=N_PAD, channel_multiplier=1).then_inc(made, 1)
            pool.iota(c.payload[1][:, :], pattern=[[-P, SLOT_TILES]], base=N_PAD + E_PAD - 1,
                      channel_multiplier=-1).then_inc(made, 1)
            pool.wait_ge(made, 1)
            pool.dma_start(dram.slot_map.rearrange("(p n) o -> p (n o)", p=map_rows),
                           own_row[:, :, :].rearrange("p n o -> p (n o)")).then_inc(map_started, 16)
            for t, value in ((c.ident, 0.0), (c.anti, 0.0), (same_head[4], 1.0), (same_head[8], 1.0),
                             (same_head[16], 1.0), (c.minus_half, -0.5), (c.eps, LN_EPS), (c.minus_one, -1.0), (c.ones, 1.0),
                             (c.b1_rows, 0.0), (c.b2_rows, 0.0), (c.bias_rows, 0.0), (c.bl2_rows, 0.0)):
                pool.memset(t[:, :], value).then_inc(made, 1)
            pool.wait_ge(made, 16)
            pool.affine_select(out=c.ident[:, :], in_=c.ident[:, :], compare_op=ALU.not_equal, fill=1.0, base=0,
                               pattern=[[-1, P]], channel_multiplier=1).then_inc(made, 1)
            pool.affine_select(out=c.anti[:, :], in_=c.anti[:, :], compare_op=ALU.not_equal, fill=1.0, base=-(P - 1),
                               pattern=[[1, P]], channel_multiplier=1).then_inc(made, 1)
            for h, t in same_head.items():
                pool.affine_select(out=t[:, :], in_=t[:, :], compare_op=ALU.is_ge, fill=0.0, base=0,
                                   pattern=[[-(D // h), h], [0, D // h]], channel_multiplier=1).then_inc(made, 1)
            pool.wait_ge(made, 21)
            for h, t in same_head.items():
                pool.affine_select(out=t[:, :], in_=t[:, :], compare_op=ALU.is_ge, fill=0.0, base=D // h - 1,
                                   pattern=[[D // h, h], [0, D // h]], channel_multiplier=-1).then_inc(made, 1)
            pool.wait_ge(made, 24)
            pool.wait_ge(map_started, 16)

        @block.vector
        def _(v):
            v.wait_ge(loaded, 16 * len(loads))
            for o in range(2):
                v.tensor_tensor(keep[o][:, :], row_here[o][:, :], row_prev[o][:, :], ALU.is_equal).then_inc(masks, 1)
            v.wait_ge(made, 24)
            v.tensor_scalar(c.center[:, :], c.ident[:, :], -1.0 / D, None, ALU.add).then_inc(worked, 1)
            for n in S:
                v.tensor_scalar(S[n][:, :], same_head[4][:, :], vectors[n][:, 0:1], None, ALU.mult).then_inc(worked, 1)
            v.tensor_scalar(c.S1[:, :], same_head[8][:, :], vectors["att1"][:, 0:1], None, ALU.mult).then_inc(worked, 1)
            v.tensor_copy(c.S2[:, :], vectors["att2"][:, 0:1].broadcast_to([C2, D])).then_inc(worked, 1)
            v.tensor_tensor(c.Wlr1[:, :], c.Wl1[:, :], c.Wr1[:, :], ALU.add).then_inc(worked, 1)
            v.tensor_tensor(c.Wlr2[:, :], c.Wl2[:, :], c.Wr2[:, :], ALU.add).then_inc(worked, 1)
            v.tensor_tensor(c.blr1[:, :], c.bl1[:, :], br1[:, :], ALU.add).then_inc(worked, 1)
            v.tensor_tensor(c.blr2[:, :], c.bl2[:, :], c.br2[:, :], ALU.add).then_inc(worked, 1)
            v.tensor_tensor(c.node_bias1[:, :], c.bl1[:, :], c.bias1[:, :], ALU.add).then_inc(worked, 1)
            v.tensor_tensor(c.node_bias2[:, :], c.bl2[:, :], c.bias2[:, :], ALU.add).then_inc(worked, 1)
            for o in range(2):
                v.tensor_tensor(c.last[o][:, :], here[o][:, :], after[o][:, :], ALU.not_equal).then_inc(worked, 1)
            v.tensor_tensor(first[:, :], here[0][:, :], before[:, :], ALU.not_equal).then_inc(worked, 1)
            v.tensor_copy(row_f[3][:, 0:C2], raw_bl2[:, :]).then_inc(worked, 1)
            to_center = ((raw["W1a"], c.W1a), (raw["W1b"], c.W1b), (raw["W2"], c.W2), (c.W, c.Wc),
                         (raw_b1, row_f[0]), (raw_b2, row_f[1]), (raw_bias, row_f[2]))
            for k, (source, _) in enumerate(to_center):
                v.bn_stats(stats[:, k, :], source[:, :]).then_inc(worked, 1)
            n = 18 + len(to_center)
            v.wait_ge(worked, n)
            v.tensor_scalar(skip[0][:, :], c.last[0][:, :], -1.0 * OUT_OF_RANGE, 1.0 * OUT_OF_RANGE, ALU.mult,
                            ALU.add).then_inc(worked, 1)
            v.tensor_scalar(skip[1][:, :], first[:, :], -1.0 * OUT_OF_RANGE, 1.0 * OUT_OF_RANGE + 1.0, ALU.mult,
                            ALU.add).then_inc(worked, 1)
            for k in range(len(to_center)):
                v.bn_aggr(mean[:, k, :], stats[:, k, :]).then_inc(worked, 1)
            n += 9
            v.wait_ge(worked, n)
            for o in range(2):
                v.scalar_tensor_tensor(out=c.map_index[o][:, :], in0=here[0][:, :], scalar=2.0, in1=skip[o][:, :],
                                       op0=ALU.mult, op1=ALU.add).then_inc(worked, 1)
            v.tensor_tensor(c.out_index[:, :], here[0][:, :], skip[0][:, :], ALU.add).then_inc(worked, 1)
            for k, (source, out) in enumerate(to_center):
                v.tensor_scalar(out[:, :], source[:, :], mean[:, k, 0:1], None, ALU.subtract).then_inc(worked, 1)
            n += 10
            targets = ((c.b1_rows, D), (c.b2_rows, D), (c.bias_rows, D), (c.bl2_rows, C2))
            rest = row_f
            for level in range(3):
                v.wait_ge(worked, n)
                for k, (_, m) in enumerate(targets):
                    v.tensor_copy(part[k][:, 0:m], rest[k][:, 0:m]).then_inc(worked, 1)
                n += len(targets)
                v.wait_ge(worked, n)
                p = 32 * level
                for k, (out, m) in enumerate(targets):
                    v.tensor_copy(tiles_of(out[p:p + 1, :]), part[k][p:p + 1, 0:m].unsqueeze(1).broadcast_to([1, TILES, m]))\
                     .then_inc(worked, 1)
                n += len(targets)
                if level < 2:
                    following = row_rest if level == 0 else row_f
                    for k, (_, m) in enumerate(targets):
                        v.tensor_tensor(following[k][:, 0:m], rest[k][:, 0:m], part[k][:, 0:m], ALU.subtract)\
                         .then_inc(worked, 1)
                    n += len(targets)
                    rest = following
            v.wait_ge(products, 1)
            v.tensor_copy(WT[:, :], psum[:, 0, 0:D]).then_inc(worked, 1)
            n += 1
            v.wait_ge(products, 2)
            for b, out in ((1, c.Wsa), (2, c.Wda), (3, c.Wsrc), (4, c.Wtgt)):
                v.tensor_copy(out[:, :], psum[:, b, 0:D]).then_inc(worked, 1)
            v.tensor_copy(c.Wedge[:, :], psum[0:EF, 5, 0:D]).then_inc(worked, 1)
            n += 5
            v.wait_ge(worked, n)
            v.tensor_tensor(c.Wsd[:, :], c.Wsa[:, :], c.Wda[:, :], ALU.add).then_inc(worked, 1)
            v.wait_ge(worked, n + 1)

        @block.tensor
        def _(pe):
            pe.wait_ge(loaded, 16 * len(loads))
            pe.wait_ge(made, 24)
            pe.transpose(psum[:, 0, 0:D], c.W[:, :], c.ident[:, :]).then_inc(products, 1)
            pe.wait_ge(worked, 25 + 9 + 10 + 4 * 8 + 1)
            for b, lhs, rhs, m in ((1, WT, S["att_src"], D), (2, WT, S["att_dst"], D), (3, raw["Wn"], S["a_src"], D),
                                   (4, raw["Wn"], S["a_tgt"], D), (5, raw_edge, S["a_edge"], EF)):
                ins = pe.matmul(psum[0:m, b, 0:D], lhs[:, :], rhs[:, :], start=True, stop=True)
            ins.then_inc(products, 1)



def chain0(slots, tail_T):
    return [("PE", "h0")] + norm_chain("sq0", "z0") + \
        [("PE", "z0T"), ("ACT", "relu0"), ("PE", "y0")] + norm_chain("sq1", "x1", slots) + \
        [("ACT", "store_x1")] + ([("PE", "x1T"), ("DVE", "x1T")] if tail_T else [])


def chain1(slots, tail_T):
    return [("PE", "h1")] + norm_chain("sq2", "z1") + \
        [("PE", "z1T"), ("ACT", "gelu1")] + ([] if slots else [("DVE", "y1T")]) + \
        [("PE", "y1")] + norm_chain("sq3", "x2", slots) + \
        [("ACT", "store_x2")] + ([("PE", "x2T"), ("DVE", "x2T")] if tail_T else [])


def chain2a(slots):
    return ([] if slots else [("PE", "z2")]) + \
        [("ACT", "exp2"), ("DVE", "h2_em1"), ("DVE", "h2"), ("PE", "xl"), ("ACT", "xl"),
         ("ACT", "store_xl")]


def chain2b(slots):
    return ([] if slots else [("PE", "z3")]) + \
        [("ACT", "exp3"), ("DVE", "h3_em1"), ("DVE", "h3"), ("PE", "z4"), ("ACT", "exp4"),
         ("DVE", "h4_em1"), ("DVE", "h4"), ("POOL" if slots else "DVE", "y2T"), ("PE", "y2")] + \
        norm_chain("sq4", "x3", slots) + [("ACT", "store_x3")]


def pe_update(pe, g, u, i, step):
    c = g.c
    if step == "h0":
        if g.slots:
            pe.wait_ge(*g.DVE.done(u, i, "agg"))
            pe_rows(pe, g, u, g.A, [(g.xT[u], c.W1b[:, :]), (g.agg[u], c.W1a[:, :])], c.b1_rows)
        else:
            pe.wait_ge(*g.DVE.before(u, i))
            pe.wait_ge(g.x_loaded[u], i * 16 + 16)
            pe_rows(pe, g, u, g.A, [(g.xT[u], c.W1b[:, :])], c.b1_rows)
    if step == "z0T":
        pe.wait_ge(*g.DVE.done(u, i, "z0"))
        pe_transposes(pe, g, u, g.B, g.z[u])
    if step == "y0":
        pe.wait_ge(*g.ACT.done(u, i, "relu0"))
        pe_rows(pe, g, u, g.A, [(g.act_T[u], c.W2[:, :]), (g.xT[u], c.center[:, :])], c.b2_rows)
    if step == "x1T":
        pe.wait_ge(*g.DVE.done(u, i, "x1"))
        pe_transposes(pe, g, u, g.B, g.x1[u])
    if step == "h1":
        if g.slots:
            pe.wait_ge(*g.DVE.done(u, i, "agg"))
            pe_rows(pe, g, u, g.A, [(g.agg[u], c.center[:, :])], c.bias_rows)
        else:
            pe.wait_ge(*g.DVE.done(u, i, "x1T"))
            pe_rows(pe, g, u, g.A, [(g.xT1[u], c.Wc[:, :])], c.bias_rows)
    if step == "z1T":
        pe.wait_ge(*g.DVE.done(u, i, "z1"))
        pe_transposes(pe, g, u, g.B, g.z[u])
    if step == "y1":
        if g.slots:
            pe.wait_ge(*g.ACT.done(u, i, "gelu1"))
            pe_rows(pe, g, u, g.A, [(g.act_T[u], c.center[:, :]), (g.xT1[u], c.center[:, :])])
        else:
            pe.wait_ge(*g.DVE.done(u, i, "y1T"))
            pe_rows(pe, g, u, g.A, [(g.yT[u], c.center[:, :])])
    if step == "x2T":
        pe.wait_ge(*g.DVE.done(u, i, "x2"))
        pe_transposes(pe, g, u, g.B, g.x2[u])
    if step == "z2":
        pe.wait_ge(*g.DVE.done(u, i, "x2T"))
        pe.matmul(g.A(u), c.Wl1[:, :], g.xT2[u][:, :], start=True, stop=True).then_inc(g.pe_out[u], 1)
    if step == "xl":
        pe.wait_ge(*g.DVE.done(u, i, "h2"))
        pe_rows(pe, g, u, g.B, [(g.act_T[u], c.Wl2[:, :])], c.bl2_rows, C2)
    if step == "z3":
        pe.wait_ge(*g.ACT.done(u, i, "xl"))
        pe.matmul(g.A(u)[0:C2, :], c.Wl2[:, :], g.act_T[u][:, :], start=True, stop=True).then_inc(g.pe_out[u], 1)
    if step == "z4":
        pe.wait_ge(*(g.DVE.done(u, i, "agg") if g.slots else g.ACT.done(u, i, "xl")))
        pe.wait_ge(*g.DVE.done(u, i, "h3"))
        pe.matmul(g.B(u), c.Wlin[:, :], g.act_T[u][0:C2, :], start=True, stop=True).then_inc(g.pe_out[u], 1)
    if step == "y2":
        pe.wait_ge(*(g.POOL if g.slots else g.DVE).done(u, i, "y2T"))
        pe_rows(pe, g, u, g.A, [(g.yT[u], c.center[:, :])])


def act_update(act, g, u, i, step):
    c = g.c
    rows = {"sq0": "h0", "sq1": "y0", "sq2": "h1", "sq3": "y1", "sq4": "y2"}
    if step in rows:
        act.wait_ge(*g.PE.done(u, i, rows[step]))
        act_squares(act, g, u, tiles_of(g.A(u)))
    if step == "relu0":
        act.wait_ge(*g.PE.done(u, i, "z0T"))
        act_copy(act, g, u, g.act_T[u][:, :], g.B(u), ACT.Relu, c.ln_b[:, 0:1], c.ln_g[:, 0:1])
    if step == "gelu1":
        act.wait_ge(*g.PE.done(u, i, "z1T"))
        act_copy(act, g, u, g.act_T[u][:, :], g.B(u), ACT.Gelu, c.beta[:, 0:1], c.gamma[:, 0:1])
    if step == "exp2":
        if g.slots:
            act.wait_ge(*g.DVE.done(u, i, "agg"))
            act_copy(act, g, u, g.expz[u][:, :], g.agg[u][:, :], ACT.Exp, c.bias1[:, 0:1])
        else:
            act.wait_ge(*g.PE.done(u, i, "z2"))
            act_copy(act, g, u, g.expz[u][:, :], g.A(u), ACT.Exp, c.node_bias1[:, 0:1])
    if step == "xl":
        act.wait_ge(g.xl_stored[u], i * 16 + 16)
        act.wait_ge(*g.PE.done(u, i, "xl"))
        act_copy(act, g, u, g.xl[u][:, :, :], tiles_of(g.B(u)[:, 0:TILES * C2]))
    if step == "exp3":
        if g.slots:
            act.wait_ge(*g.DVE.done(u, i, "agg"))
            act_copy(act, g, u, g.expz[u][0:C2, :], g.agg[u][0:C2, :], ACT.Exp, c.bias2[:, 0:1])
        else:
            act.wait_ge(*g.PE.done(u, i, "z3"))
            act_copy(act, g, u, g.expz[u][0:C2, :], g.A(u)[0:C2, :], ACT.Exp, c.node_bias2[:, 0:1])
    if step == "exp4":
        act.wait_ge(*g.PE.done(u, i, "z4"))
        act_copy(act, g, u, g.expz[u][:, :], g.B(u), ACT.Exp, c.blin[:, 0:1])
    if step == "store_x1":
        act.wait_ge(*g.DVE.done(u, i, "x1"))
        act.dma_start(g.rows_in_table(c.dram.x1, i, u), g.x1[u][:, :, :]).then_inc(g.x1_stored[u], 16)
    if step == "store_x2":
        act.wait_ge(*g.DVE.done(u, i, "x2"))
        act.dma_start(g.rows_in_table(c.dram.x2, i, u), g.x2[u][:, :, :]).then_inc(g.x2_stored[u], 16)
    if step == "store_xl":
        act.wait_ge(*g.ACT.done(u, i, "xl"))
        act.dma_start(g.rows_in_table(c.dram.xl2, i, u), g.xl[u][:, :, :]).then_inc(g.xl_stored[u], 16)
    if step == "store_x3":
        act.wait_ge(*g.DVE.done(u, i, "x3"))
        act.dma_start(g.rows_in_table(c.dram.x3, i, u), g.x3[u][:, :, :]).then_inc(g.x3_stored[u], 16)


def dve_update(v, g, u, i, step):
    c = g.c
    if step == "z0":
        v.wait_ge(*g.POOL.done(u, i, "sq0_rstd"))
        dve_scale_rows(v, g, u, tiles_of(g.A(u)), g.z[u])
    if step == "z1":
        v.wait_ge(*g.POOL.done(u, i, "sq2_rstd"))
        dve_scale_rows(v, g, u, tiles_of(g.A(u)), g.z[u])
    if step == "x1":
        v.wait_ge((g.x1_stored if g.slots else g.x4_stored)[u], i * 16 + 16)
        v.wait_ge(*g.POOL.done(u, i, "sq1_rstd"))
        dve_scale_rows(v, g, u, tiles_of(g.A(u)), g.x1[u])
    if step == "x2":
        v.wait_ge(g.x2_stored[u], i * 16 + 16)
        v.wait_ge(*g.POOL.done(u, i, "sq3_rstd"))
        dve_scale_rows(v, g, u, tiles_of(g.A(u)), g.x2[u])
    if step == "x3":
        v.wait_ge(g.x3_stored[u], i * 16 + 16)
        v.wait_ge(*g.POOL.done(u, i, "sq4_rstd"))
        dve_scale_rows(v, g, u, tiles_of(g.A(u)), g.x3[u])
    if step in ("x1T", "x2T"):
        v.wait_ge(*g.PE.done(u, i, step))
        v.tensor_copy((g.xT1 if step == "x1T" else g.xT2)[u][:, :], g.B(u)).then_inc(g.dve_out[u], 1)
    if step == "y1T":
        v.wait_ge(*g.ACT.done(u, i, "gelu1"))
        v.tensor_tensor(g.yT[u][:, :], g.act_T[u][:, :], g.xT1[u][:, :], ALU.add).then_inc(g.dve_out[u], 1)
    m = C2 if step.startswith("h3") else P
    exp_step = {"h2_em1": "exp2", "h3_em1": "exp3", "h4_em1": "exp4"}
    if step in exp_step:
        v.wait_ge(*g.ACT.done(u, i, exp_step[step]))
        v.tensor_scalar(g.expz[u][0:m, :], g.expz[u][0:m, :], 1.0, -1.0, ALU.min, ALU.add).then_inc(g.dve_out[u], 1)
    if step in ("h2", "h3", "h4"):
        if step == "h4":
            source, bias = g.B(u), c.blin
        elif g.slots:
            source, bias = g.agg[u][0:m, :], {"h2": c.bias1, "h3": c.bias2}[step]
        else:
            source, bias = g.A(u)[0:m, :], {"h2": c.node_bias1, "h3": c.node_bias2}[step]
        v.wait_ge(*g.DVE.done(u, i, step + "_em1"))
        v.scalar_tensor_tensor(out=g.act_T[u][0:m, :], in0=source, scalar=bias[:, 0:1], in1=g.expz[u][0:m, :],
                               op0=ALU.add, op1=ALU.max).then_inc(g.dve_out[u], 1)
    if step == "y2T":
        v.wait_ge(*g.DVE.done(u, i, "h4"))
        v.tensor_tensor(g.yT[u][:, :], g.act_T[u][:, :], g.res2(u), ALU.add).then_inc(g.dve_out[u], 1)


def pool_update(pool, g, u, i, step):
    squares, _, what = step.partition("_")
    if what == "eps":
        pool.wait_ge(*g.ACT.done(u, i, squares))
        pool.tensor_tensor(g.variance[u][:, :], g.mean_square[u][:, :], g.c.eps[:, :], ALU.add).then_inc(g.pool_out[u], 1)
    flagged = squares + "_pow" in g.POOL.names
    if what == "pow" or (what == "rstd" and not flagged):
        pool.wait_ge(*g.POOL.done(u, i, squares + "_eps"))
        out = g.raw[u] if flagged else g.rstd[u]
        pool.tensor_tensor(out[:, :], g.variance[u][:, :], g.c.minus_half[:, :], ALU.pow).then_inc(g.pool_out[u], 1)
    if what == "rstd" and flagged:
        pool.wait_ge(*g.POOL.done(u, i, squares + "_pow"))
        flags = g.last_flags[:, ds((i * STREAMS + u) * TILES, TILES)]
        pool.tensor_tensor(g.rstd[u][:, :], g.raw[u][:, :], flags, ALU.mult).then_inc(g.pool_out[u], 1)



def node_pass(nc, a, c, dram):
    with ExitStack() as ctx:
        g = Named(c)
        phase_tiles(ctx, nc, g, "node", NODE_STREAMS, primed=1)
        g.A = g.B = lambda u: c.psum[:, u, :]
        gathers = [(0, t) for t in range(SIDE_TILES)]
        scatters = [(k, t) for t in range(SIDE_TILES) for k in (1, 2)]
        plan(g, chain0(False, True) + chain1(False, True) + chain2a(False) + chain2b(False) +
             norm_chain("sq5", "x4") + [("ACT", "store_x4")], "node", gathers + scatters)
        middle = [n for n, item in enumerate(g.order) if item[3] == scatters[4]][0]
        g.order = [(-1, 0, "POOL", "side_index")] + g.order[:middle] + [(-1, 0, "ACT", "stage")] + g.order[middle:] + \
            [(-1, 0, "POOL", "side_end")]
        g.xT = g.many("xT", [P, CHUNK])
        g.z = g.many("z", [P, TILES, D])
        g.act_T = g.many("act_T", [P, CHUNK])
        g.yT = g.act_T
        g.expz = [t[:, :, :].rearrange("p t n -> p (t n)") for t in g.z]
        g.x1 = g.many("x1", [P, TILES, D])
        g.x2 = g.many("x2", [P, TILES, D])
        g.x3 = g.many("x3", [P, TILES, D])
        x4 = g.x1
        g.xl = g.many("xl", [P, TILES, C2])
        g.xT1 = g.many("xT1", [P, CHUNK])
        g.xT2 = g.xT1
        g.res2 = lambda u: g.xT2[u][:, :]
        g.x_loaded = g.sems("x_loaded")
        g.x1_stored, g.x2_stored, g.x3_stored = g.sems("x1_stored"), g.sems("x2_stored"), g.sems("x3_stored")
        g.xl_stored, g.x4_stored = g.sems("xl_stored"), g.sems("x4_stored")
        g.rows_in_table = lambda table, i, u: table[ds(i * NODES_PER_ITER + u * CHUNK, CHUNK), :]\
            .rearrange("(t p) f -> p t f", p=P)

        gathered = g.sb("gathered", [P, SIDE_TILES, D])
        index = [g.sb(f"index{k}", [P, SIDE_TILES], I32) for k in range(3)]
        value = [g.sb(f"value{k}", [P, SIDE_TILES], I32) for k in range(2)]
        gathers_done, staged = g.sem("gathers_done"), g.sem("staged")
        scattered = [g.sem(f"scattered{k}") for k in range(2)]
        index_ready = g.sem("index_ready")
        ctx.callback(end_phase, nc, g.all_sems)
        block = ctx.enter_context(nc.Block())

        @block.sync
        def _(sp):
            def load(i):
                for u in g.streams:
                    if not isinstance(i, int):
                        sp.wait_ge(*g.PE.done(u, i - 1, "y0"))
                    sp.dma_start(g.xT[u][:, :], a["x_T"][:, ds(i * NODES_PER_ITER + u * CHUNK, CHUNK)]).then_inc(g.x_loaded[u], 16)

            load(0)
            with sp.Fori(1, NODE_ITERS) as i:
                load(i)

        @block.scalar
        def _(act):
            def stage(i):
                act.wait_ge(gathers_done, (i + 1) * 16 * SIDE_TILES)
                act.dma_start(dram.staged[ds(i * (SIDE_TILES * P), SIDE_TILES * P), :].rearrange("(t p) f -> p t f", p=P),
                              gathered[:, :, :]).then_inc(staged, 16)

            def run(i, part):
                for u, i, step in turns(g, "ACT", i, part):
                    if step == "stage":
                        stage(i)
                    else:
                        act_update(act, g, u, i, step)
                    if step == "sq5":
                        act.wait_ge(*g.DVE.done(u, i, "x3"))
                        act_squares(act, g, u, g.x3[u])
                    if step == "store_x4":
                        act.wait_ge(*g.DVE.done(u, i, "x4"))
                        act.dma_start(g.rows_in_table(a["out"], i, u), x4[u][:, :, :]).then_inc(g.x4_stored[u], 16)

            run(0, "in")
            with act.Fori(1, NODE_ITERS) as i:
                run(i, "all")
            run(NODE_ITERS, "out")
            for stored in (g.x1_stored, g.x2_stored, g.xl_stored, g.x3_stored, g.x4_stored):
                for u in g.streams:
                    act.wait_ge(stored[u], 16 * NODE_ITERS + 16)
            act.wait_ge(staged, 16 * NODE_ITERS + 16)

        @block.tensor
        def _(pe):
            def run(i, part):
                for u, i, step in turns(g, "PE", i, part):
                    pe_update(pe, g, u, i, step)

            run(0, "in")
            with pe.Fori(1, NODE_ITERS) as i:
                run(i, "all")
            run(NODE_ITERS, "out")

        @block.vector
        def _(v):
            for u in g.streams:
                for k, stored in enumerate((g.x1_stored, g.x2_stored, g.x3_stored, g.x4_stored)):
                    v.memset(g.raw[u][:, k:k + 1], 0.0).then_inc(stored[u], 16)
                v.memset(g.variance[u][:, 0:1], 0.0).then_inc(g.xl_stored[u], 16)
                v.memset(g.variance[u][:, 1:], 0.0).then_inc(g.dve_out[u], 1)

            def run(i, part):
                for u, i, step in turns(g, "DVE", i, part):
                    dve_update(v, g, u, i, step)
                    if step == "x4":
                        v.wait_ge(g.x1_stored[u], i * 16 + 32)
                        v.wait_ge(*g.POOL.done(u, i, "sq5_rstd"))
                        dve_scale_rows(v, g, u, g.x3[u][:, :, :], x4[u])

            run(0, "in")
            with v.Fori(1, NODE_ITERS) as i:
                run(i, "all")
            run(NODE_ITERS, "out")

        @block.gpsimd
        def _(pool):
            lists = (c.src_cols, c.map_index[0], c.map_index[1])
            pool.memset(index[0][:, :], 0).then_inc(staged, 16)

            def side_work(i, step):
                if step == "side_index":
                    cols = ds(i * SIDE_TILES, SIDE_TILES)
                    pool.wait_ge(staged, i * 16 + 16)
                    for k in range(3):
                        pool.tensor_copy(index[k][:, :], lists[k][:, cols]).then_inc(index_ready, 1)
                    for k in range(2):
                        pool.tensor_copy(value[k][:, :], c.payload[k][:, cols]).then_inc(index_ready, 1)
                    pool.wait_ge(index_ready, len(lists) + len(value))
                elif step == "side_end":
                    pool.sem_clear(index_ready)
                    for k in range(2):
                        pool.wait_ge(scattered[k], (i + 1) * 16 * SIDE_TILES)
                elif step[0] == 0:
                    t = step[1]
                    pool.indirect_dma_start(gathered[:, t, :], None, a["x"],
                                            at_index(index[0][:, t:t + 1], 0)).then_inc(gathers_done, 16)
                else:
                    k, t = step
                    pool.indirect_dma_start(dram.slot_map_flat, at_index(index[k][:, t:t + 1], 0),
                                            value[k - 1][:, t:t + 1], None, bounds_check=2 * N - 1,
                                            oob_is_err=False).then_inc(scattered[k - 1], 16)

            def run(i, part):
                for u, i, step in turns(g, "POOL", i, part):
                    if u >= 0:
                        pool_update(pool, g, u, i, step)
                    else:
                        side_work(i, step)

            run(0, "in")
            with pool.Fori(1, NODE_ITERS) as i:
                run(i, "all")
            run(NODE_ITERS, "out")



HEADS = {"0": 16, "1": 4, "2a": 8, "2b": 1, "3": 4}
ORDER = {"0": 0, "1": 1, "2a": 0, "2b": 1, "3": 0}
ITER_TILES = PER_ITER // P


def slot_chain(layer):
    own = layer in ("1", "2a", "2b")
    transposes = [("PE", "srcT")] + ([] if layer == "2b" else [("PE", "dstT")]) + [("ACT", "srcT")]
    front = {
        "0": [("ACT", "dstT"), ("PE", "k"), ("PE", "q"), ("ACT", "k"), ("PE", "e0"), ("DVE", "qk"), ("ACT", "e0"),
              ("PE", "e1"), ("DVE", "qke"), ("ACT", "e1"), ("PE", "l"), ("ACT", "l"), ("PE", "v")],
        "1": [("DVE", "dst"), ("PE", "l"), ("PE", "ls"), ("ACT", "l"), ("ACT", "ls"), ("DVE", "l"), ("DVE", "ls"),
              ("PE", "v"), ("PE", "o"), ("DVE", "lm")],
        "2a": [("DVE", "dst"), ("PE", "z"), ("PE", "zo"), ("ACT", "z"), ("ACT", "zo"), ("DVE", "z"), ("DVE", "zo"),
               ("PE", "l"), ("PE", "ls"), ("ACT", "l"), ("ACT", "ls"), ("PE", "v"), ("PE", "o"), ("DVE", "lm")],
        "2b": [("DVE", "dst"), ("PE", "z"), ("PE", "zo"), ("ACT", "z"), ("ACT", "zo"), ("DVE", "z"), ("DVE", "zo"),
               ("PE", "l"), ("PE", "ls"), ("ACT", "l"), ("ACT", "ls"), ("PE", "o"), ("DVE", "lm")],
        "3": [("DVE", "dst"), ("DVE", "deg"), ("PE", "l"), ("ACT", "l"), ("DVE", "l"), ("PE", "v"), ("DVE", "lm")]}[layer]
    softmax = [("DVE", "fc"), ("DVE", "f"), ("POOL", "shift"), ("DVE", "e_p")] + {"1": [("DVE", "e_s")], "2a": [("DVE", "e_s")], "2b": [("POOL", "e_s")]}.get(layer, []) + \
        [("DVE", "e_c"), ("ACT", "exp")] + {"0": [("DVE", "v")], "3": [("ACT", "exps")]}.get(layer, []) + \
        [("DVE", "den"), ("DVE", "pv"), ("PE", "tot"), ("DVE", "num")] + \
        ([("DVE", "sv"), ("POOL", "ns")] if own else []) + \
        {"0": [("DVE", "tot")], "1": [("DVE", "tot")], "3": [("DVE", "degE"), ("DVE", "rest"), ("DVE", "tot")]}\
        .get(layer, []) + [("DVE", "rec"), ("ACT", "rs"), ("PE", "rB"), ("DVE", "agg")]
    back = {"0": chain0(True, False), "1": chain1(True, False), "2a": chain2a(True) + [("ACT", "store_T")],
            "2b": chain2b(True), "3": [("PE", "y3")] + norm_chain("sq5", "x4") + [("POOL", "scatter")]}[layer]
    side = [("POOL", "index")] + [("POOL", f"gather{t}") for t in range(TILES)]
    if layer == "0":
        side += [("POOL", "dst_index")] + [("POOL", f"dst_gather{t}") for t in range(TILES)] + [("POOL", "keep_map")]
    return [("ACT", "neg")] + ([("DVE", "mask")] if layer == "2b" else []) + transposes + front + softmax + back + side


def slot_pass(nc, a, c, dram, layer):
    H = HEADS[layer]
    order = ORDER[layer]
    M = C2 if layer == "2b" else P
    own = layer in ("1", "2a", "2b")
    gatv2 = layer in ("2a", "2b")
    final = SLOT_ITERS - 1
    with ExitStack() as ctx:
        g = Named(c, True, c.last[order])
        phase_tiles(ctx, nc, g, f"slot{layer}", STREAMS, primed=5)
        A, B = g.A, g.B
        plan(g, slot_chain(layer), layer)

        src_width = C2 if layer == "2b" else D
        src_rows = g.many("src_rows", [P, TILES, D])
        dst_rows = g.many("dst_rows", [P, TILES, D])
        keep, neg = g.many("keep", [P, CHUNK]), g.many("neg", [P, CHUNK])
        xs, xd = g.many("xs", [P, CHUNK]), g.many("xd", [P, CHUNK])
        t1, t2 = g.many("t1", [P, CHUNK]), g.many("t2", [P, CHUNK])
        logit_rows = g.many("logit", [P, TILES, D])
        logit = [t[:, :, :].rearrange("p t n -> p (t n)") for t in logit_rows]
        fmax = g.many("fmax", [P, CHUNK + 1])
        expo = g.many("expo", [P, 3, CHUNK])
        den, num = g.many("den", [P, CHUNK]), g.many("num", [P, CHUNK])
        new = g.many("new", [P, TILES, D])
        extra = g.many("extra", [P, CHUNK])
        edge = g.many("edge", [EF, CHUNK]) if layer in ("0", "3") else None
        h2_before = g.many("h2_before", [P, CHUNK]) if layer == "2b" else None
        g.xl = g.many("xl", [P, TILES, C2]) if layer == "2a" else None
        small, recip = g.many("small", [P, TILES, H]), g.many("recip", [P, TILES, H])
        count = g.many("count", [P, TILES])
        g.agg = g.yT = t1
        g.act_T = t2
        g.z = logit_rows
        g.expz = [t[:, 1, :] for t in expo]
        g.x1 = g.x2 = g.x3 = new
        g.xT = g.xT1 = xd
        index, side_index = g.many("index", [P, TILES], I32), g.many("side_index", [P, TILES], I32)
        map_rows = g.many("map_rows", [P, TILES, 2], I32)

        src_ready, dst_ready, keep_ready = g.sems("src_ready"), g.sems("dst_ready"), g.sems("keep_ready")
        edge_ready, g.res_ready = g.sems("edge_ready"), g.sems("res_ready")
        stored, stored_T = g.sems("stored"), g.sems("stored_T")
        g.x1_stored = g.x2_stored = g.x3_stored = g.xl_stored = stored
        index_ready, side_index_ready = g.sems("index_ready"), g.sems("side_index_ready")
        map_ready, map_kept, cleared = g.sems("map_ready"), g.sems("map_kept"), g.sem("cleared")

        g.res2 = lambda u: dst_rows[u][:, :, :].rearrange("p t n -> p (t n)")[:, ::-1]
        start = lambda i, u: i * PER_ITER + u * CHUNK
        mirrored = lambda i, u: i * -PER_ITER + (E_PAD - (u + 1) * CHUNK)
        table = {"1": dram.x1, "2a": dram.x2, "2b": dram.xl2, "3": dram.x3}.get(layer)

        def rows_of(array, first):
            return array[ds(first, CHUNK), :].rearrange("(t p) f -> p t f", p=P)

        g.rows_in_table = lambda array, i, u: rows_of(array, start(i, u) + N_PAD)
        ctx.callback(end_phase, nc, g.all_sems)
        block = ctx.enter_context(nc.Block())

        @block.sync
        def _(sp):
            def load(i, first):
                for u in g.streams:
                    if not first:
                        sp.wait_ge(*g.DVE.done(u, i - 1, "e_c"))
                    sp.dma_start(keep[u][:, :], dram.keep_flat[order][ds(start(i, u), CHUNK)].partition_broadcast(P))\
                      .then_inc(keep_ready[u], 16)
                    if layer == "0":
                        sp.dma_start(src_rows[u][:, :, :], rows_of(dram.staged, start(i, u))).then_inc(src_ready[u], 16)
                    elif layer == "2b":
                        sp.dma_start(h2_before[u][:, :], dram.h2_T[:, ds(mirrored(i, u), CHUNK)]).then_inc(dst_ready[u], 16)
                    else:
                        sp.dma_start(dst_rows[u][:, :, :], rows_of(table, mirrored(i, u) + N_PAD)).then_inc(dst_ready[u], 16)
                    if layer in ("0", "3"):
                        sp.dma_start(edge[u][:, :], a["edge_T"][:, ds(start(i, u), CHUNK)]).then_inc(edge_ready[u], 16)
                    if layer == "2b":
                        if not first:
                            sp.wait_ge(*g.POOL.done(u, i - 1, "y2T"))
                        sp.dma_start(dst_rows[u][:, :, :].rearrange("p t n -> p (t n)"),
                                     dram.x2_T[:, ds(mirrored(i, u), CHUNK)]).then_inc(g.res_ready[u], 16)

            load(0, True)
            with sp.Fori(1, SLOT_ITERS) as i:
                load(i, False)

        @block.gpsimd
        def _(pool):
            def serve(u, i, step):
                if step == "index" and layer == "0":
                    pool.wait_ge(map_kept[u], i + 1)
                    cols, tile_index = c.src_cols, i * ITER_TILES + u * TILES
                elif step == "index":
                    pool.wait_ge(*g.PE.done(u, i, "srcT"))
                    cols, tile_index = c.src_table_cols[order], i * ITER_TILES + (ITER_TILES + u * TILES)
                if step == "index":
                    pool.tensor_copy(index[u][:, :], cols[:, ds(tile_index, TILES)]).then_inc(index_ready[u], 1)
                    pool.wait_ge(index_ready[u], 1)
                    pool.sem_clear(index_ready[u])
                if step.startswith("gather"):
                    gather(u, int(step[-1]))
                if step == "dst_index":
                    pool.wait_ge(*g.PE.done(u, i, "dstT"))
                    pool.tensor_copy(side_index[u][:, :], c.dst_gather_cols[:, ds(i * ITER_TILES + (ITER_TILES + u * TILES), TILES)])\
                        .then_inc(side_index_ready[u], 1)
                    pool.wait_ge(side_index_ready[u], 1)
                    pool.sem_clear(side_index_ready[u])
                if step.startswith("dst_gather"):
                    gather_target(u, int(step[-1]))
                if step == "keep_map":
                    pool.wait_ge(map_ready[u], (i + 1) * 16 * TILES)
                    pool.tensor_copy(c.map_cols[:, ds(i * ITER_TILES + u * TILES, TILES), :], map_rows[u][:, :, :])\
                        .then_inc(map_kept[u], 1)
                if step == "scatter":
                    pool.wait_ge(*g.DVE.done(u, i, "x4"))
                    pool.tensor_copy(side_index[u][:, :], c.out_index[:, ds(i * ITER_TILES + u * TILES, TILES)])\
                        .then_inc(side_index_ready[u], 1)
                    pool.wait_ge(side_index_ready[u], 1)
                    pool.sem_clear(side_index_ready[u])
                    for t in range(TILES):
                        pool.indirect_dma_start(a["out"], at_index(side_index[u][:, t:t + 1], 0), new[u][:, t, :], None,
                                                bounds_check=N - 1, oob_is_err=False).then_inc(stored[u], 16)

            def gather_target(u, t):
                pool.indirect_dma_start(dst_rows[u][:, t, :], None, a["x"], at_index(side_index[u][:, t:t + 1], 0))\
                    .then_inc(dst_ready[u], 16)

            def gather(u, t):
                if layer == "0":
                    pool.indirect_dma_start(map_rows[u][:, t, :], None, dram.slot_map, at_index(index[u][:, t:t + 1], 0))\
                        .then_inc(map_ready[u], 16)
                else:
                    pool.indirect_dma_start(src_rows[u][:, t, 0:src_width], None, table, at_index(index[u][:, t:t + 1], 0))\
                        .then_inc(src_ready[u], 16)

            def run(i, part):
                for u, i, step in turns(g, "POOL", i, part):
                    if step == "index" and layer == "3" and not (isinstance(i, int) and i == 0):
                        pool.wait_ge(stored[u], i * 16 * TILES)
                    if step == "shift":
                        pool.wait_ge(*g.ACT.done(u, i, "neg"))
                        pool.wait_ge(*g.DVE.done(u, i, "f"))
                        pool.tensor_tensor(expo[u][0:M, 1, :], fmax[u][0:M, 0:CHUNK], neg[u][0:M, :], ALU.add)\
                            .then_inc(g.pool_out[u], 1)
                    elif step == "ns":
                        pool.wait_ge(*g.DVE.done(u, i, "sv"))
                        pool.tensor_tensor(t2[u][0:M, :], t2[u][0:M, :], num[u][0:M, :], ALU.add).then_inc(g.pool_out[u], 1)
                    elif step == "e_s":
                        pool.wait_ge(*g.DVE.done(u, i, "f"))
                        pool.tensor_tensor(expo[u][0:M, 2, :], extra[u][0:M, :], fmax[u][0:M, 1:CHUNK + 1], ALU.subtract)\
                            .then_inc(g.pool_out[u], 1)
                    elif step == "y2T":
                        pool.wait_ge(g.res_ready[u], (i + 1) * 16)
                        pool.wait_ge(*g.DVE.done(u, i, "h4"))
                        pool.tensor_tensor(g.yT[u][:, :], g.act_T[u][:, :], g.res2(u), ALU.add).then_inc(g.pool_out[u], 1)
                    elif step.startswith("sq"):
                        pool_update(pool, g, u, i, step)
                    elif not (isinstance(i, int) and i == final) or step == "scatter" or \
                            (layer == "0" and not step.startswith("dst")):
                        serve(u, i, step)

            if layer == "0":
                for u in g.streams:
                    pool.memset(map_rows[u][:, :, :], 0).then_inc(map_kept[u], 1)
                    pool.tensor_copy(side_index[u][:, :], c.dst_gather_cols[:, u * TILES:(u + 1) * TILES])\
                        .then_inc(side_index_ready[u], 1)
                for u in g.streams:
                    pool.wait_ge(side_index_ready[u], 1)
                    pool.sem_clear(side_index_ready[u])
                    for t in range(TILES):
                        gather_target(u, t)
            else:
                if layer == "2b":
                    for u in g.streams:
                        pool.memset(src_rows[u][:, :, src_width:], 0.0).then_inc(cleared, 1)
                    pool.wait_ge(cleared, STREAMS)
                for u in g.streams:
                    pool.tensor_copy(index[u][:, :], c.src_table_cols[order][:, u * TILES:(u + 1) * TILES])\
                        .then_inc(index_ready[u], 1)
                for u in g.streams:
                    pool.wait_ge(index_ready[u], 1)
                    pool.sem_clear(index_ready[u])
                    for t in range(TILES):
                        gather(u, t)
            run(0, "in")
            with pool.Fori(1, final) as i:
                run(i, "all")
            run(final, "all")
            run(SLOT_ITERS, "out")
            if layer == "3":
                for u in g.streams:
                    pool.wait_ge(stored[u], SLOT_ITERS * 16 * TILES)

        @block.scalar
        def _(act):
            exps = 3 if own else 2
            z_bias, own_bias = (c.blr1, c.blr1) if layer == "2a" else (c.br2, c.blr2)

            def run(i, part):
                for u, i, step in turns(g, "ACT", i, part):
                    if step == "neg":
                        act.wait_ge(keep_ready[u], (i + 1) * 16)
                        act_copy(act, g, u, neg[u][:, :], keep[u][:, :], scale=BIG, bias=-BIG)
                    elif step == "srcT":
                        act.wait_ge(*g.PE.done(u, i, "srcT"))
                        act_copy(act, g, u, xs[u][0:src_width, :], A(u)[0:src_width, :])
                    elif step == "dstT":
                        act.wait_ge(*g.PE.done(u, i, "dstT"))
                        act_copy(act, g, u, xd[u][:, :], B(u))
                    elif step == "k":
                        act.wait_ge(*g.PE.done(u, i, "k"))
                        act_copy(act, g, u, t1[u][:, :], A(u))
                    elif step == "e0":
                        act.wait_ge(*g.PE.done(u, i, "e0"))
                        act_copy(act, g, u, t2[u][:, :], A(u), ACT.Tanh)
                    elif step == "e1":
                        act.wait_ge(*g.PE.done(u, i, "e1"))
                        act_copy(act, g, u, extra[u][:, :], B(u), ACT.Tanh)
                    elif step == "z":
                        if layer == "2a":
                            act.wait_ge(stored_T[u], i * 32 + 16)
                        act.wait_ge(*g.PE.done(u, i, "z"))
                        act_copy(act, g, u, t1[u][0:M, :], A(u)[0:M, :], ACT.Identity, z_bias[:, 0:1])
                    elif step == "zo":
                        act.wait_ge(*g.PE.done(u, i, "zo"))
                        act_copy(act, g, u, t2[u][0:M, :], B(u)[0:M, :], ACT.Identity, own_bias[:, 0:1])
                    elif step == "l":
                        act.wait_ge(*g.PE.done(u, i, "l"))
                        if layer == "0":
                            act_copy(act, g, u, logit[u], A(u), scale=float((D // H) ** -0.5))
                        elif gatv2:
                            act_copy(act, g, u, logit[u][0:M, :], A(u)[0:M, :])
                        else:
                            act_copy(act, g, u, t1[u][:, :], A(u), scale=SLOPE)
                    elif step == "ls":
                        act.wait_ge(*g.PE.done(u, i, "ls"))
                        if gatv2:
                            act_copy(act, g, u, extra[u][0:M, :], B(u)[0:M, :])
                        else:
                            act_copy(act, g, u, t2[u][:, :], B(u), scale=SLOPE)
                    elif step == "exp":
                        if layer == "2b":
                            act.wait_ge(*g.POOL.done(u, i, "e_s"))
                        act.wait_ge(*g.DVE.done(u, i, "e_c"))
                        act_copy(act, g, u, expo[u][0:M, 0:exps, :], expo[u][0:M, 0:exps, :], ACT.Exp)
                    elif step == "exps":
                        act_copy(act, g, u, expo[u][:, 2, :], fmax[u][:, 1:CHUNK + 1], ACT.Exp, scale=-1.0)
                    elif step == "rs":
                        act.wait_ge(*g.DVE.done(u, i, "rec"))
                        act_copy(act, g, u, expo[u][:, 0, :].rearrange("p (t h k) -> p t h k", t=TILES, h=H),
                                 recip[u][:, :, :].unsqueeze(3).broadcast_to([P, TILES, H, D // H]))
                    elif step == "sq5":
                        act.wait_ge(*g.PE.done(u, i, "y3"))
                        act_squares(act, g, u, tiles_of(A(u)))
                    elif step == "store_T":
                        for array, tile, ready in ((dram.x2_T, xd, "dst"), (dram.h2_T, g.act_T, "h2")):
                            act.wait_ge(*g.DVE.done(u, i, ready))
                            act.dma_start(array[:, ds(start(i, u), CHUNK)], tile[u][:, :]).then_inc(stored_T[u], 16)
                    else:
                        act_update(act, g, u, i, step)

            run(0, "in")
            with act.Fori(1, SLOT_ITERS) as i:
                run(i, "all")
            run(SLOT_ITERS, "out")
            if layer != "3":
                for u in g.streams:
                    act.wait_ge(stored[u], 16 * SLOT_ITERS + 16)
            if layer == "2a":
                for u in g.streams:
                    act.wait_ge(stored_T[u], 32 * SLOT_ITERS + 16)

        @block.tensor
        def _(pe):
            heads = c.ident[0:M, 0:M:D // H] if layer != "2b" else c.ident[0:M, 0:1]

            def product(u, bank, pairs, m=P):
                for k, (weights, tile) in enumerate(pairs):
                    ins = pe.matmul(bank(u)[0:m, :], weights, tile, start=k == 0, stop=k == len(pairs) - 1)
                ins.then_inc(g.pe_out[u], 1)

            def run(i, part):
                for u, i, step in turns(g, "PE", i, part):
                    src, dst, first, second = xs[u][:, :], xd[u][:, :], t1[u][0:M, :], t2[u][0:M, :]
                    if step == "srcT":
                        pe.wait_ge(*g.DVE.before(u, i))
                        if layer == "2a":
                            pe.wait_ge(stored[u], i * 16 + 16)
                        pe.wait_ge(src_ready[u], (i + 1) * (16 if layer == "0" else 16 * TILES))
                        pe_transposes(pe, g, u, A, src_rows[u])
                    elif step == "dstT":
                        pe.wait_ge(dst_ready[u], (i + 1) * (16 * TILES if layer == "0" else 16))
                        pe_transposes(pe, g, u, B, dst_rows[u])
                    elif layer == "0" and step == "k":
                        pe.wait_ge(*g.ACT.done(u, i, "srcT"))
                        product(u, A, [(c.Wk[:, :], src)])
                    elif layer == "0" and step == "q":
                        pe.wait_ge(*g.ACT.done(u, i, "dstT"))
                        product(u, B, [(c.Wq[:, :], dst)])
                    elif layer == "0" and step == "e0":
                        pe.wait_ge(edge_ready[u], (i + 1) * 16)
                        pe.wait_ge(*g.ACT.done(u, i, "k"))
                        product(u, A, [(c.We0[:, :], edge[u][:, :])])
                    elif layer == "0" and step == "e1":
                        pe.wait_ge(*g.DVE.done(u, i, "qk"))
                        product(u, B, [(c.We1[:, :], edge[u][:, :])])
                    elif layer == "0" and step == "l":
                        pe.wait_ge(*g.DVE.done(u, i, "qke"))
                        product(u, A, [(c.S16[:, :], first)])
                    elif layer == "0" and step == "v":
                        pe.wait_ge(*g.ACT.done(u, i, "e1"))
                        product(u, B, [(c.Wv[:, :], src)])
                    elif layer == "1" and step == "l":
                        pe.wait_ge(*g.ACT.done(u, i, "srcT"))
                        pe.wait_ge(*g.DVE.done(u, i, "dst"))
                        product(u, A, [(c.Wsa[:, :], src), (c.Wda[:, :], dst)])
                    elif layer == "1" and step == "ls":
                        product(u, B, [(c.Wsd[:, :], dst)])
                    elif layer == "1" and step in ("v", "o"):
                        pe.wait_ge(*g.DVE.done(u, i, "l" if step == "v" else "ls"))
                        product(u, A if step == "v" else B, [(c.W[:, :], src if step == "v" else dst)])
                    elif gatv2 and step == "z":
                        pe.wait_ge(*g.ACT.done(u, i, "srcT"))
                        pe.wait_ge(*g.DVE.done(u, i, "dst"))
                        if layer == "2a":
                            product(u, A, [(c.Wl1[:, :], src), (c.Wr1[:, :], dst)])
                        else:
                            product(u, A, [(c.Wr2[:, :], dst), (c.ident[0:C2, 0:C2], xs[u][0:C2, :])], M)
                    elif gatv2 and step == "zo":
                        pe.wait_ge(*g.DVE.done(u, i, "dst"))
                        product(u, B, [((c.Wlr1 if layer == "2a" else c.Wlr2)[:, :], dst)], M)
                    elif gatv2 and step in ("l", "ls"):
                        pe.wait_ge(*g.DVE.done(u, i, "z" if step == "l" else "zo"))
                        product(u, A if step == "l" else B,
                                [((c.S1 if layer == "2a" else c.S2)[:, :], first if step == "l" else second)])
                    elif gatv2 and step in ("v", "o"):
                        pe.wait_ge(*g.ACT.done(u, i, "l" if step == "v" else "ls"))
                        product(u, A if step == "v" else B,
                                [((c.Wl1 if layer == "2a" else c.Wl2)[:, :], src if step == "v" else dst)], M)
                    elif layer == "3" and step == "l":
                        pe.wait_ge(edge_ready[u], (i + 1) * 16)
                        pe.wait_ge(*g.ACT.done(u, i, "srcT"))
                        pe.wait_ge(*g.DVE.done(u, i, "dst"))
                        product(u, A, [(c.Wsrc[:, :], src), (c.Wtgt[:, :], dst), (c.Wedge[:, :], edge[u][:, :])])
                    elif layer == "3" and step == "v":
                        pe.wait_ge(*g.DVE.done(u, i, "l"))
                        product(u, A, [(c.WnT[:, :], src)])
                    elif step == "tot":
                        pe.wait_ge(*g.DVE.done(u, i, "pv"))
                        for t in range(TILES):
                            cols = slice(t * H, (t + 1) * H)
                            ins = pe.matmul(A(u)[:, cols], den[u][0:M, tile_cols(t)], heads, start=True, stop=not own)
                            if own:
                                ins = pe.matmul(A(u)[:, cols], expo[u][0:M, 2, tile_cols(t)], heads, start=False, stop=True)
                            if layer == "3":
                                pe.matmul(A(u)[:, 16 + t * H:16 + (t + 1) * H], expo[u][:, 2, tile_cols(t)], heads,
                                          start=True, stop=True)
                                ins = pe.matmul(A(u)[:, 32 + t:33 + t], extra[u][:, tile_cols(t)], c.ident[:, 0:1],
                                                start=True, stop=True)
                        ins.then_inc(g.pe_out[u], 1)
                    elif step == "rB":
                        pe.wait_ge(*g.ACT.done(u, i, "rs"))
                        pe_transposes(pe, g, u, B, tiles_of(expo[u][:, 0, :]))
                    elif step == "y3":
                        pe.wait_ge(*g.DVE.done(u, i, "agg"))
                        pe_rows(pe, g, u, A, [(g.agg[u], c.center[:, :]), (xd[u], c.center[:, :])])
                    else:
                        pe_update(pe, g, u, i, step)

            run(0, "in")
            with pe.Fori(1, SLOT_ITERS) as i:
                run(i, "all")
            run(SLOT_ITERS, "out")

        @block.vector
        def _(v):
            for u in g.streams:
                if layer != "3":
                    v.memset(new[u][:, 0, 0:1], 0.0).then_inc(stored[u], 16)
                v.memset(t2[u][:, 0:1], 0.0).then_inc(stored_T[u], 16)
                for t, col in ((xd, CHUNK - 1), (extra, CHUNK - 1), (fmax, CHUNK), (den, CHUNK - 1), (num, CHUNK - 1)):
                    v.memset(t[u][:, col:col + 1], 0.0).then_inc(g.dve_out[u], 1)

            sums = lambda u: A(u)[:, 0:TILES * H].rearrange("p (t h) -> p t h", t=TILES)

            def carry(u, i, tile, step, m=P):
                if u > 0:
                    v.wait_ge(*g.DVE.done(u - 1, i, step))
                elif isinstance(i, int):
                    v.wait_ge(*g.DVE.before(STREAMS - 1, 0))
                else:
                    v.wait_ge(*g.DVE.done(STREAMS - 1, i - 1, step))
                return tile[u - 1][0:m, -1:]

            def run(i, part):
                for u, i, step in turns(g, "DVE", i, part):
                    def after(name):
                        v.wait_ge(*g.DVE.done(u, i, name))

                    ins = None
                    f = fmax[u][0:M, 1:CHUNK + 1]
                    if step == "mask":
                        v.wait_ge(dst_ready[u], (i + 1) * 16)
                        v.wait_ge(keep_ready[u], (i + 1) * 16)
                        ins = v.scalar_tensor_tensor(out=t1[u][:, :], in0=keep[u][:, :], scalar=-1.0,
                                                     in1=h2_before[u][:, ::-1], op0=ALU.add, op1=ALU.mult)
                    elif step == "dst":
                        before = carry(u, i, xd, "dst")
                        if layer == "2b":
                            after("mask")
                            ins = v.tensor_tensor_scan(xd[u][:, :], keep[u][:, :], t1[u][:, :], before, ALU.mult, ALU.subtract)
                        else:
                            if layer == "2a":
                                v.wait_ge(stored_T[u], i * 32 + 16)
                            v.wait_ge(keep_ready[u], (i + 1) * 16)
                            v.wait_ge(*g.PE.done(u, i, "dstT"))
                            ins = v.tensor_tensor_scan(xd[u][:, :], keep[u][:, :], B(u)[:, ::-1], before, ALU.mult, ALU.add)
                    elif step == "deg":
                        before = carry(u, i, extra, "deg")
                        ins = v.tensor_tensor_scan(extra[u][:, :], keep[u][:, :], c.minus_one[:, :], before, ALU.mult, ALU.add)
                    elif step == "qk":
                        v.wait_ge(*g.PE.done(u, i, "q"))
                        v.wait_ge(*g.ACT.done(u, i, "k"))
                        ins = v.tensor_tensor(t1[u][:, :], B(u), t1[u][:, :], ALU.mult)
                    elif step == "qke":
                        after("qk")
                        v.wait_ge(*g.ACT.done(u, i, "e0"))
                        ins = v.tensor_tensor(t1[u][:, :], t1[u][:, :], t2[u][:, :], ALU.mult)
                    elif step == "l":
                        v.wait_ge(*g.ACT.done(u, i, "l"))
                        ins = v.tensor_tensor(logit[u], A(u), t1[u][:, :], ALU.max)
                    elif step == "ls":
                        v.wait_ge(*g.ACT.done(u, i, "ls"))
                        ins = v.tensor_tensor(extra[u][:, :], B(u), t2[u][:, :], ALU.max)
                    elif step in ("z", "zo"):
                        z = (t1 if step == "z" else t2)[u][0:M, :]
                        v.wait_ge(*g.ACT.done(u, i, step))
                        ins = v.scalar_tensor_tensor(out=z, in0=z, scalar=SLOPE, in1=z, op0=ALU.mult, op1=ALU.max)
                    elif step == "lm" and own:
                        if gatv2:
                            v.wait_ge(*g.ACT.done(u, i, "ls"))
                        else:
                            after("ls")
                        ins = v.tensor_tensor(t1[u][0:M, :], logit[u][0:M, :], extra[u][0:M, :], ALU.max)
                    elif step == "lm":
                        after("l")
                        ins = v.tensor_scalar(t1[u][:, :], logit[u], 0.0, None, ALU.max)
                    elif step == "fc":
                        ins = v.tensor_copy(fmax[u][0:M, 0:1], carry(u, i, fmax, "f", M))
                    elif step == "f":
                        highest = logit[u] if layer == "0" else t1[u][:, :]
                        v.wait_ge(*g.ACT.done(u, i, "l" if layer == "0" else "neg"))
                        after("fc")
                        ins = v.tensor_tensor_scan(f, neg[u][0:M, :], highest[0:M, :], fmax[u][0:M, 0:1], ALU.add, ALU.max)
                    elif step == "e_p":
                        after("f")
                        ins = v.tensor_tensor(expo[u][0:M, 0, :], logit[u][0:M, :], f, ALU.subtract)
                    elif step == "e_s":
                        after("f")
                        ins = v.tensor_tensor(expo[u][0:M, 2, :], extra[u][0:M, :], f, ALU.subtract)
                    elif step == "e_c":
                        v.wait_ge(*g.POOL.done(u, i, "shift"))
                        ins = v.tensor_tensor(expo[u][0:M, 1, :], expo[u][0:M, 1, :], f, ALU.subtract)
                    elif step == "v":
                        v.wait_ge(*g.PE.done(u, i, "v"))
                        ins = v.tensor_tensor(extra[u][:, :], B(u), extra[u][:, :], ALU.mult)
                    elif step == "den":
                        before = carry(u, i, den, "den", M)
                        v.wait_ge(*g.ACT.done(u, i, "exps" if layer == "3" else "exp"))
                        ins = v.tensor_tensor_scan(den[u][0:M, :], expo[u][0:M, 1, :], expo[u][0:M, 0, :], before,
                                                   ALU.mult, ALU.add)
                    elif step == "pv" and layer == "0":
                        after("v")
                        ins = v.tensor_tensor(t1[u][:, :], extra[u][:, :], expo[u][:, 0, :], ALU.mult)
                    elif step == "pv" and layer == "2b":
                        ins = v.tensor_tensor(t1[u][0:M, :], xs[u][0:M, :], expo[u][0:M, 0, :], ALU.mult)
                    elif step == "pv":
                        v.wait_ge(*g.PE.done(u, i, "v"))
                        if layer == "2a":
                            ins = v.scalar_tensor_tensor(out=t1[u][:, :], in0=A(u), scalar=c.bl1[:, 0:1],
                                                         in1=expo[u][:, 0, :], op0=ALU.add, op1=ALU.mult)
                        else:
                            ins = v.tensor_tensor(t1[u][:, :], A(u), expo[u][:, 0, :], ALU.mult)
                    elif step == "num":
                        before = carry(u, i, num, "num", M)
                        after("pv")
                        ins = v.tensor_tensor_scan(num[u][0:M, :], expo[u][0:M, 1, :], t1[u][0:M, :], before, ALU.mult, ALU.add)
                    elif step == "sv":
                        v.wait_ge(*g.PE.done(u, i, "o"))
                        if layer == "1":
                            ins = v.tensor_tensor(t2[u][:, :], B(u), expo[u][:, 2, :], ALU.mult)
                        else:
                            bias = c.bl1 if layer == "2a" else c.bl2
                            ins = v.scalar_tensor_tensor(out=t2[u][0:M, :], in0=B(u)[0:M, :], scalar=bias[:, 0:1],
                                                         in1=expo[u][0:M, 2, :], op0=ALU.add, op1=ALU.mult)
                    elif step == "degE":
                        v.wait_ge(*g.PE.done(u, i, "tot"))
                        ins = v.tensor_scalar(count[u][:, :], A(u)[:, 32:32 + TILES], float(E), None, ALU.add)
                    elif step == "rest":
                        after("degE")
                        ins = v.tensor_tensor(small[u][:, :, :], A(u)[:, 16:16 + TILES * H].rearrange("p (t h) -> p t h", t=TILES),
                                              count[u][:, :].unsqueeze(2).broadcast_to([P, TILES, H]), ALU.mult)
                    elif step == "tot" and layer == "3":
                        after("rest")
                        ins = v.tensor_tensor(small[u][:, :, :], sums(u), small[u][:, :, :], ALU.add)
                    elif step == "tot":
                        v.wait_ge(*g.PE.done(u, i, "tot"))
                        ins = v.tensor_scalar(small[u][:, :, :], sums(u), SOFTMAX_EPS, None, ALU.add)
                    elif step == "rec" and gatv2:
                        v.wait_ge(*g.PE.done(u, i, "tot"))
                        ins = v.reciprocal(recip[u][:, :, :], sums(u))
                    elif step == "rec":
                        after("tot")
                        ins = v.reciprocal(recip[u][:, :, :], small[u][:, :, :])
                    elif step == "agg":
                        if own:
                            v.wait_ge(*g.POOL.done(u, i, "ns"))
                        else:
                            after("num")
                        v.wait_ge(*g.PE.done(u, i, "rB"))
                        weighted = (t2 if own else num)[u]
                        ins = v.tensor_tensor(g.agg[u][0:M, :], weighted[0:M, :], B(u)[0:M, :], ALU.mult)
                    elif step == "x4":
                        v.wait_ge(*g.POOL.done(u, i, "sq5_rstd"))
                        dve_scale_rows(v, g, u, tiles_of(A(u)), new[u])
                    else:
                        dve_update(v, g, u, i, step)
                    if ins is not None:
                        ins.then_inc(g.dve_out[u], 1)

            run(0, "in")
            with v.Fori(1, SLOT_ITERS) as i:
                run(i, "all")
            run(SLOT_ITERS, "out")


def source_columns(nc, c):
    with ExitStack() as own:
        as_float = own.enter_context(nc.sbuf_tensor("map_as_float", [P, SLOT_TILES], F32))
        sem = lambda name: own.enter_context(nc.semaphore(name))
        copied, flipped = sem("map_copied"), sem("map_flipped")
        block = own.enter_context(nc.Block())

        @block.vector
        def _(v):
            v.tensor_copy(as_float[:, :], c.map_cols[:, :, 0]).then_inc(copied, 1)
            v.tensor_copy(c.src_table_cols[0][:, :], c.map_cols[:, :, 1]).then_inc(copied, 1)
            v.wait_ge(flipped, 1)
            v.tensor_copy(c.src_table_cols[1][:, :], c.psum[:, 0, SLOT_TILES - 1::-1]).then_inc(copied, 1)
            v.wait_ge(copied, 3)

        @block.tensor
        def _(pe):
            pe.wait_ge(copied, 1)
            pe.matmul(c.psum[:, 0, 0:SLOT_TILES], c.anti[:, :], as_float[:, :], start=True, stop=True).then_inc(flipped, 1)


def build(nc, a):
    c, dram = Named(), Named()
    c.dram = dram

    def scratch(name, shape, dt=F32):
        return nc.dram_tensor(name, shape, dt, kind="Internal").ap()

    dram.x1, dram.x2, dram.x3 = (scratch(n, [ROWS, D]) for n in ("x1", "x2", "x3"))
    dram.xl2 = scratch("xl2", [ROWS, C2])
    dram.x2_T, dram.h2_T = scratch("x2_T", [D, E_PAD]), scratch("h2_T", [D, E_PAD])
    dram.staged = scratch("staged", [E_PAD, D])
    dram.slot_map = scratch("slot_map", [N, 2], I32)
    dram.slot_map_flat = dram.slot_map.rearrange("n (o k) -> (n o) k", k=1)
    dram.keep = [scratch(f"keep{o}", [SLOT_CHUNKS, CHUNK]) for o in range(2)]
    dram.keep_flat = [t.rearrange("a b -> (a b)") for t in dram.keep]

    with ExitStack() as ctx:
        c.psum = ctx.enter_context(nc.psum_tensor("psum", [P, 8, CHUNK], F32))
        c.map_cols = ctx.enter_context(nc.sbuf_tensor("map_cols", [P, SLOT_TILES, 2], I32))
        c.src_table_cols = [ctx.enter_context(nc.sbuf_tensor(f"src_table_cols{o}", [P, SLOT_TILES], I32)) for o in range(2)]
        prepare(nc, a, c, dram, ctx)
        node_pass(nc, a, c, dram)
        slot_pass(nc, a, c, dram, "0")
        source_columns(nc, c)
        for layer in ("1", "2a", "2b", "3"):
            slot_pass(nc, a, c, dram, layer)



def lay_out(inputs):
    out = {k: np.ascontiguousarray(v) for k, v in inputs.items() if k not in ("src", "dst", "edge_attr_64", "L3_gnn_W_node")}
    out["L3_gnn_W_node"] = np.ascontiguousarray(inputs["L3_gnn_W_node"])
    out["W_node_T"] = np.ascontiguousarray(np.asarray(inputs["L3_gnn_W_node"]).T)
    x_T = np.zeros((D, N_PAD), np.float32)
    x_T[:, :N] = np.asarray(inputs["x"]).T
    out["x_T"] = x_T
    edge_T = np.zeros((EF, E_PAD), np.float32)
    edge_T[:, :E] = np.asarray(inputs["edge_attr_64"]).T
    out["edge_T"] = edge_T
    src, dst = np.asarray(inputs["src"]), np.asarray(inputs["dst"])
    more = E_PAD - E

    def columns(t):
        return np.ascontiguousarray(t.reshape(SLOT_TILES, P).T)

    def chunks(t):
        return np.ascontiguousarray(t.reshape(SLOT_CHUNKS, CHUNK))

    out["src_cols"] = columns(np.concatenate([src, np.zeros(more, src.dtype)]))
    out["dst_gather_cols"] = columns(np.concatenate([dst, np.zeros(more, dst.dtype)]))
    ended = np.concatenate([np.full(1, -1, dst.dtype), dst, np.full(more, N, dst.dtype), np.full(1, -1, dst.dtype)])
    both = [ended, ended[::-1]]
    out["dst_cols"] = np.stack([columns(t[1:-1]) for t in both])
    out["dst_next_cols"] = np.stack([columns(t[2:]) for t in both])
    out["dst_prev_cols"] = columns(ended[:-2])
    out["dst_rows"] = np.stack([chunks(t[1:-1]) for t in both])
    out["dst_prev_rows"] = np.stack([chunks(t[:-2]) for t in both])
    return out


def kernel(**inputs):
    import concourse.bacc as bacc
    from concourse.bass_utils import run_bass_kernel_spmd

    nc = bacc.Bacc("TRN2", target_bir_lowering=False, num_devices=1)
    a = {}
    arrays = {}
    for name, array in lay_out(inputs).items():
        arrays[f"in_{name}"] = array
        a[name] = nc.dram_tensor(f"in_{name}", array.shape, mybir.dt.from_np(array.dtype),
                                          kind="ExternalInput").ap()
    a["out"] = nc.dram_tensor("out_nodes", [N_PAD, D], F32, kind="ExternalOutput").ap()
    build(nc, a)
    r = run_bass_kernel_spmd(nc, [arrays], core_ids=[0])
    return r.results[0]["out_nodes"][:N]
```
